# Optimizing a Trainium2 kernel written in Bass

```python
import numpy as np
import jax
import jax.numpy as jnp

def _softmax(x, axis=-1):
    return jax.nn.softmax(x, axis=axis)

def _gelu(x):
    return jax.nn.gelu(x, approximate=True)

def _silu(x):
    return jax.nn.silu(x)

def _sigmoid(x):
    return jax.nn.sigmoid(x)

def _layernorm(x, axis=-1, eps=1e-05):
    m = jnp.mean(x, axis=axis, keepdims=True)
    v = jnp.var(x, axis=axis, keepdims=True)
    return (x - m) / jnp.sqrt(v + eps)

def _scatter_add(tgt, idx, src, axis=0):
    return tgt.at[idx].add(src)

def _segment_sum(src, seg, n):
    return jax.ops.segment_sum(src, seg, n)
kernel_name = 'mk_gnn_resnorm_d4_gnn_r8_8d980d'

def setup_inputs(seed: int=0):
    np.random.seed(seed)
    _w = jnp.asarray

    def _rec_inputs():
        import jax
        import jax.numpy as jnp
        _gk = jax.random.key(seed)
        x = -0.000202 + 1 * jax.random.normal(jax.random.fold_in(_gk, 1), (6250, 128), jnp.float32)
        _s = jax.random.randint(jax.random.fold_in(_gk, 2), (50000,), 0, 6250, jnp.int32)
        _d = jax.random.randint(jax.random.fold_in(_gk, 3), (50000,), 0, 6250, jnp.int32)
        _loop = jnp.arange(6250, dtype=jnp.int32)
        src = jnp.concatenate([_s, _d, _loop])
        dst = jnp.concatenate([_d, _s, _loop])
        _o = jnp.argsort(dst, stable=True)
        src = src[_o]
        dst = dst[_o]
        edge_attr_128 = -8.16379e-05 + 0.999858 * jax.random.normal(jax.random.fold_in(_gk, 12), (106250, 128), jnp.float32)
        return (x, src, dst, edge_attr_128)
    x, src, dst, edge_attr_128 = _rec_inputs()

    def _L0_gnn_setup():
        import jax, jax.numpy as jnp
        import numpy as np
        N, E, F, H = (6250, 100000, 128, 8)
        D = F // H
        SCALING = D ** (-0.5)
        key = jax.random.key(seed)
        ks = jax.random.split(key, 10)
        w_scale = (2.0 / (F + F)) ** 0.5
        return {'feat': jax.random.normal(ks[0], (N, F), jnp.float32), 'edge_feat': jax.random.normal(ks[1], (E, F), jnp.float32), 'Wq': jax.random.normal(ks[2], (F, F), jnp.float32) * w_scale, 'Wk': jax.random.normal(ks[3], (F, F), jnp.float32) * w_scale, 'Wv': jax.random.normal(ks[4], (F, F), jnp.float32) * w_scale, 'Wnode': jax.random.normal(ks[5], (F, F), jnp.float32) * w_scale, 'Wedge': jax.random.normal(ks[6], (H, F), jnp.float32) * w_scale, 'Wgate': jax.random.normal(ks[7], (H, F), jnp.float32) * w_scale, 'src': jax.random.randint(ks[8], (E,), 0, N, jnp.int32), 'dst': jax.random.randint(ks[9], (E,), 0, N, jnp.int32)}
    _L0_gnn_all = _L0_gnn_setup()
    _L0_gnn_in = {k: v for k, v in _L0_gnn_all.items() if k in ('Wq', 'Wk', 'Wv', 'Wnode', 'Wedge', 'Wgate')}
    del _L0_gnn_all

    def _L1_gnn_setup():
        import jax, jax.numpy as jnp
        import numpy as np
        N_NODES = 6250
        N_EDGES = 200000
        DIM = 128
        HEADS = 4
        HEAD_DIM = DIM // HEADS
        NEG_SLOPE = 0.2
        key = jax.random.key(seed)
        k1, k2, k3, k4, k5 = jax.random.split(key, 5)
        x = jax.random.normal(k1, (N_NODES, DIM), dtype=jnp.float32)
        edge_index = jax.random.randint(k2, (2, N_EDGES), 0, N_NODES, dtype=jnp.int64)
        glorot = 1.0 / np.sqrt(DIM)
        W = jax.random.uniform(k3, (HEADS * HEAD_DIM, DIM), dtype=jnp.float32, minval=-glorot, maxval=glorot)
        ga = 1.0 / np.sqrt(HEAD_DIM)
        att_src = jax.random.uniform(k4, (HEADS, HEAD_DIM), dtype=jnp.float32, minval=-ga, maxval=ga)
        att_dst = jax.random.uniform(k5, (HEADS, HEAD_DIM), dtype=jnp.float32, minval=-ga, maxval=ga)
        return {'x': x, 'W': W, 'att_src': att_src, 'att_dst': att_dst, 'edge_index': edge_index}
    _L1_gnn_all = _L1_gnn_setup()
    _L1_gnn_in = {k: v for k, v in _L1_gnn_all.items() if k in ('W', 'att_src', 'att_dst')}
    del _L1_gnn_all

    def _L2_gnn_setup():
        import jax, jax.numpy as jnp
        import numpy as np
        N_NODES = 12500
        N_EDGES = 200000
        IN_CH = 128
        HEADS = 4
        OUT_CH = 32
        EPS_BN = 1e-05
        key = jax.random.key(seed)
        ks = jax.random.split(key, 8)
        s = 1.0 / np.sqrt(IN_CH)
        return {'x': jax.random.normal(ks[0], (N_NODES, IN_CH), jnp.float32), 'edge_index': jax.random.randint(ks[1], (2, N_EDGES), 0, N_NODES, jnp.int32), 'W_src': jax.random.normal(ks[2], (IN_CH, HEADS * OUT_CH), jnp.float32) * s, 'W_dst': jax.random.normal(ks[3], (IN_CH, HEADS * OUT_CH), jnp.float32) * s, 'att': jax.random.normal(ks[4], (HEADS, OUT_CH), jnp.float32) * s, 'bias': jnp.zeros((HEADS * OUT_CH,), jnp.float32), 'bn_gamma': jnp.ones((HEADS * OUT_CH,), jnp.float32), 'bn_beta': jnp.zeros((HEADS * OUT_CH,), jnp.float32)}
    _L2_gnn_all = _L2_gnn_setup()
    _L2_gnn_in = {k: v for k, v in _L2_gnn_all.items() if k in ('W_src', 'W_dst', 'att', 'bias', 'bn_gamma', 'bn_beta')}
    del _L2_gnn_all

    def _L3_gnn_setup():
        import jax, jax.numpy as jnp
        import numpy as np
        N = 6250
        E = 100000
        F = 128
        ATT_DIM = 64
        H = 4
        D_K = ATT_DIM // H

        def _segment_softmax(scores, seg, n):
            m = jax.ops.segment_max(scores, seg, num_segments=n)
            m = jnp.where(jnp.isfinite(m), m, 0.0)
            ex = jnp.exp(scores - m[seg])
            denom = jax.ops.segment_sum(ex, seg, num_segments=n)
            return ex / (denom[seg] + 1e-16)
        key = jax.random.key(seed)
        ks = jax.random.split(key, 9)
        x = jax.random.normal(ks[0], (N, F), dtype=jnp.float32)
        Wq = jax.random.normal(ks[1], (ATT_DIM, F), dtype=jnp.float32) * 0.05
        bq = jax.random.normal(ks[2], (ATT_DIM,), dtype=jnp.float32) * 0.05
        Wk = jax.random.normal(ks[3], (ATT_DIM, F), dtype=jnp.float32) * 0.05
        bk = jax.random.normal(ks[4], (ATT_DIM,), dtype=jnp.float32) * 0.05
        Wv = jax.random.normal(ks[5], (ATT_DIM, F), dtype=jnp.float32) * 0.05
        bv = jax.random.normal(ks[6], (ATT_DIM,), dtype=jnp.float32) * 0.05
        edge_index = jax.random.randint(ks[7], (2, E), 0, N, dtype=jnp.int64)
        return {'x': x, 'Wq': Wq, 'bq': bq, 'Wk': Wk, 'bk': bk, 'Wv': Wv, 'bv': bv, 'edge_index': edge_index}
    _L3_gnn_all = _L3_gnn_setup()
    _L3_gnn_in = {k: v for k, v in _L3_gnn_all.items() if k in ('Wq', 'bq', 'Wk', 'bk', 'Wv', 'bv')}
    del _L3_gnn_all
    return {'x': x, 'src': src, 'dst': dst, 'edge_attr_128': edge_attr_128, 'L0_gnn_Wq': _L0_gnn_in['Wq'], 'L0_gnn_Wk': _L0_gnn_in['Wk'], 'L0_gnn_Wv': _L0_gnn_in['Wv'], 'L0_gnn_Wnode': _L0_gnn_in['Wnode'], 'L0_gnn_Wedge': _L0_gnn_in['Wedge'], 'L0_gnn_Wgate': _L0_gnn_in['Wgate'], 'L1_gnn_W': _L1_gnn_in['W'], 'L1_gnn_att_src': _L1_gnn_in['att_src'], 'L1_gnn_att_dst': _L1_gnn_in['att_dst'], 'L2_gnn_W_src': _L2_gnn_in['W_src'], 'L2_gnn_W_dst': _L2_gnn_in['W_dst'], 'L2_gnn_att': _L2_gnn_in['att'], 'L2_gnn_bias': _L2_gnn_in['bias'], 'L2_gnn_bn_gamma': _L2_gnn_in['bn_gamma'], 'L2_gnn_bn_beta': _L2_gnn_in['bn_beta'], 'L3_gnn_Wq': _L3_gnn_in['Wq'], 'L3_gnn_bq': _L3_gnn_in['bq'], 'L3_gnn_Wk': _L3_gnn_in['Wk'], 'L3_gnn_bk': _L3_gnn_in['bk'], 'L3_gnn_Wv': _L3_gnn_in['Wv'], 'L3_gnn_bv': _L3_gnn_in['bv']}

def reference(x, src, dst, edge_attr_128, L0_gnn_Wq, L0_gnn_Wk, L0_gnn_Wv, L0_gnn_Wnode, L0_gnn_Wedge, L0_gnn_Wgate, L1_gnn_W, L1_gnn_att_src, L1_gnn_att_dst, L2_gnn_W_src, L2_gnn_W_dst, L2_gnn_att, L2_gnn_bias, L2_gnn_bn_gamma, L2_gnn_bn_beta, L3_gnn_Wq, L3_gnn_bq, L3_gnn_Wk, L3_gnn_bk, L3_gnn_Wv, L3_gnn_bv):
    import jax
    import jax.numpy as jnp

    def _L0_gnn_ref(feat, edge_feat, Wq, Wk, Wv, Wnode, Wedge, Wgate, src, dst):
        import jax, jax.numpy as jnp
        import numpy as np
        N, E, F, H = (6250, 100000, 128, 8)
        D = F // H
        SCALING = D ** (-0.5)
        q = (feat @ Wq.T).reshape(N, H, D)
        k = (feat @ Wk.T).reshape(N, H, D)
        v = (feat @ Wv.T).reshape(N, H, D)
        a = jnp.einsum('ehd,ehd->eh', q[src], k[dst])
        e_bias = edge_feat @ Wedge.T
        gates = jax.nn.sigmoid(edge_feat @ Wgate.T)
        logits = (jnp.clip(a, -5.0, 5.0) + e_bias) / SCALING
        m = jax.ops.segment_max(logits, dst, num_segments=N)
        ex = jnp.exp(logits - m[dst])
        s = jax.ops.segment_sum(ex, dst, num_segments=N)
        sa = ex / s[dst] * gates
        agg = jax.ops.segment_sum(v[src] * sa[:, :, None], dst, num_segments=N)
        rst = agg.reshape(N, F) @ Wnode.T
        return rst

    def _L1_gnn_ref(x, W, att_src, att_dst, edge_index):
        import jax, jax.numpy as jnp
        import numpy as np
        N_NODES = 6250
        N_EDGES = 200000
        DIM = 128
        HEADS = 4
        HEAD_DIM = DIM // HEADS
        NEG_SLOPE = 0.2
        N = x.shape[0]
        loops = jnp.arange(N, dtype=edge_index.dtype)
        ei = jnp.concatenate([edge_index, jnp.stack([loops, loops])], axis=1)
        src, dst = (ei[0], ei[1])
        h = (x @ W.T).reshape(N, HEADS, HEAD_DIM)
        a_src = jnp.einsum('nhc,hc->nh', h, att_src)
        a_dst = jnp.einsum('nhc,hc->nh', h, att_dst)
        logits = jax.nn.leaky_relu(a_src[src] + a_dst[dst], NEG_SLOPE)
        m = jax.ops.segment_max(logits, dst, num_segments=N)
        m = jnp.where(jnp.isfinite(m), m, 0.0)
        e = jnp.exp(logits - m[dst])
        s = jax.ops.segment_sum(e, dst, num_segments=N)
        alpha = e / (s[dst] + 1e-16)
        msg = h[src] * alpha[:, :, None]
        out = jax.ops.segment_sum(msg, dst, num_segments=N)
        return out.reshape(N, HEADS * HEAD_DIM)

    def _L2_gnn_ref(x, edge_index, W_src, W_dst, att, bias, bn_gamma, bn_beta):
        import jax, jax.numpy as jnp
        import numpy as np
        N_NODES = 12500
        N_EDGES = 200000
        IN_CH = 128
        HEADS = 4
        OUT_CH = 32
        EPS_BN = 1e-05
        N = x.shape[0]
        H, C = att.shape
        loop = jnp.arange(N, dtype=edge_index.dtype)
        src = jnp.concatenate([edge_index[0], loop])
        dst = jnp.concatenate([edge_index[1], loop])
        h_src = (x @ W_src).reshape(N, H, C)
        h_dst = (x @ W_dst).reshape(N, H, C)
        e = jax.nn.leaky_relu(h_src[src] + h_dst[dst], 0.2)
        logits = jnp.einsum('ehc,hc->eh', e, att)
        m = jax.ops.segment_max(logits, dst, num_segments=N)
        ex = jnp.exp(logits - m[dst])
        denom = jax.ops.segment_sum(ex, dst, num_segments=N)
        alpha = ex / denom[dst]
        out = jax.ops.segment_sum(alpha[:, :, None] * h_src[src], dst, num_segments=N)
        out = out.reshape(N, H * C) + bias
        mean = out.mean(axis=0)
        var = out.var(axis=0)
        y = bn_gamma * (out - mean) * jax.lax.rsqrt(var + EPS_BN) + bn_beta
        return jax.nn.leaky_relu(y, 0.02)

    def _L3_gnn_ref(x, Wq, bq, Wk, bk, Wv, bv, edge_index):
        import jax, jax.numpy as jnp
        import numpy as np
        N = 6250
        E = 100000
        F = 128
        ATT_DIM = 64
        H = 4
        D_K = ATT_DIM // H

        def _segment_softmax(scores, seg, n):
            m = jax.ops.segment_max(scores, seg, num_segments=n)
            m = jnp.where(jnp.isfinite(m), m, 0.0)
            ex = jnp.exp(scores - m[seg])
            denom = jax.ops.segment_sum(ex, seg, num_segments=n)
            return ex / (denom[seg] + 1e-16)
        n = x.shape[0]
        row, col = (edge_index[0], edge_index[1])
        q = (x @ Wq.T + bq).reshape(n, H, D_K)
        k = (x @ Wk.T + bk).reshape(n, H, D_K)
        v = (x @ Wv.T + bv).reshape(n, H, D_K)
        prods = jnp.einsum('ehd,ehd->eh', q[row], k[col]) / jnp.sqrt(jnp.asarray(D_K, dtype=x.dtype))
        attention = _segment_softmax(prods, row, n)
        mean_attention = attention.mean(axis=1)
        agg = jax.ops.segment_sum(mean_attention[:, None] * x[col], row, num_segments=n)
        grad_x = agg - x
        grad_x_norm = jnp.sqrt(jnp.sum(jnp.maximum(grad_x * grad_x, 0.1), axis=1))
        grad_x_norm_inv = 1.0 / grad_x_norm
        attention2 = grad_x_norm_inv[row] + grad_x_norm_inv[col]
        new_attn = mean_attention * _segment_softmax(attention2, row, n)
        rowsum = jax.ops.segment_sum(new_attn, row, num_segments=n)
        ax = jax.ops.segment_sum(new_attn[:, None] * x[col], row, num_segments=n)
        dx = rowsum[:, None] * x
        return ax - dx
    edge_index = jnp.stack([src, dst])
    x = _layernorm(x + _L0_gnn_ref(x, edge_attr_128, L0_gnn_Wq, L0_gnn_Wk, L0_gnn_Wv, L0_gnn_Wnode, L0_gnn_Wedge, L0_gnn_Wgate, src, dst), axis=-1)
    x = _layernorm(x + _L1_gnn_ref(x, L1_gnn_W, L1_gnn_att_src, L1_gnn_att_dst, edge_index), axis=-1)
    x = _layernorm(x + _L2_gnn_ref(x, edge_index, L2_gnn_W_src, L2_gnn_W_dst, L2_gnn_att, L2_gnn_bias, L2_gnn_bn_gamma, L2_gnn_bn_beta), axis=-1)
    x = _layernorm(x + _L3_gnn_ref(x, L3_gnn_Wq, L3_gnn_bq, L3_gnn_Wk, L3_gnn_bk, L3_gnn_Wv, L3_gnn_bv, edge_index), axis=-1)
    return x

_drawn_inputs = setup_inputs


def setup_inputs(seed=0):
    import zlib

    import numpy as np

    out = dict(_drawn_inputs(seed))
    spreads = {'L2_gnn_bias': (0.0, 2.0), 'L2_gnn_bn_gamma': (1.0, 0.2), 'L2_gnn_bn_beta': (0.0, 0.1)}
    factors = {'L1_gnn_att_dst': 3.716,
     'L3_gnn_Wq': 8.0,
     'L3_gnn_bq': 61.582,
     'L3_gnn_Wk': 8.0,
     'L3_gnn_bk': 64.0}
    for name, (base, spread) in spreads.items():
        noise = np.random.default_rng([zlib.crc32(name.encode()), seed]).standard_normal(out[name].shape)
        drawn = base * np.exp(spread * noise) if base else spread * noise
        out[name] = jnp.asarray(drawn.astype(out[name].dtype))
    for name, factor in factors.items():
        out[name] = (out[name] * factor).astype(out[name].dtype)
    return out
```

```python
from contextlib import ExitStack

import concourse.bass as bass
from concourse import mybir

F32 = mybir.dt.float32
BF16 = mybir.dt.bfloat16
I32 = mybir.dt.int32
ALU = mybir.AluOpType
ACT = mybir.ActivationFunctionType
X_AXIS = mybir.AxisListType.X

P = 128
N = 6250
E = 106250
F = 128
T = -(-N // P)
NPAD = T * P
LAST = N - (T - 1) * P
GT = 7
NG = T // GT
SLOTS = 8
RING = 4
BUCKETS = 64
BLK = 250
NBLK = E // BLK
LIST_W = 108
CAP = P * LIST_W
REC = 20
MASK_AT = 12
MASKED = -3.0e38
LOWEST = -1.0e37
assert T % GT == 0 and E % BLK == 0
assert CAP >= (E + E // P + BUCKETS) // SLOTS + T and CAP % RING == 0

ER = 10
E_MAIN = E // P // ER * ER
ESTEPS = E_MAIN // ER
E_TAIL = E - P * E_MAIN

L0_SCALE = 4.0


def bc(ap, shape):
    return ap.to_broadcast(shape)


class Core:
    pass


def build(nc, x, src, dst, edge_attr, w, out, stop=None, dump=None):
    ctx = ExitStack()
    with ctx:
        c = Core()
        c.nc = nc

        def sb(name, shape, dt=F32, where=ctx):
            return where.enter_context(nc.sbuf_tensor(name, shape, dt))

        def sem(name, where=ctx):
            return where.enter_context(nc.semaphore(name))

        c.sb, c.sem = sb, sem
        c.passed = sem("passed")
        c.src, c.dst, c.x, c.edge_attr, c.w, c.out = src, dst, x, edge_attr, w, out
        def dram(name, shape, dt=F32):
            return nc.dram_tensor(name, shape, dt).ap()

        c.samples_d = dram("samples_d", [1, NBLK], I32)
        c.src_pad = dram("src_pad", [E + 16], I32)
        c.src_win = dram("src_win", [E + 1, SLOTS], I32)
        c.edge_gate = dram("edge_gate", [E + SLOTS, 16])
        c.gate_win = dram("gate_win", [E + 1, SLOTS * 16])
        c.order = dram("order", [NPAD, 4], I32)
        c.meta_d = dram("meta_d", [CAP, 4], I32)
        c.rec_d = dram("rec_d", [CAP, P, REC], I32)
        c.att_d = dram("att_d", [CAP, P, SLOTS])
        c.tab = [dram("tab0", [NPAD, 2 * F]), dram("tab1", [NPAD, F + 4]), dram("tab2", [NPAD, F]),
                 dram("tab3", [NPAD, 64 + F]), dram("tab4", [NPAD, F + 1])]
        c.X = sb("X", [P, T, F])
        c.K = sb("K", [P, T, F])
        c.O = sb("O", [P, T, F])
        c.M = sb("M", [P, T, 8])
        c.S = sb("S", [P, T, 8])
        c.rs = sb("rs", [P, T, 8])
        c.adst = sb("adst", [P, T, 4])
        c.g = sb("g", [P, T])
        c.rowsum = sb("rowsum", [P, T])
        c.ids = sb("ids", [P, T], I32)
        c.start = sb("start", [P, T])
        c.first = sb("first", [P, T])
        c.deg = sb("deg", [P, T])
        c.bodies = sb("bodies", [1, 1], I32)
        c.slot = sb("slot", [P, SLOTS])
        c.diag = sb("diag", [P, P])
        c.ident = sb("ident", [P, P])
        c.ones = sb("ones", [P, P])
        c.valid = sb("valid", [P, P])
        c.eps = sb("eps", [P, 1])
        c.id_st = sb("id_st", [P, GT], I32)
        c.pass_sems = ([sem(f"rec{u}") for u in range(RING)], sem("item"), sem("lg"), sem("ex"), sem("weighed"), sem("acc"))
        c.project_sems = tuple(sem("p_" + n) for n in ("staged", "turned", "copied", "mm", "rows", "scat", "free"))
        constants(c)
        edge_projection_and_search(c)
        sort_nodes(c)
        item_list(c)
        item_records(c)
        load_nodes(c)
        if dump and stop == "prep":
            return dump(c)
        load_weights(c)
        project(c, 0)
        edge_pass(c, "L0")
        close_layer0(c)
        if stop == "L0":
            return dump(c)
        project(c, 1)
        edge_pass(c, "L1")
        close_layer1(c)
        if stop == "L1":
            return dump(c)
        project(c, 2)
        edge_pass(c, "L2")
        close_layer2(c)
        if stop == "L2":
            return dump(c)
        project(c, 3)
        edge_pass(c, "L3a")
        attention_scale(c)
        edge_pass(c, "L3b")
        gradient_norm(c)
        project(c, 4)
        edge_pass(c, "L3c")
        close_layer3(c)
        store_nodes(c)


def constants(c):
    nc = c.nc
    iota_done, made = c.sem("iota_done"), c.sem("const_made")
    with nc.Block() as block:
        @block.gpsimd
        def _(pool):
            nc.gpsimd.iota(c.slot[:], pattern=[[1, SLOTS]], base=0, channel_multiplier=0,
                           allow_small_or_imprecise_dtypes=True)
            nc.gpsimd.iota(c.diag[:], pattern=[[1, P]], base=0, channel_multiplier=-1,
                           allow_small_or_imprecise_dtypes=True).then_inc(iota_done, 1)

        @block.vector
        def _(dve):
            nc.vector.memset(c.ones[:], 1.0)
            nc.vector.memset(c.valid[:], 0.0)
            nc.vector.memset(c.eps[:], 1e-5)
            dve.drain()
            nc.vector.memset(c.valid[0:LAST - LAST % 32, :], 1.0)
            dve.wait_ge(iota_done, 1)
            nc.vector.tensor_scalar(c.ident[:], c.diag[:], 0.0, None, ALU.is_equal)
            dve.drain()
            nc.vector.tensor_reduce(c.valid[96:P, 0:1], c.ident[96:P, 0:LAST], X_AXIS, ALU.add)
            dve.drain()
            nc.vector.tensor_scalar(c.valid[96:P, :], c.ones[96:P, :], c.valid[96:P, 0:1], None,
                                    ALU.mult).then_inc(made, 1)


def edge_projection_and_search(c):
    nc, w = c.nc, c.w
    sem = c.sem
    with ExitStack() as local:
        sb = lambda n, s, d=F32: c.sb(n, s, d, local)
        ps = lambda n, s: local.enter_context(nc.psum_tensor(n, s, F32))
        w_eg = sb("w_eg", [16, F])
        w_egT = sb("w_egT", [F, 16])
        feat = sb("feat", [P, 3, ER, F])
        featT = sb("featT", [P, 2, ER, P])
        res = sb("res", [P, 2, ER, 16])
        tailf = sb("tailf", [16, F])
        zeros = sb("zeros", [1, 16 * SLOTS])
        zeros_i = sb("zeros_i", [1, 16], I32)
        node = sb("node", [P, T])
        heads = sb("heads", [P, NBLK], I32)
        less = sb("less", [P, GT, NBLK])
        cnt = sb("cnt", [P, GT])
        blk = sb("blk", [P, GT])
        blk_i = sb("blk_i", [P, GT], I32)
        rows = sb("rows", [P, GT, BLK], I32)
        pT = [ps(f"pT{i}", [P, 4, P]) for i in range(3)]
        pO = [ps(f"pO{i}", [P, ER, 16]) for i in range(2)]
        w_in, w_ready, w_t = sem("eg_w_in"), sem("eg_w_ready"), sem("eg_w_t")
        feat_in = [sem(f"feat_in{i}") for i in range(3)]
        tr_done, tr_copied, mm_done, res_done = sem("eg_tr"), sem("eg_copied"), sem("eg_mm"), sem("eg_res")
        res_out = [sem(f"res_out{i}") for i in range(2)]
        heads_out, heads_in, pads = sem("heads_out"), sem("heads_in"), sem("pads")
        wins, zero_done = sem("wins"), sem("zero_done")
        node_done, blk_done, rows_in = sem("node_done"), sem("blk_done"), sem("rows_in")
        ea = c.edge_attr[0:P * E_MAIN, :].rearrange("(p s r) f -> s p r f", p=P, r=ER)
        eg = c.edge_gate[0:P * E_MAIN, :].rearrange("(p s r) f -> s p r f", p=P, r=ER)
        with nc.Block() as block:
            @block.sync
            def _(sp):
                sp.dma_start(w_eg[0:8, :], w["L0_gnn_Wedge"]).then_inc(w_in, 16)
                sp.dma_start(w_eg[8:16, :], w["L0_gnn_Wgate"]).then_inc(w_in, 16)
                sp.dma_start(tailf[0:E_TAIL, :], c.edge_attr[P * E_MAIN:E, :]).then_inc(w_in, 16)
                sp.dma_start(c.samples_d, c.dst.rearrange("(b r) -> r b", r=BLK)[0:1, :],
                             allow_slow_non_contiguous=True).then_inc(heads_out, 16)
                sp.wait_ge(heads_out, 16)
                sp.dma_start(heads[:], c.samples_d.to_broadcast([P, NBLK])).then_inc(heads_in, 16)
                sp.dma_start(c.src_pad[0:E].rearrange("(a b) -> a b", a=50),
                             c.src.rearrange("(a b) -> a b", a=50)).then_inc(pads, 16)
                sp.wait_ge(zero_done, 1)
                sp.dma_start(c.src_pad[E:E + 16].rearrange("(a b) -> a b", a=1), zeros_i[:]).then_inc(pads, 16)
                sp.dma_start(c.edge_gate[E:E + SLOTS, :].rearrange("(o a) b -> o (a b)", o=1), zeros[:]).then_inc(pads, 16)
                for i in range(2):
                    sp.dma_start(feat[:, i, :, :], ea[i]).then_inc(feat_in[i], 16)
                sp.wait_ge(pads, 48)
                h = E // 2
                for a, b in ((0, h), (h, E + 1)):
                    sp.dma_start(c.src_win[a:b, :], bass.AP(c.src_pad.tensor, a, [[1, b - a], [1, SLOTS]])).then_inc(wins, 16)
                for i in range(2, ESTEPS):
                    if i >= 3:
                        sp.wait_ge(tr_done, 3 * (i - 2))
                    sp.dma_start(feat[:, i % 3, :, :], ea[i]).then_inc(feat_in[i % 3], 16)
                sp.wait_ge(wins, 32)

            @block.tensor
            def _(pe):
                pe.wait_ge(w_in, 48)
                nc.tensor.transpose(pT[0][:, 0, 0:16], w_eg[:], c.ident[0:16, 0:16])
                nc.tensor.transpose(pT[0][:, 1, 0:E_TAIL], tailf[0:E_TAIL, :], c.ident[0:E_TAIL, 0:E_TAIL]).then_inc(w_ready, 1)
                pe.wait_ge(w_t, 1)
                nc.tensor.matmul(pO[0][0:E_TAIL, 0, :], featT[:, 0, 0, 0:E_TAIL], w_egT[:], start=True, stop=True).then_inc(w_ready, 1)

                def project_step(i):
                    pe.wait_ge(tr_copied, 3 * (i + 1))
                    if i != 1:
                        pe.wait_ge(res_done, max(i, 1))
                    for r in range(ER):
                        mm = nc.tensor.matmul(pO[i % 2][:, r, :], featT[:, i % 2, r, :], w_egT[:], start=True, stop=True)
                    mm.then_inc(mm_done, 1)

                for i in range(ESTEPS):
                    pe.wait_ge(feat_in[i % 3], 16 * (i // 3 + 1))
                    for q, (a, b) in enumerate(((0, 4), (4, 8), (8, ER))):
                        if i:
                            pe.wait_ge(tr_copied, 3 * (i - 1) + q + 1)
                        else:
                            pe.wait_ge(w_t, 1)
                        for r in range(a, b):
                            mm = nc.tensor.transpose(pT[q][:, r - a, :], feat[:, i % 3, r, :], c.ident[:])
                        mm.then_inc(tr_done, 1)
                    if i:
                        project_step(i - 1)
                project_step(ESTEPS - 1)

            @block.scalar
            def _(act):
                act.wait_ge(w_ready, 1)
                nc.scalar.copy(w_egT[:], pT[0][:, 0, 0:16])
                nc.scalar.copy(featT[:, 0, 0, 0:E_TAIL], pT[0][:, 1, 0:E_TAIL]).then_inc(w_t, 1)
                act.wait_ge(w_ready, 2)
                nc.scalar.copy(res[0:E_TAIL, 0, 0, 0:8], pO[0][0:E_TAIL, 0, 0:8])
                nc.scalar.activation(res[0:E_TAIL, 0, 0, 8:16], pO[0][0:E_TAIL, 0, 8:16], ACT.Sigmoid).then_inc(res_done, 1)
                act.wait_ge(res_done, 1)
                act.dma_start(c.edge_gate[P * E_MAIN:E, :], res[0:E_TAIL, 0, 0, :]).then_inc(res_out[0], 16)

                def results(i):
                    act.wait_ge(mm_done, i + 1)
                    n = (i // 2 + (1 if i % 2 == 0 else 0))
                    if n:
                        act.wait_ge(res_out[i % 2], 16 * n)
                    nc.scalar.copy(res[:, i % 2, :, 0:8], pO[i % 2][:, :, 0:8])
                    nc.scalar.activation(res[:, i % 2, :, 8:16], pO[i % 2][:, :, 8:16], ACT.Sigmoid).then_inc(res_done, 1)
                    act.wait_ge(res_done, i + 2)
                    act.dma_start(eg[i], res[:, i % 2, :, :]).then_inc(res_out[i % 2], 16)

                for i in range(ESTEPS):
                    for q, (a, b) in enumerate(((0, 4), (4, 8), (8, ER))):
                        act.wait_ge(tr_done, 3 * i + q + 1)
                        if i >= 2:
                            act.wait_ge(mm_done, i - 1)
                        nc.scalar.copy(featT[:, i % 2, a:b, :], pT[q][:, 0:b - a, :]).then_inc(tr_copied, 1)
                    if i:
                        results(i - 1)
                results(ESTEPS - 1)
                act.wait_ge(res_out[0], 16 * (1 + (ESTEPS + 1) // 2))
                act.wait_ge(res_out[1], 16 * (ESTEPS // 2))

            @block.gpsimd
            def _(pool):
                nc.gpsimd.iota(node[:], pattern=[[P, T]], base=0, channel_multiplier=1,
                               allow_small_or_imprecise_dtypes=True).then_inc(node_done, 1)
                dst_rows = c.dst.rearrange("(b r) -> b r", r=BLK)
                with pool.Fori(0, NG) as g:
                    pool.wait_ge(blk_done, g + 1)
                    held(c, pool)
                    for k in range(GT):
                        pool.indirect_dma_start(out=rows[:, k, :], out_offset=None, in_=dst_rows,
                                                in_offset=bass.IndirectOffsetOnAxis(ap=blk_i[:, k:k + 1], axis=0)).then_inc(rows_in, 16)

            @block.vector
            def _(dve):
                nc.vector.memset(zeros[:], 0.0)
                nc.vector.memset(zeros_i[:], 0).then_inc(zero_done, 1)
                dve.wait_ge(node_done, 1)
                dve.wait_ge(heads_in, 16)
                with dve.Fori(0, NG) as g:
                    nodes = node[:, bass.ds(g * GT, GT)].unsqueeze(2)
                    nc.vector.tensor_tensor(less[:], heads[:].unsqueeze(1).to_broadcast([P, GT, NBLK]),
                                            nodes.to_broadcast([P, GT, NBLK]), ALU.is_lt)
                    dve.drain()
                    nc.vector.tensor_reduce(cnt[:], less[:], X_AXIS, ALU.add)
                    dve.drain()
                    nc.vector.tensor_scalar(blk[:], cnt[:], -1.0, 0.0, ALU.add, ALU.max)
                    dve.drain()
                    nc.vector.tensor_copy(blk_i[:], blk[:]).then_inc(blk_done, 1)
                    dve.wait_ge(rows_in, (g + 1) * (16 * GT))
                    nc.vector.tensor_tensor(less[:, :, 0:BLK], rows[:], nodes.to_broadcast([P, GT, BLK]), ALU.is_lt)
                    dve.drain()
                    nc.vector.tensor_reduce(cnt[:], less[:, :, 0:BLK], X_AXIS, ALU.add)
                    dve.drain()
                    nc.vector.scalar_tensor_tensor(c.start[:, bass.ds(g * GT, GT)], blk[:], float(BLK), cnt[:], ALU.mult, ALU.add)
                    dve.drain()


def sort_nodes(c):
    nc, sem = c.nc, c.sem
    B = BUCKETS
    with ExitStack() as local:
        sb = lambda n, s, d=F32: c.sb(n, s, d, local)
        up1 = sb("up1", [P, P])
        up127 = sb("up127", [P, P])
        below = sb("below", [P, P], BF16)
        ones_b = sb("ones_b", [P, P], BF16)
        nxt = sb("nxt", [P, T])
        deg = sb("deg0", [P, T])
        cls = sb("cls", [P, T])
        cls_io = sb("cls_io", [P, B])
        hot = sb("hot", [P, B, T], BF16)
        tot = sb("tot", [P, B * T])
        incl = sb("incl", [P, B * T])
        zero = sb("zero", [P, B * T])
        rank = sb("rank", [P, T])
        rank_i = sb("rank_i", [P, T], I32)
        node_f = sb("node_f", [P, T])
        recs = sb("recs", [P, T, 4], I32)
        rank_st = sb("rank_st", [P, GT], I32)
        rec_st = sb("rec_st", [P, GT, 4], I32)
        back = sb("back", [P, T, 4], I32)
        CH = B * T // 7
        pn = local.enter_context(nc.psum_tensor("pn", [P, T], F32))
        pc = local.enter_context(nc.psum_tensor("pc", [P, 7, 512], F32))
        io, mats, shifted, hot_done, tots, tot_got, pres, rank_done = (
            sem(n) for n in ("so_io", "so_mats", "so_shift", "so_hot", "so_tots", "so_got", "so_pres", "so_rank"))
        order_out, order_in, gwin = sem("order_out"), sem("order_in"), sem("gwin")
        hotf = hot[:].rearrange("p b t -> p (b t)")
        with nc.Block() as block:
            @block.scalar
            def _(act):
                n = 4
                cuts = [(E + 1) * i // n for i in range(n + 1)]
                for a, b in zip(cuts, cuts[1:]):
                    act.dma_start(c.gate_win[a:b, :], bass.AP(c.edge_gate.tensor, 16 * a, [[16, b - a], [1, 16 * SLOTS]])).then_inc(gwin, 16)
                act.wait_ge(gwin, 16 * n)

            @block.gpsimd
            def _(pool):
                nc.gpsimd.iota(node_f[:], pattern=[[P, T]], base=0, channel_multiplier=1, allow_small_or_imprecise_dtypes=True)
                nc.gpsimd.iota(cls_io[:], pattern=[[1, B]], base=0, channel_multiplier=0,
                               allow_small_or_imprecise_dtypes=True).then_inc(io, 1)
                pool.wait_ge(rank_done, 1)
                with pool.Fori(0, NG) as g:
                    nc.gpsimd.tensor_copy(rank_st[:], rank_i[:, bass.ds(g * GT, GT)])
                    nc.gpsimd.tensor_copy(rec_st[:], recs[:, bass.ds(g * GT, GT), :])
                    pool.drain()
                    for k in range(GT):
                        pool.indirect_dma_start(out=c.order, out_offset=bass.IndirectOffsetOnAxis(ap=rank_st[:, k:k + 1], axis=0),
                                                in_=rec_st[:, k, :], in_offset=None).then_inc(order_out, 16)
                    pool.wait_ge(order_out, (g + 1) * (16 * GT))
                    held(c, pool)

            @block.sync
            def _(sp):
                sp.wait_ge(order_out, 16 * T)
                sp.dma_start(back[:], c.order.rearrange("(t p) c -> p t c", p=P)).then_inc(order_in, 16)
                sp.wait_ge(order_in, 16)

            @block.tensor
            def _(pe):
                pe.wait_ge(mats, 1)
                nc.tensor.matmul(pn[:], up1[:], c.start[:], start=True, stop=False)
                nc.tensor.matmul(pn[:], up127[:], nxt[:], start=False, stop=True).then_inc(shifted, 1)
                pe.wait_ge(hot_done, 1)
                for k in range(7):
                    mm = nc.tensor.matmul(pc[:, k, 0:CH], ones_b[:], hotf[:, k * CH:(k + 1) * CH], start=True, stop=True)
                mm.then_inc(tots, 1)
                pe.wait_ge(tot_got, 1)
                for k in range(7):
                    mm = nc.tensor.matmul(pc[:, k, 0:CH], below[:], hotf[:, k * CH:(k + 1) * CH], start=True, stop=True)
                mm.then_inc(pres, 1)

            @block.vector
            def _(dve):
                v = nc.vector
                v.tensor_scalar(up1[:], c.diag[:], -1.0, None, ALU.is_equal)
                v.tensor_scalar(up127[:], c.diag[:], 127.0, None, ALU.is_equal)
                v.tensor_scalar(below[:], c.diag[:], 0.0, None, ALU.is_gt)
                v.memset(ones_b[:], 1.0)
                v.memset(zero[:], 0.0)
                v.memset(nxt[:, T - 1:T], float(E))
                v.memset(recs[:], 0)
                v.tensor_copy(nxt[:, 0:T - 1], c.start[:, 1:T]).then_inc(mats, 1)
                dve.wait_ge(shifted, 1)
                v.tensor_tensor(deg[:], pn[:], c.start[:], ALU.subtract)
                dve.drain()
                v.tensor_scalar(cls[:], deg[:], -1.0, float(B - 1), ALU.mult, ALU.add)
                dve.drain()
                v.tensor_scalar(cls[:], cls[:], 0.0, None, ALU.max)
                dve.drain()
                dve.wait_ge(io, 1)
                v.tensor_tensor(hot[:], cls_io[:].unsqueeze(2).to_broadcast([P, B, T]),
                                cls[:].unsqueeze(1).to_broadcast([P, B, T]), ALU.is_equal).then_inc(hot_done, 1)
                dve.wait_ge(tots, 1)
                v.tensor_copy(tot[:].rearrange("p (a b) -> p a b", a=7), pc[:, :, 0:CH]).then_inc(tot_got, 1)
                dve.drain()
                v.tensor_tensor_scan(incl[:], tot[:], zero[:], 0.0, ALU.add, ALU.add)
                dve.drain()
                v.tensor_tensor(incl[:], incl[:], tot[:], ALU.subtract)
                dve.drain()
                dve.wait_ge(pres, 1)
                v.tensor_tensor(incl[:].rearrange("p (a b) -> p a b", a=7), incl[:].rearrange("p (a b) -> p a b", a=7),
                                pc[:, :, 0:CH], ALU.add)
                dve.drain()
                v.tensor_tensor(incl[:], incl[:], hotf, ALU.mult)
                dve.drain()
                v.tensor_reduce(rank[:], incl[:].rearrange("p (b t) -> p t b", t=T), X_AXIS, ALU.add)
                v.tensor_copy(recs[:, :, 0], node_f[:])
                v.tensor_copy(recs[:, :, 1], c.start[:])
                v.tensor_copy(recs[:, :, 2], deg[:])
                dve.drain()
                v.tensor_copy(rank_i[:], rank[:]).then_inc(rank_done, 1)
                dve.wait_ge(order_in, 16)
                v.tensor_copy(c.ids[:], back[:, :, 0])
                v.tensor_copy(c.first[:], back[:, :, 1])
                v.tensor_copy(c.deg[:], back[:, :, 2])


def item_list(c):
    nc, sem = c.nc, c.sem
    W = LIST_W
    with ExitStack() as local:
        sb = lambda n, s, d=F32: c.sb(n, s, d, local)
        jmax = sb("jmax", [T, 2])
        jint = sb("jint", [T, 1], I32)
        dj = sb("dj", [T, 2, T])
        jn = sb("jn", [P, 2, T])
        iend = sb("iend", [P, T])
        ibeg = sb("ibeg", [P, T])
        zero = sb("zero2", [P, T])
        item = sb("item", [P, W])
        past = sb("past", [P, W, T])
        begun = sb("begun", [P, W, T])
        tile_of = sb("tile_of", [P, W])
        base = sb("base", [P, W])
        jm = sb("jm", [P, W])
        s0 = sb("s0", [P, W])
        meta = sb("meta", [P, W, 4], I32)
        nb = sb("nb", [1, 1])
        before = sb("before", [P, P])
        cum = sb("cum", [P, W // RING, RING])
        zw = sb("zw", [P, W // RING])
        pcum = local.enter_context(nc.psum_tensor("pcum", [P, RING], F32))
        nbi = sb("nbi", [1, 1], I32)
        pt = local.enter_context(nc.psum_tensor("pt", [P, P], F32))
        pj = local.enter_context(nc.psum_tensor("pj", [P, 2 * T], F32))
        io, tr, dj_done, bcast, meta_done, meta_out, rows_done, rows_sum = (
            sem(n) for n in ("il_io", "il_tr", "il_dj", "il_bc", "il_meta", "il_out", "il_rows", "il_rsum"))
        with nc.Block() as block:
            @block.gpsimd
            def _(pool):
                nc.gpsimd.iota(item[:], pattern=[[1, W]], base=0, channel_multiplier=W,
                               allow_small_or_imprecise_dtypes=True).then_inc(io, 1)

            @block.tensor
            def _(pe):
                nc.tensor.transpose(pt[0:T, :], c.deg[:], c.ident[:]).then_inc(tr, 1)
                pe.wait_ge(dj_done, 1)
                nc.tensor.matmul(pj[:], c.ones[0:T, :], dj[:].rearrange("a b t -> a (b t)"), start=True, stop=True).then_inc(bcast, 1)
                pe.wait_ge(rows_done, 1)
                nc.tensor.matmul(pcum[:], before[:], cum[:, W // RING - 1, :], start=True, stop=True).then_inc(rows_sum, 1)

            @block.vector
            def _(dve):
                v = nc.vector
                dve.wait_ge(tr, 1)
                v.tensor_reduce(jmax[:, 0:1], pt[0:T, :], X_AXIS, ALU.max)
                dve.drain()
                v.tensor_scalar(jint[:], jmax[:, 0:1], float(SLOTS - 1), None, ALU.add)
                dve.drain()
                v.tensor_scalar(jint[:], jint[:], 3, None, ALU.logical_shift_right)
                dve.drain()
                v.tensor_copy(jmax[:, 1:2], jint[:])
                dve.drain()
                v.tensor_scalar(dj[:, 0, :], c.ident[0:T, 0:T], jmax[:, 0:1], None, ALU.mult)
                v.tensor_scalar(dj[:, 1, :], c.ident[0:T, 0:T], jmax[:, 1:2], None, ALU.mult).then_inc(dj_done, 1)
                v.memset(zero[:], 0.0)
                v.memset(meta[:], 0)
                dve.wait_ge(bcast, 1)
                v.tensor_copy(jn[:].rearrange("p b t -> p (b t)"), pj[:])
                dve.drain()
                v.tensor_tensor_scan(iend[:], jn[:, 1, :], zero[:], 0.0, ALU.add, ALU.add)
                dve.drain()
                v.tensor_tensor(ibeg[:], iend[:], jn[:, 1, :], ALU.subtract)
                v.tensor_scalar(nb[:], iend[0:1, T - 1:T], float(RING - 1), None, ALU.add)
                dve.wait_ge(io, 1)
                ib = item[:].unsqueeze(2).to_broadcast([P, W, T])
                bt = lambda a: a.unsqueeze(1).to_broadcast([P, W, T])
                dve.drain()
                v.tensor_copy(nbi[:], nb[:])
                v.tensor_tensor(past[:], bt(iend[:]), ib, ALU.is_le)
                v.tensor_tensor(begun[:], bt(ibeg[:]), ib, ALU.is_le)
                dve.drain()
                v.tensor_scalar(c.bodies[:], nbi[:], 2, None, ALU.logical_shift_right)
                v.tensor_reduce(tile_of[:], past[:], X_AXIS, ALU.add)
                v.tensor_tensor(begun[:], begun[:], past[:], ALU.subtract)
                dve.drain()
                v.tensor_tensor(past[:], past[:], bt(jn[:, 1, :]), ALU.mult)
                v.tensor_tensor(begun[:], begun[:], bt(jn[:, 0, :]), ALU.mult)
                dve.drain()
                v.tensor_reduce(base[:], past[:], X_AXIS, ALU.add)
                v.tensor_reduce(jm[:], begun[:], X_AXIS, ALU.add)
                dve.drain()
                v.tensor_tensor(s0[:], item[:], base[:], ALU.subtract)
                dve.drain()
                v.tensor_scalar(s0[:], s0[:], float(SLOTS), None, ALU.mult)
                dve.drain()
                v.tensor_tensor(jm[:], jm[:], s0[:], ALU.subtract)
                dve.drain()
                v.tensor_scalar(meta[:, :, 0], tile_of[:], float(T - 1), None, ALU.min)
                v.tensor_scalar(jm[:], jm[:], 0.0, float(SLOTS), ALU.max, ALU.min)
                v.tensor_copy(meta[:, :, 2], s0[:])
                v.tensor_scalar(before[:], c.diag[:], 0.0, None, ALU.is_gt)
                v.memset(zw[:], 0.0)
                dve.drain()
                v.tensor_copy(meta[:, :, 1], jm[:])
                jq = jm[:].rearrange("p (q u) -> p q u", u=RING)
                for u in range(RING):
                    last = v.tensor_tensor_scan(cum[:, :, u], jq[:, :, u], zw[:], 0.0, ALU.add, ALU.add)
                last.then_inc(rows_done, 1)
                dve.wait_ge(rows_sum, 1)
                v.tensor_tensor(meta[:, :, 3].rearrange("p (q u) -> p q u", u=RING), cum[:],
                                pcum[:].unsqueeze(1).to_broadcast([P, W // RING, RING]), ALU.add).then_inc(meta_done, 1)

            @block.sync
            def _(sp):
                sp.wait_ge(meta_done, 1)
                sp.dma_start(c.meta_d.rearrange("(p w) c -> p w c", p=P), meta[:]).then_inc(meta_out, 16)
                sp.wait_ge(meta_out, 16)


def held(c, eng):
    eng.sem_inc(c.passed, 1)


def body_count(c, eng):
    return eng.value_load(c.bodies[0:1, 0:1], min_val=1, max_val=CAP // RING)


def item_records(c):
    nc, sem = c.nc, c.sem
    with ExitStack() as local:
        sb = lambda n, s, d=F32: c.sb(n, s, d, local)
        meta = sb("meta_all", [P, RING, 4], I32)
        rec = sb("rec_b", [P, RING, REC], I32)
        s0 = sb("s0f", [P, RING])
        offf = sb("offf", [P, RING])
        off = sb("off", [P, RING], I32)
        left = sb("left", [P, RING])
        win = [sb(f"win{u}", [P, SLOTS], I32) for u in range(RING)]
        meta_in = [sem(f"ir_meta{u}") for u in range(RING)]
        off_done, rec_done, freed = sem("ir_off"), sem("ir_rec"), sem("ir_freed")
        win_in = [sem(f"ir_win{u}") for u in range(RING)]
        rec_out = [sem(f"ir_out{u}") for u in range(RING)]
        maskf = rec[:].bitcast(F32)
        with nc.Block() as block:
            @block.sync
            def _(sp):
                nb = body_count(c, sp)
                sp.wait_ge(freed, 1)
                with sp.Fori(0, nb) as b:
                    for u in range(RING):
                        sp.wait_ge(freed, b * RING + (u + 1))
                        sp.dma_start(meta[:, u, :], c.meta_d[bass.ds(b * RING + u, 1), :].to_broadcast([P, 4])).then_inc(meta_in[u], 16)

            @block.gpsimd
            def _(pool):
                nb = body_count(c, pool)
                with pool.Fori(0, nb) as b:
                    for u in range(RING):
                        pool.wait_ge(off_done, b * RING + (u + 1))
                        held(c, pool)
                        pool.indirect_dma_start(out=win[u][:], out_offset=None, in_=c.src_win,
                                                in_offset=bass.IndirectOffsetOnAxis(ap=off[:, u:u + 1], axis=0)).then_inc(win_in[u], 16)

            @block.vector
            def _(dve):
                v = nc.vector
                v.memset(rec[:], 0).then_inc(freed, RING)
                nb = body_count(c, dve)
                with dve.Fori(0, nb) as b:
                    for u in range(RING):
                        dve.wait_ge(meta_in[u], (b + 1) * 16)
                        held(c, dve)
                        t = dve.value_load(meta[0:1, u, 0:1], min_val=0, max_val=T - 1)
                        v.tensor_tensor(offf[:, u:u + 1], c.first[:, bass.ds(t, 1)], meta[:, u, 2:3], ALU.add)
                        v.tensor_tensor(left[:, u:u + 1], c.deg[:, bass.ds(t, 1)], meta[:, u, 2:3], ALU.subtract)
                        dve.drain()
                        v.tensor_scalar(off[:, u:u + 1], offf[:, u:u + 1], float(E), None, ALU.min).then_inc(off_done, 1)
                    for u in range(RING):
                        dve.wait_ge(rec_out[u], b * 16 + 16)
                        dve.wait_ge(win_in[u], (b + 1) * 16)
                        v.tensor_copy(rec[:, u, 0:SLOTS], win[u][:])
                        v.tensor_copy(rec[:, u, SLOTS:SLOTS + 1], off[:, u:u + 1])
                        v.tensor_scalar(maskf[:, u, MASK_AT:MASK_AT + SLOTS], c.slot[:], left[:, u:u + 1], MASKED,
                                        ALU.is_ge, ALU.mult)
                        dve.drain()
                        dve.sem_inc(rec_done, 1)
                        dve.sem_inc(freed, 1)

            @block.scalar
            def _(act):
                for u in range(RING):
                    act.sem_inc(rec_out[u], 16)
                nb = body_count(c, act)
                with act.Fori(0, nb) as b:
                    for u in range(RING):
                        act.wait_ge(rec_done, b * RING + (u + 1))
                        act.dma_start(c.rec_d[bass.ds(b * RING + u, 1), :, :].rearrange("o p c -> (o p) c"), rec[:, u, :]).then_inc(rec_out[u], 16)
                for u in range(RING):
                    act.wait_ge(rec_out[u], (nb + 1) * 16)
                held(c, act)


def load_nodes(c):
    nc = c.nc
    with ExitStack() as local:
        stage = c.sb("x_st", [P, 2, GT, F], F32, local)
        x_in, moved = [c.sem("x_in0"), c.sem("x_in1")], c.sem("x_moved")
        with nc.Block() as block:
            @block.gpsimd
            def _(pool):
                for g in range(NG):
                    if g >= 2:
                        pool.wait_ge(moved, g - 1)
                    for k in range(GT):
                        i = g * GT + k
                        n = LAST if i == T - 1 else P
                        pool.indirect_dma_start(out=stage[0:n, g % 2, k, :], out_offset=None, in_=c.x,
                                                in_offset=bass.IndirectOffsetOnAxis(ap=c.ids[0:n, i:i + 1], axis=0)).then_inc(x_in[g % 2], 16)

            @block.vector
            def _(dve):
                nc.vector.memset(c.X[:, T - 1, :], 0.0)
                dve.drain()
                for g in range(NG):
                    dve.wait_ge(x_in[g % 2], 16 * GT * (g // 2 + 1))
                    if g < NG - 1:
                        nc.vector.tensor_copy(c.X[:, g * GT:(g + 1) * GT, :], stage[:, g % 2, :, :]).then_inc(moved, 1)
                    else:
                        nc.vector.tensor_copy(c.X[:, g * GT:(g + 1) * GT - 1, :], stage[:, g % 2, 0:GT - 1, :])
                        nc.vector.tensor_copy(c.X[0:LAST, T - 1, :], stage[0:LAST, g % 2, GT - 1, :]).then_inc(moved, 1)


def store_nodes(c):
    nc = c.nc
    with ExitStack() as local:
        stage = c.sb("y_st", [P, GT, F], F32, local)
        y_out = c.sem("y_out")
        with nc.Block() as block:
            @block.gpsimd
            def _(pool):
                for g in range(NG):
                    for k in range(GT):
                        i = g * GT + k
                        n = LAST if i == T - 1 else P
                        pool.indirect_dma_start(out=c.out, out_offset=bass.IndirectOffsetOnAxis(ap=c.ids[0:n, i:i + 1], axis=0),
                                                in_=c.X[0:n, g * GT + k, :], in_offset=None).then_inc(y_out, 16)
                pool.wait_ge(y_out, 16 * T)


Q0, V0, K0, NODE0, W1, SRC2, DST2, KQ3 = (F * i for i in range(8))
PROJECTED = {0: (Q0, 3 * F), 1: (W1, F), 2: (SRC2, 2 * F), 3: (KQ3, F)}
TABLE_W = [2 * F, F + 4, F, 64 + F, F + 1]


def load_weights(c):
    nc, w = c.nc, c.w
    c.raw = c.sb("raw", [P, 6, F])
    c.wt = c.sb("wt", [P, 8 * F])
    c.att1 = c.sb("att1", [P, 2, F])
    c.att2 = c.sb("att2", [P, F])
    c.bias = c.sb("bias", [P, F])
    c.gamma = c.sb("gamma", [P, F])
    c.beta = c.sb("beta", [P, F])
    c.bkq = c.sb("bkq", [P, F])
    w_in, turned = c.sem("w_in"), c.sem("w_turned")
    with ExitStack() as local:
        pw = local.enter_context(nc.psum_tensor("pw", [P, 8, F], F32))
        with nc.Block() as block:
            @block.sync
            def _(sp):
                n = 0
                for i, name in enumerate(("L0_gnn_Wq", "L0_gnn_Wv", "L0_gnn_Wk", "L0_gnn_Wnode", "L1_gnn_W")):
                    sp.dma_start(c.raw[:, i, :], w[name]).then_inc(w_in, 16)
                sp.dma_start(c.raw[0:64, 5, :], w["L3_gnn_Wk"]).then_inc(w_in, 16)
                sp.dma_start(c.raw[64:P, 5, :], w["L3_gnn_Wq"]).then_inc(w_in, 16)
                sp.dma_start(c.wt[:, SRC2:SRC2 + F], w["L2_gnn_W_src"]).then_inc(w_in, 16)
                sp.dma_start(c.wt[:, DST2:DST2 + F], w["L2_gnn_W_dst"]).then_inc(w_in, 16)
                n = 9
                row = lambda v: v.rearrange("(a b) -> a b", a=1)
                flat = lambda v: row(v.rearrange("h d -> (h d)"))
                for to, of in ((c.att1[:, 0, :], flat(w["L1_gnn_att_src"])), (c.att1[:, 1, :], flat(w["L1_gnn_att_dst"])),
                               (c.att2[:], flat(w["L2_gnn_att"])), (c.bias[:], row(w["L2_gnn_bias"])),
                               (c.gamma[:], row(w["L2_gnn_bn_gamma"])), (c.beta[:], row(w["L2_gnn_bn_beta"])),
                               (c.bkq[:, 0:64], row(w["L3_gnn_bk"])), (c.bkq[:, 64:F], row(w["L3_gnn_bq"]))):
                    sp.dma_start(to, of.to_broadcast(list(to.shape))).then_inc(w_in, 16)
                    n += 1
                sp.wait_ge(w_in, 16 * n)

            @block.tensor
            def _(pe):
                pe.wait_ge(w_in, 16 * 17)
                for i in range(6):
                    mm = nc.tensor.transpose(pw[:, i, :], c.raw[:, i, :], c.ident[:])
                mm.then_inc(turned, 1)

            @block.vector
            def _(dve):
                dve.wait_ge(turned, 1)
                nc.vector.tensor_copy(c.wt[:, 0:5 * F].rearrange("p (a f) -> p a f", f=F), pw[:, 0:5, :])
                nc.vector.tensor_copy(c.wt[:, KQ3:KQ3 + F], pw[:, 5, :])


def project(c, layer):
    nc = c.nc
    R = TABLE_W[layer]
    col, width = PROJECTED.get(layer, (0, 0))
    tag = f"pr{layer}_"
    with ExitStack() as local:
        sb = lambda n, s, d=F32: c.sb(tag + n, s, d, local)
        ps = lambda n, s: local.enter_context(nc.psum_tensor(tag + n, s, F32))
        xg = sb("xg", [P, GT, F])
        xT = sb("xT", [P, 2, F])
        st = sb("st", [P, GT, R])
        tmp = sb("tmp", [P, 2, F])
        asd = sb("asd", [P, 12])
        pX = [ps(f"pX{i}", [P, 512]) for i in range(2)]
        pW = [ps(f"pW{i}", [P, 512]) for i in range(3)]
        staged, turned, copied, mm_done, rows_done, scat, stage_free = c.project_sems
        first = layer == 0
        with nc.Block() as block:
            @block.gpsimd
            def _(pool):
                if first:
                    pool.sem_inc(rows_done, 1)
                with pool.Fori(0, NG) as g:
                    G = g + NG * layer
                    pool.wait_ge(rows_done, G * GT + 1)
                    held(c, pool)
                    nc.gpsimd.tensor_copy(xg[:], c.X[:, bass.ds(g * GT, GT), :])
                    nc.gpsimd.tensor_copy(c.id_st[:], c.ids[:, bass.ds(g * GT, GT)])
                    pool.drain().then_inc(staged, 1)
                    for k in range(GT):
                        pool.wait_ge(rows_done, G * GT + (k + 2))
                        held(c, pool)
                        pool.indirect_dma_start(out=c.tab[layer], out_offset=bass.IndirectOffsetOnAxis(ap=c.id_st[:, k:k + 1], axis=0),
                                                in_=st[:, k, :], in_offset=None).then_inc(scat, 16)
                    pool.wait_ge(scat, (G + 1) * (16 * GT))
                    pool.sem_inc(stage_free, 1)

            if layer < 4:
                @block.tensor
                def _(pe):
                    def turn(G, k):
                        if k == 0:
                            pe.wait_ge(staged, G + 1)
                        if k >= 2:
                            pe.wait_ge(copied, G * GT + (k - 1))
                        nc.tensor.transpose(pX[k % 2][:, 0:F], xg[:, k, :], c.ident[:]).then_inc(turned, 1)

                    if first:
                        pe.sem_inc(mm_done, 1)
                    with pe.Fori(0, NG) as g:
                        G = g + NG * layer
                        turn(G, 0)
                        for k in range(GT):
                            if k + 1 < GT:
                                turn(G, k + 1)
                            pe.wait_ge(copied, G * GT + (k + 1))
                            if k >= 3:
                                pe.wait_ge(rows_done, G * GT + (k - 1))
                            nc.tensor.matmul(pW[k % 3][:, 0:width], xT[:, k % 2, :], c.wt[:, col:col + width],
                                             start=True, stop=True).then_inc(mm_done, 1)

                @block.scalar
                def _(act):
                    with act.Fori(0, NG) as g:
                        G = g + NG * layer
                        for k in range(GT):
                            act.wait_ge(turned, G * GT + (k + 1))
                            if k >= 2:
                                act.wait_ge(mm_done, G * GT + k)
                            nc.scalar.copy(xT[:, k % 2, :], pX[k % 2][:, 0:F]).then_inc(copied, 1)

            @block.vector
            def _(dve):
                v = nc.vector
                if first:
                    dve.sem_inc(stage_free, 1)
                if layer in (1, 2):
                    v.memset(c.S[:], 1.0)

                def at(a, t, n):
                    return a[:, bass.ds(t, 1), 0:n].rearrange("p a f -> p (a f)")

                with dve.Fori(0, NG) as g:
                    G = g + NG * layer
                    dve.wait_ge(stage_free, G + 1)
                    dve.wait_ge(staged, G + 1)
                    held(c, dve)
                    for k in range(GT):
                        t = g * GT + k
                        here = c.K[:, bass.ds(t, 1), :].rearrange("p a f -> p (a f)")
                        if layer < 4:
                            dve.wait_ge(mm_done, G * GT + (k + 2))
                            held(c, dve)
                        W = pW[k % 3]
                        if layer == 0:
                            v.tensor_copy(st[:, k, :], W[:, 0:2 * F])
                            v.tensor_copy(here, W[:, 2 * F:3 * F])
                        elif layer == 1:
                            v.tensor_copy(st[:, k, 0:F], W[:, 0:F])
                            v.tensor_tensor(tmp[:], W[:, 0:F].unsqueeze(1).to_broadcast([P, 2, F]), c.att1[:], ALU.mult)
                            dve.drain()
                            v.tensor_reduce(asd[:, 0:8], tmp[:].rearrange("p a (h d) -> p (a h) d", h=4), X_AXIS, ALU.add)
                            dve.drain()
                            v.tensor_copy(at(c.O, t, F), W[:, 0:F])
                            v.tensor_tensor(asd[:, 8:12], asd[:, 0:4], asd[:, 4:8], ALU.add)
                            dve.drain()
                            v.scalar_tensor_tensor(at(c.M, t, 4), asd[:, 8:12], 0.2, asd[:, 8:12], ALU.mult, ALU.max)
                            v.tensor_copy(st[:, k, F:F + 4], asd[:, 0:4])
                            v.tensor_copy(c.adst[:, bass.ds(t, 1), :].rearrange("p a f -> p (a f)"), asd[:, 4:8])
                        elif layer == 2:
                            v.tensor_copy(st[:, k, :], W[:, 0:F])
                            v.tensor_copy(here, W[:, F:2 * F])
                            v.tensor_copy(at(c.O, t, F), W[:, 0:F])
                            v.tensor_copy(tmp[:, 0, :], W[:, F:2 * F])
                            dve.drain()
                            v.tensor_tensor(tmp[:, 0, :], tmp[:, 0, :], W[:, 0:F], ALU.add)
                            dve.drain()
                            v.scalar_tensor_tensor(tmp[:, 0, :], tmp[:, 0, :], 0.2, tmp[:, 0, :], ALU.mult, ALU.max)
                            dve.drain()
                            v.tensor_tensor(tmp[:, 0, :], tmp[:, 0, :], c.att2[:], ALU.mult)
                            dve.drain()
                            v.tensor_reduce(at(c.M, t, 4), tmp[:, 0, :].rearrange("p (h d) -> p h d", h=4), X_AXIS, ALU.add)
                        elif layer == 3:
                            v.tensor_tensor(st[:, k, 0:64], W[:, 0:64], c.bkq[:, 0:64], ALU.add)
                            v.tensor_tensor(here[:, 0:64], W[:, 64:F], c.bkq[:, 64:F], ALU.add)
                            v.tensor_copy(st[:, k, 64:R], xg[:, k, :])
                        else:
                            v.tensor_copy(st[:, k, 0:F], xg[:, k, :])
                            v.tensor_copy(st[:, k, F:F + 1], c.g[:, bass.ds(t, 1)])
                        dve.drain().then_inc(rows_done, 1)


HEADS = {"L0": 8, "L1": 4, "L2": 4, "L3a": 4, "L3b": 4, "L3c": 1}
TABLE = {"L0": 0, "L1": 1, "L2": 2, "L3a": 3, "L3b": 3, "L3c": 4}


PASSES = ["L0", "L1", "L2", "L3a", "L3b", "L3c"]


def edge_pass(c, kind):
    nc = c.nc
    H, tab = HEADS[kind], c.tab[TABLE[kind]]
    R = TABLE_W[TABLE[kind]]
    tag = kind + "_"
    online = kind != "L3b"
    sums = kind != "L3a"
    rows_at = 64 if kind == "L3b" else F if kind == "L0" else 0
    with ExitStack() as local:
        sb = lambda n, s, d=F32: c.sb(tag + n, s, d, local)
        meta = sb("meta", [1, RING, 4], I32)
        rec = sb("rec", [P, RING, REC], I32)
        got = sb("got", [P, RING, SLOTS, R])
        gate = sb("gate", [P, RING, SLOTS, 16]) if kind == "L0" else None
        att = sb("att", [P, RING, SLOTS]) if kind in ("L3b", "L3c") else None
        prod = sb("prod", [P, SLOTS, F])
        wrow = sb("wrow", [P, 2, SLOTS, F])
        lg = sb("lg", [P, RING, SLOTS + 1, H])
        ex = sb("ex", [P, RING, SLOTS + 1, H])
        wt = sb("w", [P, SLOTS, H])
        mx = sb("mx", [P, H])
        mnew = sb("mnew", [P, H])
        psum_s = sb("ps", [P, H])
        rsum = sb("rsum", [P, 1])
        acc = [local.enter_context(nc.psum_tensor(tag + f"acc{i}", [P, 512], F32)) for i in range(2)]
        got_in = [c.sem(tag + f"got{u}") for u in range(RING)]
        att_out = [c.sem(tag + f"att{u}") for u in range(RING)] if kind == "L3b" else None
        att_done = c.sem(tag + "attd") if kind == "L3b" else None
        att_in = [c.sem(tag + f"atti{u}") for u in range(RING)] if kind == "L3c" else None
        rec_in, item_done, lg_done, ex_done, w_done, acc_done = c.pass_sems
        n_pass = PASSES.index(kind)
        n_sum = n_pass - (n_pass > PASSES.index("L3a"))
        maskf = rec[:].bitcast(F32)
        with nc.Block() as block:
            @block.vector
            def _(dve):
                v = nc.vector
                v.memset(got[:], 0.0)
                if kind not in ("L1", "L2"):
                    v.memset(c.O[:], 0.0)
                if online and kind not in ("L1", "L2"):
                    v.memset(c.S[:], 0.0)
                    v.memset(c.M[:], LOWEST)
                if kind == "L3c":
                    v.memset(c.rowsum[:], 0.0)
                v.memset(lg[:], 0.0)
        with nc.Block() as block:
            @block.sync
            def _(sp):
                nb = body_count(c, sp)
                with sp.Fori(0, nb) as b:
                    for u in range(RING):
                        i = b * RING + u
                        sp.wait_ge(item_done, (b + nb * n_pass) * RING + (u + 1))
                        sp.dma_start(meta[:, u, :], c.meta_d[bass.ds(i, 1), :]).then_inc(rec_in[u], 16)
                        sp.dma_start(rec[:, u, :], c.rec_d[bass.ds(i, 1), :, :].rearrange("o p c -> (o p) c")).then_inc(rec_in[u], 16)
                        if kind == "L3c":
                            sp.dma_start(att[:, u, :], c.att_d[bass.ds(i, 1), :, :].rearrange("o p c -> (o p) c")).then_inc(att_in[u], 16)

            @block.gpsimd
            def _(pool):
                nb = body_count(c, pool)
                with pool.Fori(0, nb) as b:
                    for u in range(RING):
                        pool.wait_ge(rec_in[u], (b + nb * n_pass) * 32 + 32)
                        held(c, pool)
                        used = pool.value_load(meta[0:1, u, 1:2], min_val=0, max_val=SLOTS)
                        if kind == "L0":
                            pool.indirect_dma_start(out=gate[:, u, :, :].rearrange("p j h -> p (j h)"), out_offset=None, in_=c.gate_win,
                                                    in_offset=bass.IndirectOffsetOnAxis(ap=rec[:, u, SLOTS:SLOTS + 1], axis=0)).then_inc(got_in[u], 16)
                        for j in range(SLOTS):
                            with pool.If(used > j):
                                pool.indirect_dma_start(out=got[:, u, j, :], out_offset=None, in_=tab,
                                                        in_offset=bass.IndirectOffsetOnAxis(ap=rec[:, u, j:j + 1], axis=0)).then_inc(got_in[u], 16)

            @block.scalar
            def _(act):
                rows = SLOTS + online
                nb = body_count(c, act)
                if kind == "L3b":
                    for u in range(RING):
                        act.sem_inc(att_out[u], 16)

                def keep(b, u):
                    act.wait_ge(att_done, b * RING + (u + 1))
                    act.dma_start(c.att_d[bass.ds(b * RING + u, 1), :, :].rearrange("o p c -> (o p) c"), att[:, u, :]).then_inc(att_out[u], 16)

                with act.Fori(0, nb) as b:
                    for u in range(RING):
                        act.wait_ge(lg_done, (b + nb * n_pass) * RING + (u + 1))
                        nc.scalar.activation(ex[:, u, 0:rows, :], lg[:, u, 0:rows, :], ACT.Exp).then_inc(ex_done, 1)
                        if kind == "L3b" and u >= 1:
                            keep(b, u - 1)
                    if kind == "L3b":
                        keep(b, RING - 1)
                if kind == "L3b":
                    for u in range(RING):
                        act.wait_ge(att_out[u], nb * 16 + 16)
                    held(c, act)

            if sums:
                @block.tensor
                def _(pe):
                    nb = body_count(c, pe)
                    with pe.Fori(0, nb) as b:
                        for u in range(RING):
                            pe.wait_ge(item_done, (b + nb * n_pass) * RING + (u + 3))
                            pe.wait_ge(w_done, (b + nb * n_sum) * RING + (u + 1))
                            for j in range(SLOTS):
                                mm = nc.tensor.matmul(acc[u % 2][:, 0:F], c.ident[:], wrow[:, u % 2, j, :],
                                                      start=(j == 0), stop=(j == SLOTS - 1))
                            mm.then_inc(acc_done, 1)

            @block.vector
            def _(dve):
                v = nc.vector
                if n_pass == 0:
                    dve.sem_inc(item_done, RING)
                nb = body_count(c, dve)
                tiles = {}

                def at(a, u, n):
                    return a[:, bass.ds(tiles[u], 1), 0:n].rearrange("p a f -> p (a f)")

                def over(ap, dims):
                    return ap.unsqueeze(1).to_broadcast(dims)

                def logits(b, u):
                    dve.wait_ge(rec_in[u], (b + nb * n_pass) * 32 + 32)
                    if kind == "L3c":
                        dve.wait_ge(att_in[u], b * 16 + 16)
                    held(c, dve)
                    tiles[u] = dve.value_load(meta[0:1, u, 0:1], min_val=0, max_val=T - 1)
                    gathers = dve.value_load(meta[0:1, u, 3:4], min_val=1, max_val=CAP * SLOTS)
                    dve.wait_ge(got_in[u], (gathers + (b + 1)) * 16 if kind == "L0" else gathers * 16)
                    l = lg[:, u, 0:SLOTS, :]
                    mask = maskf[:, u, MASK_AT:MASK_AT + SLOTS].unsqueeze(2).to_broadcast([P, SLOTS, H])
                    G = got[:, u, :, :]
                    if kind == "L0":
                        v.tensor_tensor(prod[:], G[:, :, 0:F], over(at(c.K, u, F), [P, SLOTS, F]), ALU.mult)
                        dve.drain()
                        v.tensor_reduce(l, prod[:].rearrange("p j (h d) -> p j h d", h=H), X_AXIS, ALU.add)
                        dve.drain()
                        v.tensor_scalar(l, l, 5.0, -5.0, ALU.min, ALU.max)
                        dve.drain()
                        v.tensor_tensor(l, l, gate[:, u, :, 0:8], ALU.add)
                        dve.drain()
                        v.scalar_tensor_tensor(l, l, L0_SCALE, mask, ALU.mult, ALU.add)
                    elif kind == "L1":
                        v.tensor_tensor(l, G[:, :, F:F + 4], over(at(c.adst, u, 4), [P, SLOTS, 4]), ALU.add)
                        dve.drain()
                        v.scalar_tensor_tensor(l, l, 0.2, l, ALU.mult, ALU.max)
                        dve.drain()
                        v.tensor_tensor(l, l, mask, ALU.add)
                    elif kind == "L2":
                        v.tensor_tensor(prod[:], G, over(at(c.K, u, F), [P, SLOTS, F]), ALU.add)
                        dve.drain()
                        v.scalar_tensor_tensor(prod[:], prod[:], 0.2, prod[:], ALU.mult, ALU.max)
                        dve.drain()
                        v.tensor_tensor(prod[:], prod[:], over(c.att2[:], [P, SLOTS, F]), ALU.mult)
                        dve.drain()
                        v.tensor_reduce(l, prod[:].rearrange("p j (h d) -> p j h d", h=H), X_AXIS, ALU.add)
                        dve.drain()
                        v.tensor_tensor(l, l, mask, ALU.add)
                    elif kind in ("L3a", "L3b"):
                        v.tensor_tensor(prod[:, :, 0:64], G[:, :, 0:64], over(at(c.K, u, 64), [P, SLOTS, 64]), ALU.mult)
                        dve.drain()
                        v.tensor_reduce(l, prod[:, :, 0:64].rearrange("p j (h d) -> p j h d", h=H), X_AXIS, ALU.add)
                        dve.drain()
                        v.scalar_tensor_tensor(l, l, 0.25, mask, ALU.mult, ALU.add)
                    else:
                        v.scalar_tensor_tensor(lg[:, u, 0:SLOTS, 0], G[:, :, F], c.g[:, bass.ds(tiles[u], 1)],
                                               maskf[:, u, MASK_AT:MASK_AT + SLOTS], ALU.add, ALU.add)
                    dve.drain()
                    M = at(c.M, u, H)
                    if online:
                        v.tensor_reduce(mx[:], l.rearrange("p j h -> p h j"), X_AXIS, ALU.max)
                        dve.drain()
                        v.tensor_tensor(mnew[:], M, mx[:], ALU.max)
                        dve.drain()
                        v.tensor_tensor(lg[:, u, SLOTS, :], M, mnew[:], ALU.subtract)
                        v.tensor_tensor(l, l, over(mnew[:], [P, SLOTS, H]), ALU.subtract).then_inc(lg_done, 1)
                        dve.drain()
                        v.tensor_copy(M, mnew[:])
                    else:
                        v.tensor_tensor(l, l, over(M, [P, SLOTS, H]), ALU.subtract).then_inc(lg_done, 1)

                def weigh(b, u):
                    dve.wait_ge(ex_done, (b + nb * n_pass) * RING + (u + 1))
                    held(c, dve)
                    e = ex[:, u, 0:SLOTS, :]
                    corr = ex[:, u, SLOTS, :]
                    if online:
                        v.tensor_reduce(psum_s[:], e.rearrange("p j h -> p h j"), X_AXIS, ALU.add)
                        v.tensor_tensor(at(c.S, u, H), at(c.S, u, H), corr, ALU.mult)
                    if kind == "L0":
                        v.tensor_tensor(wt[:], e, gate[:, u, :, 8:16], ALU.mult)
                    if kind == "L3b":
                        v.tensor_tensor(wt[:], e, over(at(c.rs, u, H), [P, SLOTS, H]), ALU.mult)
                        dve.wait_ge(att_out[u], b * 16 + 16)
                        held(c, dve)
                    if kind == "L3c":
                        v.tensor_tensor(wt[:, :, 0], ex[:, u, 0:SLOTS, 0], att[:, u, :], ALU.mult)
                    dve.drain()
                    if online:
                        v.tensor_tensor(at(c.S, u, H), at(c.S, u, H), psum_s[:], ALU.add)
                    if kind == "L3b":
                        v.tensor_reduce(att[:, u, :], wt[:], X_AXIS, ALU.add)
                        dve.drain().then_inc(att_done, 1)
                    if kind == "L3c":
                        r = c.rowsum[:, bass.ds(tiles[u], 1)]
                        v.tensor_reduce(rsum[:], wt[:, :, 0], X_AXIS, ALU.add)
                        v.tensor_tensor(r, r, corr, ALU.mult)
                        dve.drain()
                        v.tensor_tensor(r, r, rsum[:], ALU.add)
                    if sums:
                        x = got[:, u, :, rows_at:rows_at + F]
                        if kind in ("L3b", "L3c"):
                            a = att[:, u, :] if kind == "L3b" else wt[:, :, 0]
                            v.tensor_tensor(wrow[:, u % 2, :, :], x, a.unsqueeze(2).to_broadcast([P, SLOTS, F]),
                                            ALU.mult).then_inc(w_done, 1)
                        else:
                            a = wt[:] if kind == "L0" else e
                            v.tensor_tensor(wrow[:, u % 2, :, :].rearrange("p j (h d) -> p j h d", h=H),
                                            x.rearrange("p j (h d) -> p j h d", h=H),
                                            a.unsqueeze(3).to_broadcast([P, SLOTS, H, F // H]), ALU.mult).then_inc(w_done, 1)
                        if online:
                            o = at(c.O, u, F).rearrange("p (h d) -> p h d", h=H)
                            v.tensor_tensor(o, o, corr.unsqueeze(2).to_broadcast([P, H, F // H]), ALU.mult)
                    dve.drain()
                    if not sums:
                        dve.sem_inc(item_done, 1)

                def add_up(b, u):
                    if sums:
                        dve.wait_ge(acc_done, (b + nb * n_sum) * RING + (u + 1))
                        o = at(c.O, u, F)
                        v.tensor_tensor(o, o, acc[u % 2][:, 0:F], ALU.add)
                        dve.drain().then_inc(item_done, 1)

                with dve.Fori(0, nb) as b:
                    logits(b, 0)
                    for u in range(1, RING):
                        logits(b, u)
                        if u >= 2:
                            add_up(b, u - 2)
                        weigh(b, u - 1)
                    add_up(b, RING - 2)
                    weigh(b, RING - 1)
                    add_up(b, RING - 1)


def over_tiles(a, dims):
    return a.unsqueeze(1).to_broadcast(dims)


def layer_norm(c, dve, act, tag):
    nc = c.nc
    v = nc.vector
    centred, squared, summed, rooted = (c.sem(tag + n) for n in ("cen", "sq", "sum", "root"))

    def on_vector():
        full = [P, T, F]
        v.tensor_reduce(c.g[:], c.X[:], X_AXIS, ALU.add)
        dve.drain()
        v.tensor_scalar(c.g[:], c.g[:], 1.0 / F, None, ALU.mult)
        dve.drain()
        v.tensor_tensor(c.X[:], c.X[:], c.g[:].unsqueeze(2).to_broadcast(full), ALU.subtract).then_inc(centred, 1)
        dve.wait_ge(squared, 1)
        v.tensor_reduce(c.g[:], c.O[:], X_AXIS, ALU.add).then_inc(summed, 1)
        dve.wait_ge(rooted, 1)
        v.reciprocal(c.g[:], c.g[:])
        dve.drain()
        v.tensor_tensor(c.X[:], c.X[:], c.g[:].unsqueeze(2).to_broadcast(full), ALU.mult)

    def on_scalar():
        act.wait_ge(centred, 1)
        nc.scalar.activation(c.O[:], c.X[:], ACT.Square).then_inc(squared, 1)
        act.wait_ge(summed, 1)
        nc.scalar.activation(c.g[:], c.g[:], ACT.Sqrt, bias=c.eps[:], scale=1.0 / F).then_inc(rooted, 1)

    return on_vector, on_scalar


def normalise_sums(c, dve, H, floor, add):
    v = c.nc.vector
    s, r = c.S[:, :, 0:H], c.rs[:, :, 0:H]
    if add:
        v.tensor_scalar(r, s, add, None, ALU.add)
    else:
        v.tensor_scalar(r, s, floor, None, ALU.max)
    dve.drain()
    v.reciprocal(r, r)
    dve.drain()


def scale_rows(c, dve, H):
    o = c.O[:].rearrange("p t (h d) -> p (t h) d", h=H)
    r = c.rsd[:, 0:T * H]
    c.nc.vector.tensor_copy(r.rearrange("p (t h) -> p t h", h=H), c.rs[:, :, 0:H])
    dve.drain()
    c.nc.vector.tensor_tensor(o, o, r.unsqueeze(2).to_broadcast([P, T * H, F // H]), ALU.mult)
    dve.drain()


def close_layer0(c):
    nc = c.nc
    c.rsd = c.sb("rsd", [P, T * 8])
    with ExitStack() as local:
        ps = lambda n, s: local.enter_context(nc.psum_tensor(n, s, F32))
        og = c.sb("og", [P, GT, F], F32, local)
        oT = c.sb("oT", [P, 2, F], F32, local)
        pX = [ps(f"cX{i}", [P, 512]) for i in range(2)]
        pW = [ps(f"cW{i}", [P, 512]) for i in range(3)]
        staged, turned, copied, mm_done, taken = (c.sem("c0_" + n) for n in ("staged", "turned", "copied", "mm", "taken"))
        with nc.Block() as block:
            @block.vector
            def _(dve):
                normalise_sums(c, dve, 8, 1e-30, None)
                scale_rows(c, dve, 8)
                with dve.Fori(0, NG) as g:
                    nc.vector.tensor_copy(og[:], c.O[:, bass.ds(g * GT, GT), :]).then_inc(staged, 1)
                    for k in range(GT):
                        x = c.X[:, bass.ds(g * GT + k, 1), :].rearrange("p a f -> p (a f)")
                        dve.wait_ge(mm_done, g * GT + (k + 1))
                        nc.vector.tensor_tensor(x, x, pW[k % 3][:, 0:F], ALU.add).then_inc(taken, 1)

            @block.tensor
            def _(pe):
                def turn(g, k):
                    if k == 0:
                        pe.wait_ge(staged, g + 1)
                    if k >= 2:
                        pe.wait_ge(copied, g * GT + (k - 1))
                    nc.tensor.transpose(pX[k % 2][:, 0:F], og[:, k, :], c.ident[:]).then_inc(turned, 1)

                with pe.Fori(0, NG) as g:
                    turn(g, 0)
                    for k in range(GT):
                        if k + 1 < GT:
                            turn(g, k + 1)
                        pe.wait_ge(copied, g * GT + (k + 1))
                        if k >= 3:
                            pe.wait_ge(taken, g * GT + (k - 2))
                        nc.tensor.matmul(pW[k % 3][:, 0:F], oT[:, k % 2, :], c.wt[:, NODE0:NODE0 + F],
                                         start=True, stop=True).then_inc(mm_done, 1)

            @block.scalar
            def _(act):
                with act.Fori(0, NG) as g:
                    for k in range(GT):
                        act.wait_ge(turned, g * GT + (k + 1))
                        if k >= 2:
                            act.wait_ge(mm_done, g * GT + (k - 1))
                        nc.scalar.copy(oT[:, k % 2, :], pX[k % 2][:, 0:F]).then_inc(copied, 1)
    with nc.Block() as block:
        programs = {}

        @block.vector
        def _(dve):
            programs.update(zip("vs", layer_norm(c, dve, nc.scalar, "ln0_")))
            programs["v"]()

        @block.scalar
        def _(act):
            programs["s"]()


def close_layer1(c):
    nc = c.nc
    with nc.Block() as block:
        programs = {}

        @block.vector
        def _(dve):
            normalise_sums(c, dve, 4, None, 1e-16)
            scale_rows(c, dve, 4)
            nc.vector.tensor_tensor(c.X[:], c.X[:], c.O[:], ALU.add)
            dve.drain()
            programs.update(zip("vs", layer_norm(c, dve, nc.scalar, "ln1_")))
            programs["v"]()

        @block.scalar
        def _(act):
            programs["s"]()


def close_layer2(c):
    nc = c.nc
    full = [P, T, F]
    with ExitStack() as local:
        mean = c.sb("mean", [P, F], F32, local)
        sd = c.sb("sd", [P, F], F32, local)
        pm = local.enter_context(nc.psum_tensor("pm", [P, F], F32))
        pv = local.enter_context(nc.psum_tensor("pv", [P, F], F32))
        rows_done, summed, centred, squared, var_sum, rooted, rooted_in = (
            c.sem("c2_" + n) for n in ("rows", "sum", "cen", "sq", "var", "root", "rin"))
        with nc.Block() as block:
            programs = {}

            @block.vector
            def _(dve):
                v = nc.vector
                normalise_sums(c, dve, 4, 1e-30, None)
                scale_rows(c, dve, 4)
                v.tensor_tensor(c.O[:], c.O[:], over_tiles(c.bias[:], full), ALU.add).then_inc(rows_done, 1)
                dve.wait_ge(summed, 1)
                v.tensor_scalar(mean[:], pm[:], 1.0 / N, None, ALU.mult)
                dve.drain()
                v.tensor_tensor(c.O[:], c.O[:], over_tiles(mean[:], full), ALU.subtract).then_inc(centred, 1)
                dve.wait_ge(rooted, 1)
                v.reciprocal(sd[:], sd[:])
                dve.drain()
                v.tensor_tensor(sd[:], sd[:], c.gamma[:], ALU.mult)
                dve.drain()
                v.tensor_tensor(c.O[:], c.O[:], over_tiles(sd[:], full), ALU.mult)
                dve.drain()
                v.tensor_tensor(c.O[:], c.O[:], over_tiles(c.beta[:], full), ALU.add)
                dve.drain()
                v.scalar_tensor_tensor(c.O[:], c.O[:], 0.02, c.O[:], ALU.mult, ALU.max)
                dve.drain()
                v.tensor_tensor(c.X[:], c.X[:], c.O[:], ALU.add)
                dve.drain()
                programs.update(zip("vs", layer_norm(c, dve, nc.scalar, "ln2_")))
                programs["v"]()

            @block.tensor
            def _(pe):
                def sum_nodes(to, a, done):
                    nc.tensor.matmul(to[:], c.ones[:], a[:, 0, :], start=True, stop=False)
                    with pe.Fori(1, T - 1) as t:
                        nc.tensor.matmul(to[:], c.ones[:], a[:, bass.ds(t, 1), :].rearrange("p a f -> p (a f)"),
                                         start=False, stop=False)
                    nc.tensor.matmul(to[:], c.valid[:], a[:, T - 1, :], start=False, stop=True).then_inc(done, 1)

                pe.wait_ge(rows_done, 1)
                sum_nodes(pm, c.O, summed)
                pe.wait_ge(squared, 1)
                sum_nodes(pv, c.K, var_sum)

            @block.scalar
            def _(act):
                act.wait_ge(centred, 1)
                nc.scalar.activation(c.K[:], c.O[:], ACT.Square).then_inc(squared, 1)
                act.wait_ge(var_sum, 1)
                nc.scalar.activation(sd[:], pv[:], ACT.Sqrt, bias=c.eps[:], scale=1.0 / N).then_inc(rooted, 1)
                programs["s"]()


def attention_scale(c):
    nc = c.nc
    with nc.Block() as block:
        @block.vector
        def _(dve):
            normalise_sums(c, dve, 4, None, 1e-16)
            nc.vector.tensor_scalar(c.rs[:, :, 0:4], c.rs[:, :, 0:4], 0.25, None, ALU.mult)


def gradient_norm(c):
    nc = c.nc
    summed, rooted, minus, squared = (c.sem("gn_" + n) for n in ("sum", "root", "minus", "sq"))
    with nc.Block() as block:
        @block.vector
        def _(dve):
            v = nc.vector
            v.tensor_tensor(c.O[:], c.O[:], c.X[:], ALU.subtract).then_inc(minus, 1)
            dve.wait_ge(squared, 1)
            v.tensor_scalar(c.O[:], c.O[:], 0.1, None, ALU.max)
            dve.drain()
            v.tensor_reduce(c.g[:], c.O[:], X_AXIS, ALU.add).then_inc(summed, 1)
            dve.wait_ge(rooted, 1)
            v.reciprocal(c.g[:], c.g[:])

        @block.scalar
        def _(act):
            act.wait_ge(minus, 1)
            nc.scalar.activation(c.O[:], c.O[:], ACT.Square).then_inc(squared, 1)
            act.wait_ge(summed, 1)
            nc.scalar.activation(c.g[:], c.g[:], ACT.Sqrt).then_inc(rooted, 1)


def close_layer3(c):
    nc = c.nc
    full = [P, T, F]
    with nc.Block() as block:
        programs = {}

        @block.vector
        def _(dve):
            v = nc.vector
            normalise_sums(c, dve, 1, None, 1e-16)
            rs = c.rs[:, :, 0]
            v.tensor_tensor(c.rowsum[:], c.rowsum[:], rs, ALU.mult)
            v.tensor_tensor(c.O[:], c.O[:], rs.unsqueeze(2).to_broadcast(full), ALU.mult)
            dve.drain()
            v.tensor_tensor(c.K[:], c.X[:], c.rowsum[:].unsqueeze(2).to_broadcast(full), ALU.mult)
            dve.drain()
            v.tensor_tensor(c.O[:], c.O[:], c.K[:], ALU.subtract)
            dve.drain()
            v.tensor_tensor(c.X[:], c.X[:], c.O[:], ALU.add)
            dve.drain()
            programs.update(zip("vs", layer_norm(c, dve, nc.scalar, "ln3_")))
            programs["v"]()

        @block.scalar
        def _(act):
            programs["s"]()


_INS = ("x", "src", "dst", "edge_attr_128")


def kernel(**inputs):
    import numpy as np
    import concourse.bacc as bacc
    from concourse.bass_utils import run_bass_kernel_spmd

    nc = bacc.Bacc("TRN2", target_bir_lowering=False, num_devices=1)
    arrays, aps = {}, {}
    for name in inputs:
        a = np.ascontiguousarray(inputs[name])
        arrays["in_" + name] = a
        aps[name] = nc.dram_tensor("in_" + name, a.shape, mybir.dt.from_np(a.dtype), kind="ExternalInput").ap()
    out = nc.dram_tensor("out_x", (N, F), F32, kind="ExternalOutput").ap()
    weights = {name: ap for name, ap in aps.items() if name not in _INS}
    build(nc, aps["x"], aps["src"], aps["dst"], aps["edge_attr_128"], weights, out)
    return run_bass_kernel_spmd(nc, [arrays], core_ids=[0]).results[0]["out_x"]
```

```python
from contextlib import ExitStack

import concourse.bass as bass
from concourse import mybir

F32 = mybir.dt.float32
BF16 = mybir.dt.bfloat16
I32 = mybir.dt.int32
ALU = mybir.AluOpType
ACT = mybir.ActivationFunctionType
X_AXIS = mybir.AxisListType.X

P = 128
N = 6250
E = 106250
F = 128
T = -(-N // P)
NPAD = T * P
LAST = N - (T - 1) * P
GT = 7
NG = T // GT
SLOTS = 8
RING = 8
BATCH = 2
QS = RING // BATCH
BJ = BATCH * SLOTS
BUCKETS = 64
BLK = 250
NBLK = E // BLK
O_W = F + 8
LIST_W = 112
CAP = P * LIST_W
REC = 36
FIRST_AT = BJ
MASK_AT = 20
MASKED = -3.0e38
LOWEST = -1.0e37
assert T % GT == 0 and E % BLK == 0
assert CAP >= (E + E // P + BUCKETS) // SLOTS + T and CAP % RING == 0

ER = 10
E_MAIN = E // P // ER * ER
ESTEPS = E_MAIN // ER
E_TAIL = E - P * E_MAIN

L0_SCALE = 4.0


def bc(ap, shape):
    return ap.to_broadcast(shape)


class Core:
    pass


def build(nc, x, src, dst, edge_attr, w, out, stop=None, dump=None):
    ctx = ExitStack()
    with ctx:
        c = Core()
        c.nc = nc

        def sb(name, shape, dt=F32, where=ctx):
            return where.enter_context(nc.sbuf_tensor(name, shape, dt))

        def sem(name, where=ctx):
            return where.enter_context(nc.semaphore(name))

        c.sb, c.sem = sb, sem
        c.passed = sem("passed")
        c.src, c.dst, c.x, c.edge_attr, c.w, c.out = src, dst, x, edge_attr, w, out
        def dram(name, shape, dt=F32):
            return nc.dram_tensor(name, shape, dt).ap()

        c.samples_d = dram("samples_d", [1, NBLK], I32)
        c.src_pad = dram("src_pad", [E + 16], I32)
        c.src_win = dram("src_win", [E + 1, SLOTS], I32)
        c.edge_gate = dram("edge_gate", [E + SLOTS, 16])
        c.gate_win = dram("gate_win", [E + 1, SLOTS * 16])
        c.order = dram("order", [NPAD, 4], I32)
        c.meta_d = dram("meta_d", [CAP // BATCH, BATCH * 4], I32)
        c.rec_d = dram("rec_d", [CAP // BATCH, P, REC], I32)
        c.logit_d = dram("logit_d", [CAP // BATCH, P, BJ * 4])
        c.tab = [dram("tab0", [NPAD, 2 * F]), dram("tab1", [NPAD, F + 4]), dram("tab2", [NPAD, F + 4]),
                 dram("tab3", [NPAD, 64 + F]), dram("tab4", [NPAD, F + 1])]
        c.X = sb("X", [P, T, F])
        c.K = sb("K", [P, T, F])
        c.O = sb("O", [P, T * O_W])
        c.M = sb("M", [P, T, 8])
        c.S = sb("S", [P, T, 8])
        c.rs = sb("rs", [P, T, 8])
        c.adst = sb("adst", [P, T, 4])
        c.g = sb("g", [P, T])
        c.ids = sb("ids", [P, T], I32)
        c.start = sb("start", [P, T])
        c.first = sb("first", [P, T])
        c.deg = sb("deg", [P, T])
        c.bodies = sb("bodies", [1, 1], I32)
        c.slot = sb("slot", [P, SLOTS])
        c.diag = sb("diag", [P, P])
        c.ident = sb("ident", [P, P])
        c.ones = sb("ones", [P, P])
        c.valid = sb("valid", [P, P])
        c.eps = sb("eps", [P, 1])
        c.id_st = sb("id_st", [P, GT], I32)
        c.pass_sems = ([sem(f"rec{u}") for u in range(QS)], sem("batch"), sem("lg"), sem("ex"), sem("weighed"), sem("acc"), sem("taken"))
        c.project_sems = tuple(sem("p_" + n) for n in ("staged", "turned", "copied", "mm", "rows", "scat", "free"))
        constants(c)
        edge_projection_and_search(c)
        sort_nodes(c)
        item_list(c)
        item_records(c)
        load_nodes(c)
        if dump and stop == "prep":
            return dump(c)
        load_weights(c)
        project(c, 0)
        edge_pass(c, "L0")
        close_layer0(c)
        if stop == "L0":
            return dump(c)
        project(c, 1)
        edge_pass(c, "L1")
        close_layer1(c)
        if stop == "L1":
            return dump(c)
        project(c, 2)
        edge_pass(c, "L2")
        close_layer2(c)
        if stop == "L2":
            return dump(c)
        project(c, 3)
        edge_pass(c, "L3a")
        gradient_norm(c)
        project(c, 4)
        edge_pass(c, "L3c")
        close_layer3(c)
        store_nodes(c)


def constants(c):
    nc = c.nc
    iota_done, made = c.sem("iota_done"), c.sem("const_made")
    with nc.Block() as block:
        @block.gpsimd
        def _(pool):
            nc.gpsimd.iota(c.slot[:], pattern=[[1, SLOTS]], base=0, channel_multiplier=0,
                           allow_small_or_imprecise_dtypes=True)
            nc.gpsimd.iota(c.diag[:], pattern=[[1, P]], base=0, channel_multiplier=-1,
                           allow_small_or_imprecise_dtypes=True).then_inc(iota_done, 1)

        @block.vector
        def _(dve):
            nc.vector.memset(c.ones[:], 1.0)
            nc.vector.memset(c.valid[:], 0.0)
            nc.vector.memset(c.eps[:], 1e-5)
            dve.drain()
            nc.vector.memset(c.valid[0:LAST - LAST % 32, :], 1.0)
            dve.wait_ge(iota_done, 1)
            nc.vector.tensor_scalar(c.ident[:], c.diag[:], 0.0, None, ALU.is_equal)
            dve.drain()
            nc.vector.tensor_reduce(c.valid[96:P, 0:1], c.ident[96:P, 0:LAST], X_AXIS, ALU.add)
            dve.drain()
            nc.vector.tensor_scalar(c.valid[96:P, :], c.ones[96:P, :], c.valid[96:P, 0:1], None,
                                    ALU.mult).then_inc(made, 1)


def edge_projection_and_search(c):
    nc, w = c.nc, c.w
    sem = c.sem
    with ExitStack() as local:
        sb = lambda n, s, d=F32: c.sb(n, s, d, local)
        ps = lambda n, s: local.enter_context(nc.psum_tensor(n, s, F32))
        w_eg = sb("w_eg", [16, F])
        w_egT = sb("w_egT", [F, 16])
        feat = sb("feat", [P, 3, ER, F])
        featT = sb("featT", [P, 2, ER, P])
        res = sb("res", [P, 2, ER, 16])
        tailf = sb("tailf", [16, F])
        zeros = sb("zeros", [1, 16 * SLOTS])
        zeros_i = sb("zeros_i", [1, 16], I32)
        node = sb("node", [P, T])
        heads = sb("heads", [P, NBLK], I32)
        less = sb("less", [P, GT, NBLK])
        cnt = sb("cnt", [P, GT])
        blk = sb("blk", [P, GT])
        blk_i = sb("blk_i", [P, GT], I32)
        rows = sb("rows", [P, GT, BLK], I32)
        pT = [ps(f"pT{i}", [P, 4, P]) for i in range(3)]
        pO = [ps(f"pO{i}", [P, ER, 16]) for i in range(2)]
        w_in, w_ready, w_t = sem("eg_w_in"), sem("eg_w_ready"), sem("eg_w_t")
        feat_in = [sem(f"feat_in{i}") for i in range(3)]
        tr_done, tr_copied, mm_done, res_done = sem("eg_tr"), sem("eg_copied"), sem("eg_mm"), sem("eg_res")
        res_out = [sem(f"res_out{i}") for i in range(2)]
        heads_out, heads_in, pads = sem("heads_out"), sem("heads_in"), sem("pads")
        wins, zero_done = sem("wins"), sem("zero_done")
        node_done, blk_done, rows_in = sem("node_done"), sem("blk_done"), sem("rows_in")
        ea = c.edge_attr[0:P * E_MAIN, :].rearrange("(p s r) f -> s p r f", p=P, r=ER)
        eg = c.edge_gate[0:P * E_MAIN, :].rearrange("(p s r) f -> s p r f", p=P, r=ER)
        with nc.Block() as block:
            @block.sync
            def _(sp):
                sp.dma_start(w_eg[0:8, :], w["L0_gnn_Wedge"]).then_inc(w_in, 16)
                sp.dma_start(w_eg[8:16, :], w["L0_gnn_Wgate"]).then_inc(w_in, 16)
                sp.dma_start(tailf[0:E_TAIL, :], c.edge_attr[P * E_MAIN:E, :]).then_inc(w_in, 16)
                sp.dma_start(c.samples_d, c.dst.rearrange("(b r) -> r b", r=BLK)[0:1, :],
                             allow_slow_non_contiguous=True).then_inc(heads_out, 16)
                sp.wait_ge(heads_out, 16)
                sp.dma_start(heads[:], c.samples_d.to_broadcast([P, NBLK])).then_inc(heads_in, 16)
                sp.dma_start(c.src_pad[0:E].rearrange("(a b) -> a b", a=50),
                             c.src.rearrange("(a b) -> a b", a=50)).then_inc(pads, 16)
                sp.wait_ge(zero_done, 1)
                sp.dma_start(c.src_pad[E:E + 16].rearrange("(a b) -> a b", a=1), zeros_i[:]).then_inc(pads, 16)
                sp.dma_start(c.edge_gate[E:E + SLOTS, :].rearrange("(o a) b -> o (a b)", o=1), zeros[:]).then_inc(pads, 16)
                for i in range(2):
                    sp.dma_start(feat[:, i, :, :], ea[i]).then_inc(feat_in[i], 16)
                sp.wait_ge(pads, 48)
                h = E // 2
                for a, b in ((0, h), (h, E + 1)):
                    sp.dma_start(c.src_win[a:b, :], bass.AP(c.src_pad.tensor, a, [[1, b - a], [1, SLOTS]])).then_inc(wins, 16)
                for i in range(2, ESTEPS):
                    if i >= 3:
                        sp.wait_ge(tr_done, 3 * (i - 2))
                    sp.dma_start(feat[:, i % 3, :, :], ea[i]).then_inc(feat_in[i % 3], 16)
                sp.wait_ge(wins, 32)

            @block.tensor
            def _(pe):
                pe.wait_ge(w_in, 48)
                nc.tensor.transpose(pT[0][:, 0, 0:16], w_eg[:], c.ident[0:16, 0:16])
                nc.tensor.transpose(pT[0][:, 1, 0:E_TAIL], tailf[0:E_TAIL, :], c.ident[0:E_TAIL, 0:E_TAIL]).then_inc(w_ready, 1)
                pe.wait_ge(w_t, 1)
                nc.tensor.matmul(pO[0][0:E_TAIL, 0, :], featT[:, 0, 0, 0:E_TAIL], w_egT[:], start=True, stop=True).then_inc(w_ready, 1)

                def project_step(i):
                    pe.wait_ge(tr_copied, 3 * (i + 1))
                    if i != 1:
                        pe.wait_ge(res_done, max(i, 1))
                    for r in range(ER):
                        mm = nc.tensor.matmul(pO[i % 2][:, r, :], featT[:, i % 2, r, :], w_egT[:], start=True, stop=True)
                    mm.then_inc(mm_done, 1)

                for i in range(ESTEPS):
                    pe.wait_ge(feat_in[i % 3], 16 * (i // 3 + 1))
                    for q, (a, b) in enumerate(((0, 4), (4, 8), (8, ER))):
                        if i:
                            pe.wait_ge(tr_copied, 3 * (i - 1) + q + 1)
                        else:
                            pe.wait_ge(w_t, 1)
                        for r in range(a, b):
                            mm = nc.tensor.transpose(pT[q][:, r - a, :], feat[:, i % 3, r, :], c.ident[:])
                        mm.then_inc(tr_done, 1)
                    if i:
                        project_step(i - 1)
                project_step(ESTEPS - 1)

            @block.scalar
            def _(act):
                act.wait_ge(w_ready, 1)
                nc.scalar.copy(w_egT[:], pT[0][:, 0, 0:16])
                nc.scalar.copy(featT[:, 0, 0, 0:E_TAIL], pT[0][:, 1, 0:E_TAIL]).then_inc(w_t, 1)
                act.wait_ge(w_ready, 2)
                nc.scalar.copy(res[0:E_TAIL, 0, 0, 0:8], pO[0][0:E_TAIL, 0, 0:8])
                nc.scalar.activation(res[0:E_TAIL, 0, 0, 8:16], pO[0][0:E_TAIL, 0, 8:16], ACT.Sigmoid).then_inc(res_done, 1)
                act.wait_ge(res_done, 1)
                act.dma_start(c.edge_gate[P * E_MAIN:E, :], res[0:E_TAIL, 0, 0, :]).then_inc(res_out[0], 16)

                def results(i):
                    act.wait_ge(mm_done, i + 1)
                    n = (i // 2 + (1 if i % 2 == 0 else 0))
                    if n:
                        act.wait_ge(res_out[i % 2], 16 * n)
                    nc.scalar.copy(res[:, i % 2, :, 0:8], pO[i % 2][:, :, 0:8])
                    nc.scalar.activation(res[:, i % 2, :, 8:16], pO[i % 2][:, :, 8:16], ACT.Sigmoid).then_inc(res_done, 1)
                    act.wait_ge(res_done, i + 2)
                    act.dma_start(eg[i], res[:, i % 2, :, :]).then_inc(res_out[i % 2], 16)

                for i in range(ESTEPS):
                    for q, (a, b) in enumerate(((0, 4), (4, 8), (8, ER))):
                        act.wait_ge(tr_done, 3 * i + q + 1)
                        if i >= 2:
                            act.wait_ge(mm_done, i - 1)
                        nc.scalar.copy(featT[:, i % 2, a:b, :], pT[q][:, 0:b - a, :]).then_inc(tr_copied, 1)
                    if i:
                        results(i - 1)
                results(ESTEPS - 1)
                act.wait_ge(res_out[0], 16 * (1 + (ESTEPS + 1) // 2))
                act.wait_ge(res_out[1], 16 * (ESTEPS // 2))

            @block.gpsimd
            def _(pool):
                nc.gpsimd.iota(node[:], pattern=[[P, T]], base=0, channel_multiplier=1,
                               allow_small_or_imprecise_dtypes=True).then_inc(node_done, 1)
                dst_rows = c.dst.rearrange("(b r) -> b r", r=BLK)
                with pool.Fori(0, NG) as g:
                    pool.wait_ge(blk_done, g + 1)
                    held(c, pool)
                    for k in range(GT):
                        pool.indirect_dma_start(out=rows[:, k, :], out_offset=None, in_=dst_rows,
                                                in_offset=bass.IndirectOffsetOnAxis(ap=blk_i[:, k:k + 1], axis=0)).then_inc(rows_in, 16)

            @block.vector
            def _(dve):
                nc.vector.memset(zeros[:], 0.0)
                nc.vector.memset(zeros_i[:], 0).then_inc(zero_done, 1)
                dve.wait_ge(node_done, 1)
                dve.wait_ge(heads_in, 16)
                with dve.Fori(0, NG) as g:
                    nodes = node[:, bass.ds(g * GT, GT)].unsqueeze(2)
                    nc.vector.tensor_tensor(less[:], heads[:].unsqueeze(1).to_broadcast([P, GT, NBLK]),
                                            nodes.to_broadcast([P, GT, NBLK]), ALU.is_lt)
                    dve.drain()
                    nc.vector.tensor_reduce(cnt[:], less[:], X_AXIS, ALU.add)
                    dve.drain()
                    nc.vector.tensor_scalar(blk[:], cnt[:], -1.0, 0.0, ALU.add, ALU.max)
                    dve.drain()
                    nc.vector.tensor_copy(blk_i[:], blk[:]).then_inc(blk_done, 1)
                    dve.wait_ge(rows_in, (g + 1) * (16 * GT))
                    nc.vector.tensor_tensor(less[:, :, 0:BLK], rows[:], nodes.to_broadcast([P, GT, BLK]), ALU.is_lt)
                    dve.drain()
                    nc.vector.tensor_reduce(cnt[:], less[:, :, 0:BLK], X_AXIS, ALU.add)
                    dve.drain()
                    nc.vector.scalar_tensor_tensor(c.start[:, bass.ds(g * GT, GT)], blk[:], float(BLK), cnt[:], ALU.mult, ALU.add)
                    dve.drain()


def sort_nodes(c):
    nc, sem = c.nc, c.sem
    B = BUCKETS
    with ExitStack() as local:
        sb = lambda n, s, d=F32: c.sb(n, s, d, local)
        up1 = sb("up1", [P, P])
        up127 = sb("up127", [P, P])
        below = sb("below", [P, P], BF16)
        ones_b = sb("ones_b", [P, P], BF16)
        nxt = sb("nxt", [P, T])
        deg = sb("deg0", [P, T])
        cls = sb("cls", [P, T])
        cls_io = sb("cls_io", [P, B])
        hot = sb("hot", [P, B, T], BF16)
        tot = sb("tot", [P, B * T])
        incl = sb("incl", [P, B * T])
        zero = sb("zero", [P, B * T])
        rank = sb("rank", [P, T])
        rank_i = sb("rank_i", [P, T], I32)
        node_f = sb("node_f", [P, T])
        recs = sb("recs", [P, T, 4], I32)
        rank_st = sb("rank_st", [P, GT], I32)
        rec_st = sb("rec_st", [P, GT, 4], I32)
        back = sb("back", [P, T, 4], I32)
        CH = B * T // 7
        pn = local.enter_context(nc.psum_tensor("pn", [P, T], F32))
        pc = local.enter_context(nc.psum_tensor("pc", [P, 7, 512], F32))
        io, mats, shifted, hot_done, tots, tot_got, pres, rank_done = (
            sem(n) for n in ("so_io", "so_mats", "so_shift", "so_hot", "so_tots", "so_got", "so_pres", "so_rank"))
        order_out, order_in, gwin = sem("order_out"), sem("order_in"), sem("gwin")
        hotf = hot[:].rearrange("p b t -> p (b t)")
        with nc.Block() as block:
            @block.scalar
            def _(act):
                n = 4
                cuts = [(E + 1) * i // n for i in range(n + 1)]
                for a, b in zip(cuts, cuts[1:]):
                    act.dma_start(c.gate_win[a:b, :], bass.AP(c.edge_gate.tensor, 16 * a, [[16, b - a], [1, 16 * SLOTS]])).then_inc(gwin, 16)
                act.wait_ge(gwin, 16 * n)

            @block.gpsimd
            def _(pool):
                nc.gpsimd.iota(node_f[:], pattern=[[P, T]], base=0, channel_multiplier=1, allow_small_or_imprecise_dtypes=True)
                nc.gpsimd.iota(cls_io[:], pattern=[[1, B]], base=0, channel_multiplier=0,
                               allow_small_or_imprecise_dtypes=True).then_inc(io, 1)
                pool.wait_ge(rank_done, 1)
                with pool.Fori(0, NG) as g:
                    nc.gpsimd.tensor_copy(rank_st[:], rank_i[:, bass.ds(g * GT, GT)])
                    nc.gpsimd.tensor_copy(rec_st[:], recs[:, bass.ds(g * GT, GT), :])
                    pool.drain()
                    for k in range(GT):
                        pool.indirect_dma_start(out=c.order, out_offset=bass.IndirectOffsetOnAxis(ap=rank_st[:, k:k + 1], axis=0),
                                                in_=rec_st[:, k, :], in_offset=None).then_inc(order_out, 16)
                    pool.wait_ge(order_out, (g + 1) * (16 * GT))
                    held(c, pool)

            @block.sync
            def _(sp):
                sp.wait_ge(order_out, 16 * T)
                sp.dma_start(back[:], c.order.rearrange("(t p) c -> p t c", p=P)).then_inc(order_in, 16)
                sp.wait_ge(order_in, 16)

            @block.tensor
            def _(pe):
                pe.wait_ge(mats, 1)
                nc.tensor.matmul(pn[:], up1[:], c.start[:], start=True, stop=False)
                nc.tensor.matmul(pn[:], up127[:], nxt[:], start=False, stop=True).then_inc(shifted, 1)
                pe.wait_ge(hot_done, 1)
                for k in range(7):
                    mm = nc.tensor.matmul(pc[:, k, 0:CH], ones_b[:], hotf[:, k * CH:(k + 1) * CH], start=True, stop=True)
                mm.then_inc(tots, 1)
                pe.wait_ge(tot_got, 1)
                for k in range(7):
                    mm = nc.tensor.matmul(pc[:, k, 0:CH], below[:], hotf[:, k * CH:(k + 1) * CH], start=True, stop=True)
                mm.then_inc(pres, 1)

            @block.vector
            def _(dve):
                v = nc.vector
                v.tensor_scalar(up1[:], c.diag[:], -1.0, None, ALU.is_equal)
                v.tensor_scalar(up127[:], c.diag[:], 127.0, None, ALU.is_equal)
                v.tensor_scalar(below[:], c.diag[:], 0.0, None, ALU.is_gt)
                v.memset(ones_b[:], 1.0)
                v.memset(zero[:], 0.0)
                v.memset(nxt[:, T - 1:T], float(E))
                v.memset(recs[:], 0)
                v.tensor_copy(nxt[:, 0:T - 1], c.start[:, 1:T]).then_inc(mats, 1)
                dve.wait_ge(shifted, 1)
                v.tensor_tensor(deg[:], pn[:], c.start[:], ALU.subtract)
                dve.drain()
                v.tensor_scalar(cls[:], deg[:], -1.0, float(B - 1), ALU.mult, ALU.add)
                dve.drain()
                v.tensor_scalar(cls[:], cls[:], 0.0, None, ALU.max)
                dve.drain()
                dve.wait_ge(io, 1)
                v.tensor_tensor(hot[:], cls_io[:].unsqueeze(2).to_broadcast([P, B, T]),
                                cls[:].unsqueeze(1).to_broadcast([P, B, T]), ALU.is_equal).then_inc(hot_done, 1)
                dve.wait_ge(tots, 1)
                v.tensor_copy(tot[:].rearrange("p (a b) -> p a b", a=7), pc[:, :, 0:CH]).then_inc(tot_got, 1)
                dve.drain()
                v.tensor_tensor_scan(incl[:], tot[:], zero[:], 0.0, ALU.add, ALU.add)
                dve.drain()
                v.tensor_tensor(incl[:], incl[:], tot[:], ALU.subtract)
                dve.drain()
                dve.wait_ge(pres, 1)
                v.tensor_tensor(incl[:].rearrange("p (a b) -> p a b", a=7), incl[:].rearrange("p (a b) -> p a b", a=7),
                                pc[:, :, 0:CH], ALU.add)
                dve.drain()
                v.tensor_tensor(incl[:], incl[:], hotf, ALU.mult)
                dve.drain()
                v.tensor_reduce(rank[:], incl[:].rearrange("p (b t) -> p t b", t=T), X_AXIS, ALU.add)
                v.tensor_copy(recs[:, :, 0], node_f[:])
                v.tensor_copy(recs[:, :, 1], c.start[:])
                v.tensor_copy(recs[:, :, 2], deg[:])
                dve.drain()
                v.tensor_copy(rank_i[:], rank[:]).then_inc(rank_done, 1)
                dve.wait_ge(order_in, 16)
                v.tensor_copy(c.ids[:], back[:, :, 0])
                v.tensor_copy(c.first[:], back[:, :, 1])
                v.tensor_copy(c.deg[:], back[:, :, 2])


def item_list(c):
    nc, sem = c.nc, c.sem
    W = LIST_W
    with ExitStack() as local:
        sb = lambda n, s, d=F32: c.sb(n, s, d, local)
        jmax = sb("jmax", [T, 2])
        jint = sb("jint", [T, 1], I32)
        dj = sb("dj", [T, 2, T])
        jn = sb("jn", [P, 2, T])
        iend = sb("iend", [P, T])
        ibeg = sb("ibeg", [P, T])
        zero = sb("zero2", [P, T])
        item = sb("item", [P, W])
        past = sb("past", [P, W, T])
        begun = sb("begun", [P, W, T])
        tile_of = sb("tile_of", [P, W])
        base = sb("base", [P, W])
        jm = sb("jm", [P, W])
        s0 = sb("s0", [P, W])
        meta = sb("meta", [P, W, 4], I32)
        nb = sb("nb", [1, 1])
        before = sb("before", [P, P])
        cum = sb("cum", [P, W // RING, QS])
        pair = sb("pair", [P, W // RING, QS])
        zw = sb("zw", [P, W // RING])
        pcum = local.enter_context(nc.psum_tensor("pcum", [P, QS], F32))
        nbi = sb("nbi", [1, 1], I32)
        pt = local.enter_context(nc.psum_tensor("pt", [P, P], F32))
        pj = local.enter_context(nc.psum_tensor("pj", [P, 2 * T], F32))
        io, tr, dj_done, bcast, meta_done, meta_out, rows_done, rows_sum = (
            sem(n) for n in ("il_io", "il_tr", "il_dj", "il_bc", "il_meta", "il_out", "il_rows", "il_rsum"))
        with nc.Block() as block:
            @block.gpsimd
            def _(pool):
                nc.gpsimd.iota(item[:], pattern=[[1, W]], base=0, channel_multiplier=W,
                               allow_small_or_imprecise_dtypes=True).then_inc(io, 1)

            @block.tensor
            def _(pe):
                nc.tensor.transpose(pt[0:T, :], c.deg[:], c.ident[:]).then_inc(tr, 1)
                pe.wait_ge(dj_done, 1)
                nc.tensor.matmul(pj[:], c.ones[0:T, :], dj[:].rearrange("a b t -> a (b t)"), start=True, stop=True).then_inc(bcast, 1)
                pe.wait_ge(rows_done, 1)
                nc.tensor.matmul(pcum[:], before[:], cum[:, W // RING - 1, :], start=True, stop=True).then_inc(rows_sum, 1)

            @block.vector
            def _(dve):
                v = nc.vector
                dve.wait_ge(tr, 1)
                v.tensor_reduce(jmax[:, 0:1], pt[0:T, :], X_AXIS, ALU.max)
                dve.drain()
                v.tensor_scalar(jint[:], jmax[:, 0:1], float(SLOTS - 1), None, ALU.add)
                dve.drain()
                v.tensor_scalar(jint[:], jint[:], 3, None, ALU.logical_shift_right)
                dve.drain()
                v.tensor_copy(jmax[:, 1:2], jint[:])
                dve.drain()
                v.tensor_scalar(dj[:, 0, :], c.ident[0:T, 0:T], jmax[:, 0:1], None, ALU.mult)
                v.tensor_scalar(dj[:, 1, :], c.ident[0:T, 0:T], jmax[:, 1:2], None, ALU.mult).then_inc(dj_done, 1)
                v.memset(zero[:], 0.0)
                v.memset(meta[:], 0)
                dve.wait_ge(bcast, 1)
                v.tensor_copy(jn[:].rearrange("p b t -> p (b t)"), pj[:])
                dve.drain()
                v.tensor_tensor_scan(iend[:], jn[:, 1, :], zero[:], 0.0, ALU.add, ALU.add)
                dve.drain()
                v.tensor_tensor(ibeg[:], iend[:], jn[:, 1, :], ALU.subtract)
                v.tensor_scalar(nb[:], iend[0:1, T - 1:T], float(RING - 1), None, ALU.add)
                dve.wait_ge(io, 1)
                ib = item[:].unsqueeze(2).to_broadcast([P, W, T])
                bt = lambda a: a.unsqueeze(1).to_broadcast([P, W, T])
                dve.drain()
                v.tensor_copy(nbi[:], nb[:])
                v.tensor_tensor(past[:], bt(iend[:]), ib, ALU.is_le)
                v.tensor_tensor(begun[:], bt(ibeg[:]), ib, ALU.is_le)
                dve.drain()
                v.tensor_scalar(c.bodies[:], nbi[:], 3, None, ALU.logical_shift_right)
                v.tensor_reduce(tile_of[:], past[:], X_AXIS, ALU.add)
                v.tensor_tensor(begun[:], begun[:], past[:], ALU.subtract)
                dve.drain()
                v.tensor_tensor(past[:], past[:], bt(jn[:, 1, :]), ALU.mult)
                v.tensor_tensor(begun[:], begun[:], bt(jn[:, 0, :]), ALU.mult)
                dve.drain()
                v.tensor_reduce(base[:], past[:], X_AXIS, ALU.add)
                v.tensor_reduce(jm[:], begun[:], X_AXIS, ALU.add)
                dve.drain()
                v.tensor_tensor(s0[:], item[:], base[:], ALU.subtract)
                dve.drain()
                v.tensor_scalar(s0[:], s0[:], float(SLOTS), None, ALU.mult)
                dve.drain()
                v.tensor_tensor(jm[:], jm[:], s0[:], ALU.subtract)
                dve.drain()
                v.tensor_scalar(meta[:, :, 0], tile_of[:], float(T - 1), None, ALU.min)
                v.tensor_scalar(jm[:], jm[:], 0.0, float(SLOTS), ALU.max, ALU.min)
                v.tensor_copy(meta[:, :, 2], s0[:])
                v.tensor_scalar(before[:], c.diag[:], 0.0, None, ALU.is_gt)
                v.memset(zw[:], 0.0)
                dve.drain()
                v.tensor_copy(meta[:, :, 1], jm[:])
                jq = jm[:].rearrange("p (q u i) -> p q u i", u=QS, i=BATCH)
                v.tensor_tensor(pair[:], jq[:, :, :, 0], jq[:, :, :, 1], ALU.add)
                dve.drain()
                for u in range(QS):
                    last = v.tensor_tensor_scan(cum[:, :, u], pair[:, :, u], zw[:], 0.0, ALU.add, ALU.add)
                last.then_inc(rows_done, 1)
                dve.wait_ge(rows_sum, 1)
                for i in range(BATCH):
                    last = v.tensor_tensor(meta[:, :, 3].rearrange("p (q u i) -> p q u i", u=QS, i=BATCH)[:, :, :, i], cum[:],
                                           pcum[:].unsqueeze(1).to_broadcast([P, W // RING, QS]), ALU.add)
                last.then_inc(meta_done, 1)

            @block.sync
            def _(sp):
                sp.wait_ge(meta_done, 1)
                sp.dma_start(c.meta_d.rearrange("(p w) (i c) -> p (w i) c", p=P, i=BATCH), meta[:]).then_inc(meta_out, 16)
                sp.wait_ge(meta_out, 16)


def held(c, eng):
    eng.sem_inc(c.passed, 1)


def body_count(c, eng):
    return eng.value_load(c.bodies[0:1, 0:1], min_val=1, max_val=CAP // RING)


def item_records(c):
    nc, sem = c.nc, c.sem
    with ExitStack() as local:
        sb = lambda n, s, d=F32: c.sb(n, s, d, local)
        meta = sb("meta_all", [P, QS, BATCH, 4], I32)
        rec = sb("rec_b", [P, QS, REC], I32)
        offf = sb("offf", [P, QS, BATCH])
        off = sb("off", [P, QS, BATCH], I32)
        left = sb("left", [P, QS, BATCH])
        win = [sb(f"win{u}", [P, BATCH, SLOTS], I32) for u in range(QS)]
        meta_in = [sem(f"ir_meta{u}") for u in range(QS)]
        off_done, rec_done, freed = sem("ir_off"), sem("ir_rec"), sem("ir_freed")
        win_in = [sem(f"ir_win{u}") for u in range(QS)]
        rec_out = [sem(f"ir_out{u}") for u in range(QS)]
        maskf = rec[:].bitcast(F32)
        with nc.Block() as block:
            @block.sync
            def _(sp):
                nb = body_count(c, sp)
                with sp.Fori(0, nb) as b:
                    for q in range(QS):
                        sp.wait_ge(freed, b * QS + (q + 1))
                        sp.dma_start(meta[:, q, :, :].rearrange("p i c -> p (i c)"),
                                     c.meta_d[bass.ds(b * QS + q, 1), :].to_broadcast([P, BATCH * 4])).then_inc(meta_in[q], 16)

            @block.gpsimd
            def _(pool):
                nb = body_count(c, pool)
                with pool.Fori(0, nb) as b:
                    for q in range(QS):
                        pool.wait_ge(off_done, b * QS + (q + 1))
                        held(c, pool)
                        for i in range(BATCH):
                            pool.indirect_dma_start(out=win[q][:, i, :], out_offset=None, in_=c.src_win,
                                                    in_offset=bass.IndirectOffsetOnAxis(ap=off[:, q, i:i + 1], axis=0)).then_inc(win_in[q], 16)

            @block.vector
            def _(dve):
                v = nc.vector
                v.memset(rec[:], 0)
                dve.sem_inc(freed, QS)
                nb = body_count(c, dve)

                def offsets(b, q):
                    dve.wait_ge(meta_in[q], (b + 1) * 16)
                    held(c, dve)
                    for i in range(BATCH):
                        t = dve.value_load(meta[0:1, q, i, 0:1], min_val=0, max_val=T - 1)
                        v.tensor_tensor(offf[:, q, i:i + 1], c.first[:, bass.ds(t, 1)], meta[:, q, i, 2:3], ALU.add)
                        v.tensor_tensor(left[:, q, i:i + 1], c.deg[:, bass.ds(t, 1)], meta[:, q, i, 2:3], ALU.subtract)
                    dve.drain()
                    v.tensor_scalar(off[:, q, :], offf[:, q, :], float(E), None, ALU.min).then_inc(off_done, 1)

                def record(b, q):
                    dve.wait_ge(rec_out[q], b * 16 + 16)
                    dve.wait_ge(win_in[q], (b + 1) * (16 * BATCH))
                    v.tensor_copy(rec[:, q, 0:BJ], win[q][:].rearrange("p i j -> p (i j)"))
                    v.tensor_copy(rec[:, q, FIRST_AT:FIRST_AT + BATCH], off[:, q, :])
                    for i in range(BATCH):
                        v.tensor_scalar(maskf[:, q, MASK_AT + i * SLOTS:MASK_AT + (i + 1) * SLOTS], c.slot[:],
                                        left[:, q, i:i + 1], MASKED, ALU.is_ge, ALU.mult)
                    dve.drain()
                    dve.sem_inc(rec_done, 1)
                    dve.sem_inc(freed, 1)

                with dve.Fori(0, nb) as b:
                    for q in range(QS):
                        offsets(b, q)
                    for q in range(QS):
                        record(b, q)

            @block.scalar
            def _(act):
                for q in range(QS):
                    act.sem_inc(rec_out[q], 16)
                nb = body_count(c, act)
                with act.Fori(0, nb) as b:
                    for q in range(QS):
                        act.wait_ge(rec_done, b * QS + (q + 1))
                        act.dma_start(c.rec_d[bass.ds(b * QS + q, 1), :, :].rearrange("o p c -> (o p) c"), rec[:, q, :]).then_inc(rec_out[q], 16)
                for q in range(QS):
                    act.wait_ge(rec_out[q], (nb + 1) * 16)
                held(c, act)


def load_nodes(c):
    nc = c.nc
    with ExitStack() as local:
        stage = c.sb("x_st", [P, 2, GT, F], F32, local)
        x_in, moved = [c.sem("x_in0"), c.sem("x_in1")], c.sem("x_moved")
        with nc.Block() as block:
            @block.gpsimd
            def _(pool):
                for g in range(NG):
                    if g >= 2:
                        pool.wait_ge(moved, g - 1)
                    for k in range(GT):
                        i = g * GT + k
                        n = LAST if i == T - 1 else P
                        pool.indirect_dma_start(out=stage[0:n, g % 2, k, :], out_offset=None, in_=c.x,
                                                in_offset=bass.IndirectOffsetOnAxis(ap=c.ids[0:n, i:i + 1], axis=0)).then_inc(x_in[g % 2], 16)

            @block.vector
            def _(dve):
                nc.vector.memset(c.X[:, T - 1, :], 0.0)
                dve.drain()
                for g in range(NG):
                    dve.wait_ge(x_in[g % 2], 16 * GT * (g // 2 + 1))
                    if g < NG - 1:
                        nc.vector.tensor_copy(c.X[:, g * GT:(g + 1) * GT, :], stage[:, g % 2, :, :]).then_inc(moved, 1)
                    else:
                        nc.vector.tensor_copy(c.X[:, g * GT:(g + 1) * GT - 1, :], stage[:, g % 2, 0:GT - 1, :])
                        nc.vector.tensor_copy(c.X[0:LAST, T - 1, :], stage[0:LAST, g % 2, GT - 1, :]).then_inc(moved, 1)


def store_nodes(c):
    nc = c.nc
    with ExitStack() as local:
        stage = c.sb("y_st", [P, GT, F], F32, local)
        y_out = c.sem("y_out")
        with nc.Block() as block:
            @block.gpsimd
            def _(pool):
                for g in range(NG):
                    for k in range(GT):
                        i = g * GT + k
                        n = LAST if i == T - 1 else P
                        pool.indirect_dma_start(out=c.out, out_offset=bass.IndirectOffsetOnAxis(ap=c.ids[0:n, i:i + 1], axis=0),
                                                in_=c.X[0:n, g * GT + k, :], in_offset=None).then_inc(y_out, 16)
                pool.wait_ge(y_out, 16 * T)


Q0, V0, K0, NODE0, W1, SRC2, DST2, KQ3 = (F * i for i in range(8))
PROJECTED = {0: (Q0, 3 * F), 1: (W1, F), 2: (SRC2, 2 * F), 3: (KQ3, F)}
TABLE_W = [2 * F, F + 4, F + 4, 64 + F, F + 1]


def load_weights(c):
    nc, w = c.nc, c.w
    c.raw = c.sb("raw", [P, 6, F])
    c.wt = c.sb("wt", [P, 8 * F])
    c.att1 = c.sb("att1", [P, 2, F])
    c.att2 = c.sb("att2", [P, F])
    c.att2_relu = c.sb("att2_relu", [P, F])
    c.bias = c.sb("bias", [P, F])
    c.gamma = c.sb("gamma", [P, F])
    c.beta = c.sb("beta", [P, F])
    c.bkq = c.sb("bkq", [P, F])
    w_in, turned = c.sem("w_in"), c.sem("w_turned")
    with ExitStack() as local:
        pw = local.enter_context(nc.psum_tensor("pw", [P, 8, F], F32))
        with nc.Block() as block:
            @block.sync
            def _(sp):
                n = 0
                for i, name in enumerate(("L0_gnn_Wq", "L0_gnn_Wv", "L0_gnn_Wk", "L0_gnn_Wnode", "L1_gnn_W")):
                    sp.dma_start(c.raw[:, i, :], w[name]).then_inc(w_in, 16)
                sp.dma_start(c.raw[0:64, 5, :], w["L3_gnn_Wk"]).then_inc(w_in, 16)
                sp.dma_start(c.raw[64:P, 5, :], w["L3_gnn_Wq"]).then_inc(w_in, 16)
                sp.dma_start(c.wt[:, SRC2:SRC2 + F], w["L2_gnn_W_src"]).then_inc(w_in, 16)
                sp.dma_start(c.wt[:, DST2:DST2 + F], w["L2_gnn_W_dst"]).then_inc(w_in, 16)
                n = 9
                row = lambda v: v.rearrange("(a b) -> a b", a=1)
                flat = lambda v: row(v.rearrange("h d -> (h d)"))
                for to, of in ((c.att1[:, 0, :], flat(w["L1_gnn_att_src"])), (c.att1[:, 1, :], flat(w["L1_gnn_att_dst"])),
                               (c.att2[:], flat(w["L2_gnn_att"])), (c.bias[:], row(w["L2_gnn_bias"])),
                               (c.gamma[:], row(w["L2_gnn_bn_gamma"])), (c.beta[:], row(w["L2_gnn_bn_beta"])),
                               (c.bkq[:, 0:64], row(w["L3_gnn_bk"])), (c.bkq[:, 64:F], row(w["L3_gnn_bq"]))):
                    sp.dma_start(to, of.to_broadcast(list(to.shape))).then_inc(w_in, 16)
                    n += 1
                sp.wait_ge(w_in, 16 * n)

            @block.tensor
            def _(pe):
                pe.wait_ge(w_in, 16 * 17)
                for i in range(6):
                    mm = nc.tensor.transpose(pw[:, i, :], c.raw[:, i, :], c.ident[:])
                mm.then_inc(turned, 1)

            @block.vector
            def _(dve):
                dve.wait_ge(turned, 1)
                nc.vector.tensor_copy(c.wt[:, 0:5 * F].rearrange("p (a f) -> p a f", f=F), pw[:, 0:5, :])
                nc.vector.tensor_copy(c.wt[:, KQ3:KQ3 + F], pw[:, 5, :])
                nc.vector.tensor_scalar(c.att2_relu[:], c.att2[:], 0.8, None, ALU.mult)


def project(c, layer):
    nc = c.nc
    R = TABLE_W[layer]
    col, width = PROJECTED.get(layer, (0, 0))
    tag = f"pr{layer}_"
    with ExitStack() as local:
        sb = lambda n, s, d=F32: c.sb(tag + n, s, d, local)
        ps = lambda n, s: local.enter_context(nc.psum_tensor(tag + n, s, F32))
        xg = sb("xg", [P, GT, F])
        xT = sb("xT", [P, 2, F])
        st = sb("st", [P, GT, R])
        tmp = sb("tmp", [P, 2, F])
        asd = sb("asd", [P, 12])
        pX = [ps(f"pX{i}", [P, 512]) for i in range(2)]
        pW = [ps(f"pW{i}", [P, 512]) for i in range(3)]
        staged, turned, copied, mm_done, rows_done, scat, stage_free = c.project_sems
        first = layer == 0
        with nc.Block() as block:
            @block.gpsimd
            def _(pool):
                if first:
                    pool.sem_inc(rows_done, 1)
                with pool.Fori(0, NG) as g:
                    G = g + NG * layer
                    pool.wait_ge(rows_done, G * GT + 1)
                    held(c, pool)
                    nc.gpsimd.tensor_copy(xg[:], c.X[:, bass.ds(g * GT, GT), :])
                    nc.gpsimd.tensor_copy(c.id_st[:], c.ids[:, bass.ds(g * GT, GT)])
                    pool.drain().then_inc(staged, 1)
                    for k in range(GT):
                        pool.wait_ge(rows_done, G * GT + (k + 2))
                        held(c, pool)
                        pool.indirect_dma_start(out=c.tab[layer], out_offset=bass.IndirectOffsetOnAxis(ap=c.id_st[:, k:k + 1], axis=0),
                                                in_=st[:, k, :], in_offset=None).then_inc(scat, 16)
                    pool.wait_ge(scat, (G + 1) * (16 * GT))
                    pool.sem_inc(stage_free, 1)

            if layer < 4:
                @block.tensor
                def _(pe):
                    def turn(G, k):
                        if k == 0:
                            pe.wait_ge(staged, G + 1)
                        if k >= 2:
                            pe.wait_ge(copied, G * GT + (k - 1))
                        nc.tensor.transpose(pX[k % 2][:, 0:F], xg[:, k, :], c.ident[:]).then_inc(turned, 1)

                    if first:
                        pe.sem_inc(mm_done, 1)
                    with pe.Fori(0, NG) as g:
                        G = g + NG * layer
                        turn(G, 0)
                        for k in range(GT):
                            if k + 1 < GT:
                                turn(G, k + 1)
                            pe.wait_ge(copied, G * GT + (k + 1))
                            if k >= 3:
                                pe.wait_ge(rows_done, G * GT + (k - 1))
                            nc.tensor.matmul(pW[k % 3][:, 0:width], xT[:, k % 2, :], c.wt[:, col:col + width],
                                             start=True, stop=True).then_inc(mm_done, 1)

                @block.scalar
                def _(act):
                    with act.Fori(0, NG) as g:
                        G = g + NG * layer
                        for k in range(GT):
                            act.wait_ge(turned, G * GT + (k + 1))
                            if k >= 2:
                                act.wait_ge(mm_done, G * GT + k)
                            nc.scalar.copy(xT[:, k % 2, :], pX[k % 2][:, 0:F]).then_inc(copied, 1)

            @block.vector
            def _(dve):
                v = nc.vector
                if first:
                    dve.sem_inc(stage_free, 1)
                O, H = sums_view(c, 4), 4

                def open_sum(t, rows):
                    o = O[:, bass.ds(t, 1), :].rearrange("p a (h d) -> p (a h) d", h=H)
                    v.tensor_copy(o[:, :, 0:F // H], rows.rearrange("p (h d) -> p h d", h=H))
                    v.tensor_copy(o[:, :, F // H], c.ones[:, 0:H])

                def at(a, t, n):
                    return a[:, bass.ds(t, 1), 0:n].rearrange("p a f -> p (a f)")

                def over(ap, dims):
                    return ap.unsqueeze(1).to_broadcast(dims)

                with dve.Fori(0, NG) as g:
                    G = g + NG * layer
                    dve.wait_ge(stage_free, G + 1)
                    dve.wait_ge(staged, G + 1)
                    held(c, dve)
                    for k in range(GT):
                        t = g * GT + k
                        here = c.K[:, bass.ds(t, 1), :].rearrange("p a f -> p (a f)")
                        if layer < 4:
                            dve.wait_ge(mm_done, G * GT + (k + 2))
                            held(c, dve)
                        W = pW[k % 3]
                        if layer == 0:
                            v.tensor_copy(st[:, k, :], W[:, 0:2 * F])
                            v.tensor_copy(here, W[:, 2 * F:3 * F])
                        elif layer == 1:
                            v.tensor_copy(st[:, k, 0:F], W[:, 0:F])
                            v.tensor_tensor(tmp[:], W[:, 0:F].unsqueeze(1).to_broadcast([P, 2, F]), c.att1[:], ALU.mult)
                            dve.drain()
                            v.tensor_reduce(asd[:, 0:8], tmp[:].rearrange("p a (h d) -> p (a h) d", h=4), X_AXIS, ALU.add)
                            dve.drain()
                            open_sum(t, W[:, 0:F])
                            v.tensor_tensor(asd[:, 8:12], asd[:, 0:4], asd[:, 4:8], ALU.add)
                            dve.drain()
                            v.scalar_tensor_tensor(at(c.M, t, 4), asd[:, 8:12], 0.2, asd[:, 8:12], ALU.mult, ALU.max)
                            v.tensor_copy(st[:, k, F:F + 4], asd[:, 0:4])
                            v.tensor_copy(c.adst[:, bass.ds(t, 1), :].rearrange("p a f -> p (a f)"), asd[:, 4:8])
                        elif layer == 2:
                            v.tensor_copy(st[:, k, 0:F], W[:, 0:F])
                            v.tensor_copy(here, W[:, F:2 * F])
                            v.tensor_tensor(tmp[:], W[:, 0:2 * F].rearrange("p (a f) -> p a f", a=2), over(c.att2[:], [P, 2, F]), ALU.mult)
                            dve.drain()
                            v.tensor_reduce(asd[:, 0:8], tmp[:].rearrange("p a (h d) -> p (a h) d", h=4), X_AXIS, ALU.add)
                            dve.drain()
                            v.tensor_scalar(st[:, k, F:F + 4], asd[:, 0:4], 0.2, None, ALU.mult)
                            v.tensor_scalar(c.adst[:, bass.ds(t, 1), :].rearrange("p a f -> p (a f)"), asd[:, 4:8], 0.2, None, ALU.mult)
                            open_sum(t, W[:, 0:F])
                            v.tensor_copy(tmp[:, 0, :], W[:, F:2 * F])
                            dve.drain()
                            v.tensor_tensor(tmp[:, 0, :], tmp[:, 0, :], W[:, 0:F], ALU.add)
                            dve.drain()
                            v.scalar_tensor_tensor(tmp[:, 0, :], tmp[:, 0, :], 0.2, tmp[:, 0, :], ALU.mult, ALU.max)
                            dve.drain()
                            v.tensor_tensor(tmp[:, 0, :], tmp[:, 0, :], c.att2[:], ALU.mult)
                            dve.drain()
                            v.tensor_reduce(at(c.M, t, 4), tmp[:, 0, :].rearrange("p (h d) -> p h d", h=4), X_AXIS, ALU.add)
                        elif layer == 3:
                            v.tensor_tensor(st[:, k, 0:64], W[:, 0:64], c.bkq[:, 0:64], ALU.add)
                            v.tensor_tensor(here[:, 0:64], W[:, 64:F], c.bkq[:, 64:F], ALU.add)
                            v.tensor_copy(st[:, k, 64:R], xg[:, k, :])
                        else:
                            v.tensor_copy(st[:, k, 0:F], xg[:, k, :])
                            v.tensor_copy(st[:, k, F:F + 1], c.g[:, bass.ds(t, 1)])
                        dve.drain().then_inc(rows_done, 1)


HEADS = {"L0": 8, "L1": 4, "L2": 4, "L3a": 4, "L3c": 1}
TABLE = {"L0": 0, "L1": 1, "L2": 2, "L3a": 3, "L3c": 4}


PASSES = ["L0", "L1", "L2", "L3a", "L3c"]


def sums_view(c, H, more=0):
    w = F + H + more
    return c.O[:, 0:T * w].rearrange("p (t w) -> p t w", w=w)


def edge_pass(c, kind):
    nc = c.nc
    H, tab = HEADS[kind], c.tab[TABLE[kind]]
    R = TABLE_W[TABLE[kind]]
    D = F // H
    tag = kind + "_"
    grand = kind == "L3a"
    rows_at = 64 if grand else F if kind == "L0" else 0
    W = 4 * F if grand else F + H + (kind == "L3c")
    C = 5 if kind == "L3c" else H
    with ExitStack() as local:
        sb = lambda n, s, d=F32: c.sb(tag + n, s, d, local)
        meta = sb("meta", [1, QS, BATCH * 4], I32)
        rec = sb("rec", [P, QS, REC], I32)
        got = sb("got", [P, QS, BJ, R])
        gate = sb("gate", [P, QS, BJ, 16]) if kind == "L0" else None
        raw = sb("raw", [P, QS, BJ, 4]) if kind in ("L3a", "L3c") else None
        prod = sb("prod", [P, BJ, 64 if grand else F]) if kind in ("L0", "L2", "L3a") else None
        wrow = sb("wrow", [P, BATCH, SLOTS, W])
        lg = sb("lg", [P, QS, BJ + BATCH, C])
        ex = sb("ex", [P, QS, BJ + BATCH, C])
        wt = sb("w", [P, BJ, max(H, 4)])
        watt = sb("watt", [P, BJ])
        mx = sb("mx", [P, BATCH, H])
        mnew = sb("mnew", [P, BATCH, H])
        psum_s = sb("ps", [P, BATCH, H])
        A = sb("A", [P, W]) if grand else None
        collapse = sb("col", [P, W]) if grand else None
        rS = sb("rS", [P, H])
        acc = [local.enter_context(nc.psum_tensor(tag + f"acc{i}", [P, 512], F32)) for i in range(BATCH)]
        got_in = [c.sem(tag + f"got{q}") for q in range(QS)]
        raw_out = [c.sem(tag + f"ro{q}") for q in range(QS)] if kind == "L3a" else None
        raw_in = [c.sem(tag + f"ri{q}") for q in range(QS)] if kind == "L3c" else None
        raw_done = c.sem(tag + "rd") if kind == "L3a" else None
        z_done, relu_done = (c.sem(tag + "z"), c.sem(tag + "relu")) if kind == "L2" else (None, None)
        rec_in, batch_done, lg_done, ex_done, w_done, acc_done, taken = c.pass_sems
        n_pass = PASSES.index(kind)
        maskf = rec[:].bitcast(F32)
        O = flat_rows(c) if grand else sums_view(c, H, 1 if kind == "L3c" else 0)
        m0 = 4 if kind == "L3c" else 0
        with nc.Block() as block:
            @block.vector
            def _(dve):
                v = nc.vector
                v.memset(got[:], 0.0)
                v.memset(lg[:], 0.0)
                v.memset(wrow[:], 0.0)
                if kind not in ("L1", "L2"):
                    v.memset(c.O[:], 0.0)
                    v.memset(c.M[:, :, m0:m0 + H], LOWEST)
                if grand:
                    v.memset(c.S[:], 0.0)
                    v.memset(A[:], 0.0)
        with nc.Block() as block:
            @block.sync
            def _(sp):
                nb = body_count(c, sp)
                with sp.Fori(0, nb) as b:
                    for q in range(QS):
                        s = b * QS + q
                        sp.wait_ge(batch_done, (b + nb * n_pass) * QS + (q + 1))
                        sp.dma_start(meta[:, q, :], c.meta_d[bass.ds(s, 1), :]).then_inc(rec_in[q], 16)
                        sp.dma_start(rec[:, q, :], c.rec_d[bass.ds(s, 1), :, :].rearrange("o p c -> (o p) c")).then_inc(rec_in[q], 16)
                        if kind == "L3c":
                            sp.dma_start(raw[:, q, :, :].rearrange("p j h -> p (j h)"),
                                         c.logit_d[bass.ds(s, 1), :, :].rearrange("o p c -> (o p) c")).then_inc(raw_in[q], 16)

            @block.gpsimd
            def _(pool):
                nb = body_count(c, pool)
                with pool.Fori(0, nb) as b:
                    for q in range(QS):
                        pool.wait_ge(rec_in[q], (b + nb * n_pass) * 32 + 32)
                        held(c, pool)
                        for i in range(BATCH):
                            used = pool.value_load(meta[0:1, q, 4 * i + 1:4 * i + 2], min_val=0, max_val=SLOTS)
                            if kind == "L0":
                                pool.indirect_dma_start(out=gate[:, q, i * SLOTS:(i + 1) * SLOTS, :].rearrange("p j h -> p (j h)"),
                                                        out_offset=None, in_=c.gate_win,
                                                        in_offset=bass.IndirectOffsetOnAxis(ap=rec[:, q, FIRST_AT + i:FIRST_AT + i + 1], axis=0)
                                                        ).then_inc(got_in[q], 16)
                            for j in range(i * SLOTS, (i + 1) * SLOTS):
                                with pool.If(used > j - i * SLOTS):
                                    pool.indirect_dma_start(out=got[:, q, j, :], out_offset=None, in_=tab,
                                                            in_offset=bass.IndirectOffsetOnAxis(ap=rec[:, q, j:j + 1], axis=0)).then_inc(got_in[q], 16)

            @block.scalar
            def _(act):
                nb = body_count(c, act)
                if kind == "L3a":
                    for q in range(QS):
                        act.sem_inc(raw_out[q], 16)
                with act.Fori(0, nb) as b:
                    for q in range(QS):
                        if kind == "L2":
                            act.wait_ge(z_done, b * QS + (q + 1))
                            nc.scalar.activation(prod[:], prod[:], ACT.Relu).then_inc(relu_done, 1)
                        if kind == "L3a":
                            act.wait_ge(raw_done, b * QS + (q + 1))
                            act.dma_start(c.logit_d[bass.ds(b * QS + q, 1), :, :].rearrange("o p c -> (o p) c"),
                                          raw[:, q, :, :].rearrange("p j h -> p (j h)")).then_inc(raw_out[q], 16)
                        act.wait_ge(lg_done, (b + nb * n_pass) * QS + (q + 1))
                        nc.scalar.activation(ex[:, q, :, :], lg[:, q, :, :], ACT.Exp).then_inc(ex_done, 1)
                if kind == "L3a":
                    for q in range(QS):
                        act.wait_ge(raw_out[q], nb * 16 + 16)
                    held(c, act)

            @block.tensor
            def _(pe):
                nb = body_count(c, pe)
                with pe.Fori(0, nb) as b:
                    for u in range(RING):
                        pe.wait_ge(taken, (b + nb * n_pass) * RING + (u + 1))
                        pe.wait_ge(w_done, (b + nb * n_pass) * RING + (u + 1))
                        for j in range(SLOTS):
                            mm = nc.tensor.matmul(acc[u % BATCH][:, 0:W], c.ident[:], wrow[:, u % BATCH, j, :],
                                                  start=(j == 0), stop=(j == SLOTS - 1))
                        mm.then_inc(acc_done, 1)

            @block.vector
            def _(dve):
                v = nc.vector
                if n_pass == 0:
                    dve.sem_inc(batch_done, QS)
                    dve.sem_inc(taken, BATCH)
                nb = body_count(c, dve)
                tiles = {}

                def at(a, q, i, n, n0=0):
                    return a[:, bass.ds(tiles[q][i], 1), n0:n0 + n].rearrange("p a f -> p (a f)")

                def over(ap, n=SLOTS):
                    return ap.unsqueeze(1).to_broadcast([ap.shape[0], n, ap.shape[1]])

                def item(i):
                    return slice(i * SLOTS, (i + 1) * SLOTS)

                def arrive(b, q):
                    dve.wait_ge(rec_in[q], (b + nb * n_pass) * 32 + 32)
                    if kind == "L3c":
                        dve.wait_ge(raw_in[q], b * 16 + 16)
                    if kind == "L3a":
                        dve.wait_ge(raw_out[q], b * 16 + 16)
                    held(c, dve)
                    tiles[q] = [dve.value_load(meta[0:1, q, 4 * i:4 * i + 1], min_val=0, max_val=T - 1) for i in range(BATCH)]
                    gathers = dve.value_load(meta[0:1, q, 3:4], min_val=1, max_val=CAP * SLOTS)
                    dve.wait_ge(got_in[q], (gathers + (b + 1) * BATCH) * 16 if kind == "L0" else gathers * 16)

                def logits(b, q):
                    l = lg[:, q, 0:BJ, m0:m0 + H]
                    mask = maskf[:, q, MASK_AT:MASK_AT + BJ]
                    wide = mask.unsqueeze(2).to_broadcast([P, BJ, H])
                    G = got[:, q, :, :]
                    if kind == "L0":
                        for i in range(BATCH):
                            v.tensor_tensor(prod[:, item(i), :], G[:, item(i), 0:F], over(at(c.K, q, i, F)), ALU.mult)
                        dve.drain()
                        v.tensor_reduce(l, prod[:].rearrange("p j (h d) -> p j h d", h=H), X_AXIS, ALU.add)
                        dve.drain()
                        v.tensor_scalar(l, l, 5.0, -5.0, ALU.min, ALU.max)
                        dve.drain()
                        v.tensor_tensor(l, l, gate[:, q, :, 0:8], ALU.add)
                        dve.drain()
                        v.scalar_tensor_tensor(l, l, L0_SCALE, wide, ALU.mult, ALU.add)
                    elif kind == "L1":
                        for i in range(BATCH):
                            v.tensor_tensor(lg[:, q, item(i), :], G[:, item(i), F:F + 4], over(at(c.adst, q, i, 4)), ALU.add)
                        dve.drain()
                        v.scalar_tensor_tensor(l, l, 0.2, l, ALU.mult, ALU.max)
                        dve.drain()
                        v.tensor_tensor(l, l, wide, ALU.add)
                    elif kind == "L2":
                        dve.wait_ge(relu_done, b * QS + (q + 1))
                        v.tensor_tensor(prod[:], prod[:], over(c.att2_relu[:], BJ), ALU.mult)
                        for i in range(BATCH):
                            v.tensor_tensor(wt[:, item(i), :], G[:, item(i), F:F + 4], over(at(c.adst, q, i, 4)), ALU.add)
                        dve.drain()
                        v.tensor_reduce(l, prod[:].rearrange("p j (h d) -> p j h d", h=H), X_AXIS, ALU.add)
                        v.tensor_tensor(wt[:], wt[:], wide, ALU.add)
                        dve.drain()
                        v.tensor_tensor(l, l, wt[:], ALU.add)
                    elif kind == "L3a":
                        for i in range(BATCH):
                            v.tensor_tensor(prod[:, item(i), :], G[:, item(i), 0:64], over(at(c.K, q, i, 64)), ALU.mult)
                        dve.drain()
                        v.tensor_reduce(l, prod[:].rearrange("p j (h d) -> p j h d", h=H), X_AXIS, ALU.add)
                        dve.drain()
                        v.scalar_tensor_tensor(raw[:, q, :, :], l, 0.25, wide, ALU.mult, ALU.add)
                        dve.drain().then_inc(raw_done, 1)
                        l = raw[:, q, :, :]
                    else:
                        for i in range(BATCH):
                            v.tensor_tensor(lg[:, q, item(i), 0:4], raw[:, q, item(i), :], over(at(c.M, q, i, 4)), ALU.subtract)
                            v.scalar_tensor_tensor(lg[:, q, item(i), 4], G[:, item(i), F], c.g[:, bass.ds(tiles[q][i], 1)],
                                                   mask[:, item(i)], ALU.add, ALU.add)
                    dve.drain()
                    v.tensor_reduce(mx[:], l.rearrange("p (i j) h -> p i h j", i=BATCH), X_AXIS, ALU.max)
                    dve.drain()
                    for i in range(BATCH):
                        M = at(c.M, q, i, H, m0)
                        v.tensor_tensor(mnew[:, i, :], M, mx[:, i, :], ALU.max)
                        dve.drain()
                        v.tensor_tensor(lg[:, q, BJ + i, m0:m0 + H], M, mnew[:, i, :], ALU.subtract)
                        dve.drain()
                        v.tensor_copy(M, mnew[:, i, :])
                        dve.drain()
                    to = lg[:, q, 0:BJ, m0:m0 + H].rearrange("p (i j) h -> p i j h", i=BATCH)
                    v.tensor_tensor(to, l.rearrange("p (i j) h -> p i j h", i=BATCH),
                                    mnew[:].unsqueeze(2).to_broadcast([P, BATCH, SLOTS, H]), ALU.subtract).then_inc(lg_done, 1)

                def weights(b, q):
                    dve.wait_ge(ex_done, (b + nb * n_pass) * QS + (q + 1))
                    held(c, dve)
                    e = ex[:, q, 0:BJ, m0:m0 + H]
                    if kind == "L0":
                        v.tensor_tensor(wt[:], e, gate[:, q, :, 8:16], ALU.mult)
                        dve.drain()
                    if kind == "L3c":
                        for i in range(BATCH):
                            v.tensor_tensor(wt[:, item(i), :], ex[:, q, item(i), 0:4], over(at(c.rs, q, i, 4)), ALU.mult)
                        dve.drain()
                        v.tensor_reduce(watt[:], wt[:], X_AXIS, ALU.add)
                        dve.drain()
                        v.tensor_tensor(watt[:], watt[:], ex[:, q, 0:BJ, 4], ALU.mult)
                        dve.drain()
                    if grand:
                        v.tensor_reduce(psum_s[:], e.rearrange("p (i j) h -> p i h j", i=BATCH), X_AXIS, ALU.add)

                def weigh(b, q, i):
                    x = got[:, q, item(i), rows_at:rows_at + F]
                    to = wrow[:, i, :, :]
                    ei = ex[:, q, item(i), m0:m0 + H]
                    if grand:
                        v.tensor_tensor(to.rearrange("p j (h f) -> p j h f", h=H), x.unsqueeze(2).to_broadcast([P, SLOTS, H, F]),
                                        ei.unsqueeze(3).to_broadcast([P, SLOTS, H, F]), ALU.mult).then_inc(w_done, 1)
                        s = at(c.S, q, i, H)
                        v.tensor_tensor(s, s, ex[:, q, BJ + i, :], ALU.mult)
                        dve.drain()
                        v.tensor_tensor(s, s, psum_s[:, i, :], ALU.add)
                        dve.drain()
                    elif kind == "L3c":
                        v.tensor_copy(to[:, :, F], ex[:, q, item(i), 4])
                        v.tensor_copy(to[:, :, F + 1], watt[:, item(i)])
                        v.tensor_tensor(to[:, :, 0:F], x, watt[:, item(i)].unsqueeze(2).to_broadcast([P, SLOTS, F]),
                                        ALU.mult).then_inc(w_done, 1)
                    else:
                        parts = to.rearrange("p j (h d) -> p j h d", h=H)
                        a = wt[:, item(i), :] if kind == "L0" else ei
                        v.tensor_copy(parts[:, :, :, D], ei)
                        v.tensor_tensor(parts[:, :, :, 0:D], x.rearrange("p j (h d) -> p j h d", h=H),
                                        a.unsqueeze(3).to_broadcast([P, SLOTS, H, D]), ALU.mult).then_inc(w_done, 1)

                def release():
                    dve.drain().then_inc(batch_done, 1)

                def add_up(b, q, i):
                    corr = ex[:, q, BJ + i, m0:m0 + H]
                    if grand:
                        o, n = A[:].rearrange("p (h d) -> p h d", h=H), F
                        v.tensor_scalar(rS[:], at(c.S, q, i, H), 1e-16, float(H), ALU.add, ALU.mult)
                    elif kind == "L3c":
                        o, n = at(O, q, i, W).unsqueeze(1), W
                    else:
                        o, n = at(O, q, i, W).rearrange("p (h d) -> p h d", h=H), D + 1
                    v.tensor_tensor(o, o, corr.unsqueeze(2).to_broadcast([P, H, n]), ALU.mult)
                    dve.drain()
                    if grand:
                        v.reciprocal(rS[:], rS[:])
                    dve.wait_ge(acc_done, (b + nb * n_pass) * RING + (q * BATCH + i + 1))
                    v.tensor_tensor(o, o, acc[i][:, 0:W].rearrange("p (h d) -> p h d", h=H), ALU.add).then_inc(taken, 1)
                    dve.drain()
                    if grand:
                        v.tensor_tensor(collapse[:].rearrange("p (h f) -> p h f", h=H), o, rS[:].unsqueeze(2).to_broadcast([P, H, F]), ALU.mult)
                        v.tensor_copy(at(c.rs, q, i, H), rS[:])
                        dve.drain()
                        v.tensor_reduce(at(O, q, i, F), collapse[:].rearrange("p (h f) -> p f h", h=H), X_AXIS, ALU.add)

                def add_rows(b, q):
                    for i in range(BATCH):
                        last = v.tensor_tensor(prod[:, item(i), :], got[:, q, item(i), 0:F], over(at(c.K, q, i, F)), ALU.add)
                    last.then_inc(z_done, 1)

                def finish(b, q):
                    weights(b, q)
                    weigh(b, q, 0)
                    if q >= 1:
                        add_up(b, q - 1, 1)
                    weigh(b, q, 1)
                    release()

                with dve.Fori(0, nb) as b:
                    for q in range(QS):
                        arrive(b, q)
                        if kind == "L2":
                            add_rows(b, q)
                        if kind != "L2" and q == 0:
                            logits(b, q)
                        if q >= 1:
                            finish(b, q - 1)
                        if kind == "L2" or q >= 1:
                            logits(b, q)
                        if q >= 1:
                            add_up(b, q - 1, 0)
                    finish(b, QS - 1)
                    add_up(b, QS - 1, 0)
                    add_up(b, QS - 1, 1)


def over_tiles(a, dims):
    return a.unsqueeze(1).to_broadcast(dims)


def layer_norm(c, dve, act, tag):
    nc = c.nc
    v = nc.vector
    centred, squared, summed, rooted = (c.sem(tag + n) for n in ("cen", "sq", "sum", "root"))
    square = flat_rows(c)

    def on_vector():
        full = [P, T, F]
        v.tensor_reduce(c.g[:], c.X[:], X_AXIS, ALU.add)
        dve.drain()
        v.tensor_scalar(c.g[:], c.g[:], 1.0 / F, None, ALU.mult)
        dve.drain()
        v.tensor_tensor(c.X[:], c.X[:], c.g[:].unsqueeze(2).to_broadcast(full), ALU.subtract).then_inc(centred, 1)
        dve.wait_ge(squared, 1)
        v.tensor_reduce(c.g[:], square, X_AXIS, ALU.add).then_inc(summed, 1)
        dve.wait_ge(rooted, 1)
        v.reciprocal(c.g[:], c.g[:])
        dve.drain()
        v.tensor_tensor(c.X[:], c.X[:], c.g[:].unsqueeze(2).to_broadcast(full), ALU.mult)

    def on_scalar():
        act.wait_ge(centred, 1)
        nc.scalar.activation(square, c.X[:], ACT.Square).then_inc(squared, 1)
        act.wait_ge(summed, 1)
        nc.scalar.activation(c.g[:], c.g[:], ACT.Sqrt, bias=c.eps[:], scale=1.0 / F).then_inc(rooted, 1)

    return on_vector, on_scalar


def flat_rows(c):
    return c.O[:, 0:T * F].rearrange("p (t f) -> p t f", f=F)


def normalised_rows(c, dve, H, floor, add):
    v = c.nc.vector
    o = sums_view(c, H).rearrange("p t (h d) -> p (t h) d", h=H)
    D = F // H
    r = c.rs[:].rearrange("p t h -> p (t h)")[:, 0:T * H]
    if add:
        v.tensor_scalar(r, o[:, :, D], add, None, ALU.add)
    else:
        v.tensor_scalar(r, o[:, :, D], floor, None, ALU.max)
    dve.drain()
    v.reciprocal(r, r)
    dve.drain()
    v.tensor_tensor(c.K[:].rearrange("p t (h d) -> p (t h) d", h=H), o[:, :, 0:D],
                    r.unsqueeze(2).to_broadcast([P, T * H, D]), ALU.mult)
    dve.drain()


def close_layer0(c):
    nc = c.nc
    with ExitStack() as local:
        ps = lambda n, s: local.enter_context(nc.psum_tensor(n, s, F32))
        og = c.sb("og", [P, GT, F], F32, local)
        oT = c.sb("oT", [P, 2, F], F32, local)
        pX = [ps(f"cX{i}", [P, 512]) for i in range(2)]
        pW = [ps(f"cW{i}", [P, 512]) for i in range(3)]
        staged, turned, copied, mm_done, taken = (c.sem("c0_" + n) for n in ("staged", "turned", "copied", "mm", "taken"))
        with nc.Block() as block:
            @block.vector
            def _(dve):
                normalised_rows(c, dve, 8, 1e-30, None)
                with dve.Fori(0, NG) as g:
                    nc.vector.tensor_copy(og[:], c.K[:, bass.ds(g * GT, GT), :]).then_inc(staged, 1)
                    for k in range(GT):
                        x = c.X[:, bass.ds(g * GT + k, 1), :].rearrange("p a f -> p (a f)")
                        dve.wait_ge(mm_done, g * GT + (k + 1))
                        nc.vector.tensor_tensor(x, x, pW[k % 3][:, 0:F], ALU.add).then_inc(taken, 1)

            @block.tensor
            def _(pe):
                def turn(g, k):
                    if k == 0:
                        pe.wait_ge(staged, g + 1)
                    if k >= 2:
                        pe.wait_ge(copied, g * GT + (k - 1))
                    nc.tensor.transpose(pX[k % 2][:, 0:F], og[:, k, :], c.ident[:]).then_inc(turned, 1)

                with pe.Fori(0, NG) as g:
                    turn(g, 0)
                    for k in range(GT):
                        if k + 1 < GT:
                            turn(g, k + 1)
                        pe.wait_ge(copied, g * GT + (k + 1))
                        if k >= 3:
                            pe.wait_ge(taken, g * GT + (k - 2))
                        nc.tensor.matmul(pW[k % 3][:, 0:F], oT[:, k % 2, :], c.wt[:, NODE0:NODE0 + F],
                                         start=True, stop=True).then_inc(mm_done, 1)

            @block.scalar
            def _(act):
                with act.Fori(0, NG) as g:
                    for k in range(GT):
                        act.wait_ge(turned, g * GT + (k + 1))
                        if k >= 2:
                            act.wait_ge(mm_done, g * GT + (k - 1))
                        nc.scalar.copy(oT[:, k % 2, :], pX[k % 2][:, 0:F]).then_inc(copied, 1)
    with nc.Block() as block:
        programs = {}

        @block.vector
        def _(dve):
            programs.update(zip("vs", layer_norm(c, dve, nc.scalar, "ln0_")))
            programs["v"]()

        @block.scalar
        def _(act):
            programs["s"]()


def close_layer1(c):
    nc = c.nc
    with nc.Block() as block:
        programs = {}

        @block.vector
        def _(dve):
            normalised_rows(c, dve, 4, None, 1e-16)
            nc.vector.tensor_tensor(c.X[:], c.X[:], c.K[:], ALU.add)
            dve.drain()
            programs.update(zip("vs", layer_norm(c, dve, nc.scalar, "ln1_")))
            programs["v"]()

        @block.scalar
        def _(act):
            programs["s"]()


def close_layer2(c):
    nc = c.nc
    full = [P, T, F]
    with ExitStack() as local:
        mean = c.sb("mean", [P, F], F32, local)
        sd = c.sb("sd", [P, F], F32, local)
        pm = local.enter_context(nc.psum_tensor("pm", [P, F], F32))
        pv = local.enter_context(nc.psum_tensor("pv", [P, F], F32))
        rows_done, summed, centred, squared, var_sum, rooted, rooted_in = (
            c.sem("c2_" + n) for n in ("rows", "sum", "cen", "sq", "var", "root", "rin"))
        with nc.Block() as block:
            programs = {}

            @block.vector
            def _(dve):
                v = nc.vector
                normalised_rows(c, dve, 4, 1e-30, None)
                v.tensor_tensor(c.K[:], c.K[:], over_tiles(c.bias[:], full), ALU.add).then_inc(rows_done, 1)
                dve.wait_ge(summed, 1)
                v.tensor_scalar(mean[:], pm[:], 1.0 / N, None, ALU.mult)
                dve.drain()
                v.tensor_tensor(c.K[:], c.K[:], over_tiles(mean[:], full), ALU.subtract).then_inc(centred, 1)
                dve.wait_ge(rooted, 1)
                v.reciprocal(sd[:], sd[:])
                dve.drain()
                v.tensor_tensor(sd[:], sd[:], c.gamma[:], ALU.mult)
                dve.drain()
                v.tensor_tensor(c.K[:], c.K[:], over_tiles(sd[:], full), ALU.mult)
                dve.drain()
                v.tensor_tensor(c.K[:], c.K[:], over_tiles(c.beta[:], full), ALU.add)
                dve.drain()
                v.scalar_tensor_tensor(c.K[:], c.K[:], 0.02, c.K[:], ALU.mult, ALU.max)
                dve.drain()
                v.tensor_tensor(c.X[:], c.X[:], c.K[:], ALU.add)
                dve.drain()
                programs.update(zip("vs", layer_norm(c, dve, nc.scalar, "ln2_")))
                programs["v"]()

            @block.tensor
            def _(pe):
                def sum_nodes(to, a, done):
                    nc.tensor.matmul(to[:], c.ones[:], a[:, 0, :], start=True, stop=False)
                    with pe.Fori(1, T - 1) as t:
                        nc.tensor.matmul(to[:], c.ones[:], a[:, bass.ds(t, 1), :].rearrange("p a f -> p (a f)"),
                                         start=False, stop=False)
                    nc.tensor.matmul(to[:], c.valid[:], a[:, T - 1, :], start=False, stop=True).then_inc(done, 1)

                pe.wait_ge(rows_done, 1)
                sum_nodes(pm, c.K, summed)
                pe.wait_ge(squared, 1)
                sum_nodes(pv, flat_rows(c), var_sum)

            @block.scalar
            def _(act):
                act.wait_ge(centred, 1)
                nc.scalar.activation(flat_rows(c), c.K[:], ACT.Square).then_inc(squared, 1)
                act.wait_ge(var_sum, 1)
                nc.scalar.activation(sd[:], pv[:], ACT.Sqrt, bias=c.eps[:], scale=1.0 / N).then_inc(rooted, 1)
                programs["s"]()


def gradient_norm(c):
    nc = c.nc
    o = flat_rows(c)
    summed, rooted, minus, squared = (c.sem("gn_" + n) for n in ("sum", "root", "minus", "sq"))
    with nc.Block() as block:
        @block.vector
        def _(dve):
            v = nc.vector
            v.tensor_tensor(o, o, c.X[:], ALU.subtract).then_inc(minus, 1)
            dve.wait_ge(squared, 1)
            v.tensor_scalar(o, o, 0.1, None, ALU.max)
            dve.drain()
            v.tensor_reduce(c.g[:], o, X_AXIS, ALU.add).then_inc(summed, 1)
            dve.wait_ge(rooted, 1)
            v.reciprocal(c.g[:], c.g[:])

        @block.scalar
        def _(act):
            act.wait_ge(minus, 1)
            nc.scalar.activation(o, o, ACT.Square).then_inc(squared, 1)
            act.wait_ge(summed, 1)
            nc.scalar.activation(c.g[:], c.g[:], ACT.Sqrt).then_inc(rooted, 1)


def close_layer3(c):
    nc = c.nc
    full = [P, T, F]
    with nc.Block() as block:
        programs = {}

        @block.vector
        def _(dve):
            v = nc.vector
            o, rs = sums_view(c, 1, 1), c.rs[:].rearrange("p t h -> p (t h)")[:, 0:T]
            v.tensor_scalar(rs, o[:, :, F], 1e-16, None, ALU.add)
            v.tensor_tensor(c.K[:], c.X[:], o[:, :, F + 1:F + 2].to_broadcast(full), ALU.mult)
            dve.drain()
            v.reciprocal(rs, rs)
            v.tensor_tensor(c.K[:], o[:, :, 0:F], c.K[:], ALU.subtract)
            dve.drain()
            v.tensor_tensor(c.K[:], c.K[:], rs.unsqueeze(2).to_broadcast(full), ALU.mult)
            dve.drain()
            v.tensor_tensor(c.X[:], c.X[:], c.K[:], ALU.add)
            dve.drain()
            programs.update(zip("vs", layer_norm(c, dve, nc.scalar, "ln3_")))
            programs["v"]()

        @block.scalar
        def _(act):
            programs["s"]()


_INS = ("x", "src", "dst", "edge_attr_128")


def kernel(**inputs):
    import numpy as np
    import concourse.bacc as bacc
    from concourse.bass_utils import run_bass_kernel_spmd

    nc = bacc.Bacc("TRN2", target_bir_lowering=False, num_devices=1)
    arrays, aps = {}, {}
    for name in inputs:
        a = np.ascontiguousarray(inputs[name])
        arrays["in_" + name] = a
        aps[name] = nc.dram_tensor("in_" + name, a.shape, mybir.dt.from_np(a.dtype), kind="ExternalInput").ap()
    out = nc.dram_tensor("out_x", (N, F), F32, kind="ExternalOutput").ap()
    weights = {name: ap for name, ap in aps.items() if name not in _INS}
    build(nc, aps["x"], aps["src"], aps["dst"], aps["edge_attr_128"], weights, out)
    return run_bass_kernel_spmd(nc, [arrays], core_ids=[0]).results[0]["out_x"]
```

```python
from contextlib import ExitStack

import concourse.bass as bass
from concourse import mybir

F32 = mybir.dt.float32
BF16 = mybir.dt.bfloat16
I32 = mybir.dt.int32
ALU = mybir.AluOpType
ACT = mybir.ActivationFunctionType
X_AXIS = mybir.AxisListType.X

P = 128
N = 6250
E = 106250
F = 128
T = -(-N // P)
NPAD = T * P
LAST = N - (T - 1) * P
GT = 7
NG = T // GT
SLOTS = 8
RING = 8
BATCH = 2
QS = RING // BATCH
BJ = BATCH * SLOTS
BUCKETS = 64
BLK = 250
NBLK = E // BLK
O_W = F + 8
LIST_W = 112
CAP = P * LIST_W
TILE_BASE = 64
REC = 36
FIRST_AT = BJ
MASK_AT = 20
MASKED = -3.0e38
LOWEST = -1.0e37
assert BATCH == 2 and T <= TILE_BASE
assert T % GT == 0 and E % BLK == 0
assert O_W * T >= 2 * BUCKETS * T and F * T >= 2 * BUCKETS * T
assert CAP >= (E + E // P + BUCKETS) // SLOTS + T and CAP % RING == 0

ER = 10
E_MAIN = E // P // ER * ER
ESTEPS = E_MAIN // ER
FS = 6
E_TAIL = E - P * E_MAIN

L0_SCALE = 4.0


def bc(ap, shape):
    return ap.to_broadcast(shape)


class Core:
    pass


def build(nc, x, src, dst, edge_attr, w, out):
    ctx = ExitStack()
    with ctx:
        c = Core()
        c.nc = nc

        def sb(name, shape, dt=F32, where=ctx):
            return where.enter_context(nc.sbuf_tensor(name, shape, dt))

        def sem(name, where=ctx):
            return where.enter_context(nc.semaphore(name))

        c.sb, c.sem = sb, sem
        c.passed = sem("passed")
        c.src, c.dst, c.x, c.edge_attr, c.w, c.out = src, dst, x, edge_attr, w, out
        def dram(name, shape, dt=F32):
            return nc.dram_tensor(name, shape, dt).ap()

        c.samples_d = dram("samples_d", [1, NBLK], I32)
        c.src_pad = dram("src_pad", [E + 16], I32)
        c.src_win = dram("src_win", [E + 1, SLOTS], I32)
        c.edge_gate = dram("edge_gate", [E + SLOTS, 16])
        c.gate_win = dram("gate_win", [E + 1, SLOTS * 16])
        c.order = dram("order", [NPAD, 4], I32)
        c.meta_d = dram("meta_d", [(CAP + RING) // BATCH, BATCH * 4], I32)
        c.rec_d = dram("rec_d", [(CAP + RING) // BATCH, P, REC], I32)
        c.logit_d = dram("logit_d", [(CAP + RING) // BATCH, P, BJ * 4])
        c.tab = [dram("tab0", [NPAD, 2 * F]), dram("tab1", [NPAD, F + 4]), dram("tab2", [NPAD, F + 4]),
                 dram("tab3", [NPAD, 64 + F]), dram("tab4", [NPAD, F + 1])]
        c.X = sb("X", [P, T, F])
        c.K = sb("K", [P, T, F])
        c.O = sb("O", [P, T * O_W])
        c.M = sb("M", [P, T, 8])
        c.S = sb("S", [P, T, 8])
        c.rs = sb("rs", [P, T, 8])
        c.adst = sb("adst", [P, T, 4])
        c.g = sb("g", [P, T])
        c.ids = sb("ids", [P, T], I32)
        c.start = sb("start", [P, T])
        c.first = sb("first", [P, T])
        c.deg = sb("deg", [P, T])
        c.bodies = sb("bodies", [1, 1], I32)
        c.slot = sb("slot", [P, SLOTS])
        c.diag = sb("diag", [P, P])
        c.ident = sb("ident", [P, P])
        c.ones = sb("ones", [P, P])
        c.valid = sb("valid", [P, P])
        c.eps = sb("eps", [P, 1])
        c.id_st = sb("id_st", [P, GT], I32)
        c.pass_sems = ([sem(f"rec{u}") for u in range(QS)], sem("batch"), sem("lg"), sem("ex"), sem("weighed"), sem("acc"), sem("taken"), sem("here"))
        c.project_sems = tuple(sem("p_" + n) for n in ("turned", "copied", "mm", "rows", "scat", "free", "summed", "rooted",
                                                         "closed", "staged"))
        c.y_out = sem("y_out")
        constants(c)
        prepare(c)
        load_weights(c)
        project(c, 0)
        edge_pass(c, "L0")
        node_product(c)
        project(c, 1)
        edge_pass(c, "L1")
        project(c, 2)
        edge_pass(c, "L2")
        batch_statistics(c)
        project(c, 3)
        edge_pass(c, "L3a")
        project(c, 4)
        edge_pass(c, "L3c")
        project(c, 5)


def constants(c):
    nc = c.nc
    iota_done, made = c.sem("iota_done"), c.sem("const_made")
    with nc.Block() as block:
        @block.gpsimd
        def _(pool):
            nc.gpsimd.iota(c.slot[:], pattern=[[1, SLOTS]], base=0, channel_multiplier=0,
                           allow_small_or_imprecise_dtypes=True)
            nc.gpsimd.iota(c.diag[:], pattern=[[1, P]], base=0, channel_multiplier=-1,
                           allow_small_or_imprecise_dtypes=True).then_inc(iota_done, 1)

        @block.vector
        def _(dve):
            nc.vector.memset(c.ones[:], 1.0)
            nc.vector.memset(c.valid[:], 0.0)
            nc.vector.memset(c.eps[:], 1e-5)
            dve.drain()
            nc.vector.memset(c.valid[0:LAST - LAST % 32, :], 1.0)
            dve.wait_ge(iota_done, 1)
            nc.vector.tensor_scalar(c.ident[:], c.diag[:], 0.0, None, ALU.is_equal)
            dve.drain()
            nc.vector.tensor_reduce(c.valid[96:P, 0:1], c.ident[96:P, 0:LAST], X_AXIS, ALU.add)
            dve.drain()
            nc.vector.tensor_scalar(c.valid[96:P, :], c.ones[96:P, :], c.valid[96:P, 0:1], None,
                                    ALU.mult).then_inc(made, 1)


PE_DEGREES = 18
PE_COUNTS = 20
PE_TALLEST = 36
PE_BEFORE = 43
CHUNKS = 7
WIN_EVERY = 4


def prepare(c):
    nc, w, sem = c.nc, c.w, c.sem
    with ExitStack() as local:
        sb = lambda n, s, d=F32: c.sb(n, s, d, local)
        ps = lambda n, s: local.enter_context(nc.psum_tensor(n, s, F32))
        w_eg = sb("w_eg", [16, F])
        w_egT = sb("w_egT", [F, 16])
        feat = sb("feat", [P, FS, ER, F])
        featT = sb("featT", [P, 2, ER, P])
        res = sb("res", [P, 2, ER, 16])
        tailf = sb("tailf", [16, F])
        zeros = sb("zeros", [1, 16 * SLOTS])
        zeros_i = sb("zeros_i", [1, 16], I32)
        pT = [ps(f"pT{i}", [P, 4, P]) for i in range(3)]
        pO = [ps(f"pO{i}", [P, ER, 16]) for i in range(2)]
        w_in, w_ready, w_t = sem("eg_w_in"), sem("eg_w_ready"), sem("eg_w_t")
        feat_in = [sem(f"feat_in{i}") for i in range(FS)]
        tr_done, tr_copied, mm_done, res_done = sem("eg_tr"), sem("eg_copied"), sem("eg_mm"), sem("eg_res")
        res_out = [sem(f"res_out{i}") for i in range(2)]
        heads_out, heads_in, pads = sem("heads_out"), sem("heads_in"), sem("pads")
        wins, gwins, zero_done = sem("wins"), sem("gwins"), sem("zero_done")
        ea = c.edge_attr[0:P * E_MAIN, :].rearrange("(s p r) f -> s p r f", p=P, r=ER)
        eg = c.edge_gate[0:P * E_MAIN, :].rearrange("(s p r) f -> s p r f", p=P, r=ER)
        node = sb("node", [P, T])
        heads = sb("heads", [P, NBLK], I32)
        less = sb("less", [P, GT, NBLK])
        cnt = sb("cnt", [P, GT])
        blk = sb("blk", [P, T])
        blk_i = sb("blk_i", [P, T], I32)
        rows = sb("rows", [P, 2, GT, BLK], I32)
        node_done, blk_done, rows_used = sem("node_done"), sem("blk_done"), sem("rows_used")
        rows_in = [sem(f"rows_in{i}") for i in range(2)]
        B, CH = BUCKETS, BUCKETS * T // CHUNKS
        up1 = sb("up1", [P, P])
        up127 = sb("up127", [P, P])
        below = sb("below", [P, P], BF16)
        ones_b = sb("ones_b", [P, P], BF16)
        nxt = sb("nxt", [P, T])
        deg = sb("deg0", [P, T])
        cls = sb("cls", [P, T])
        cls_io = sb("cls_io", [P, B])
        hot = sb("hot", [P, B, T], BF16)
        hotf = hot[:].rearrange("p b t -> p (b t)")
        kflat = c.K[:].rearrange("p t f -> p (t f)")
        tot = c.O[:, 0:B * T]
        pre = c.O[:, B * T:2 * B * T]
        incl = kflat[:, 0:B * T]
        zero = kflat[:, B * T:2 * B * T]
        rank = sb("rank", [P, T])
        rank_i = sb("rank_i", [P, T], I32)
        recs = sb("recs", [P, T, 4], I32)
        rank_st = sb("rank_st", [P, GT], I32)
        rec_st = sb("rec_st", [P, GT, 4], I32)
        back = sb("back", [P, T, 4], I32)
        small = ps("small", [P, 512])
        pn, pt, pj, pcum = small[:, 0:T], small[0:T, 64:64 + P], small[:, 256:256 + 2 * T], small[:, 400:400 + QS]
        pc = [ps(f"pc{i}", [P, 512]) for i in range(2)]
        mats, shifted, hot_done, counted, counts_got, rank_done = (
            sem(n) for n in ("so_mats", "so_shift", "so_hot", "so_counted", "so_got", "so_rank"))
        order_out, order_in, ids_done, x_in = sem("order_out"), sem("order_in"), sem("ids_done"), sem("x_in")
        LW = LIST_W
        jmax = sb("jmax", [T, 2])
        jint = sb("jint", [T, 1], I32)
        dj = sb("dj", [T, 2, T])
        jn = sb("jn", [P, 2, T])
        iend = sb("iend", [P, T])
        ibeg = sb("ibeg", [P, T])
        item = sb("item", [P, LW])
        past = c.O[:, 0:LW * T].rearrange("p (w t) -> p w t", t=T)
        begun = kflat[:, 0:LW * T].rearrange("p (w t) -> p w t", t=T)
        tile_of = sb("tile_of", [P, LW])
        base = sb("base", [P, LW])
        jm = sb("jm", [P, LW])
        s0 = sb("s0", [P, LW])
        meta = sb("meta", [P, LW, 4], I32)
        nb_f = sb("nb", [1, 1])
        nb_i = sb("nbi", [1, 1], I32)
        before = sb("before", [P, P])
        cum = sb("cum", [P, LW // RING, QS])
        pair = sb("pair", [P, LW // RING, QS])
        zw = sb("zw", [P, T])
        tr, dj_done, bcast, meta_done, meta_out, rows_done, rows_sum = (
            sem(n) for n in ("il_tr", "il_dj", "il_bc", "il_meta", "il_out", "il_rows", "il_rsum"))
        mrow = sb("mrow", [P, QS * BATCH, 4], I32)
        rec = sb("rec_b", [P, QS, REC], I32)
        offf = sb("offf", [P, QS * BATCH])
        off = sb("off", [P, QS * BATCH], I32)
        left = sb("left", [P, QS * BATCH])
        HI = RING // 2
        win = sb("win", [P, QS * BATCH, SLOTS], I32)
        mrow_in = [sem(f"ir_meta{h}") for h in range(2)]
        off_done, rec_done = sem("ir_off"), sem("ir_rec")
        win_in = [sem(f"ir_win{h}") for h in range(2)]
        rec_out = [sem(f"ir_out{h}") for h in range(2)]
        maskf = rec[:].bitcast(F32)

        def res_count(i, par):
            return 16 * ((i + 1) // 2 + 1 if par == 0 else i // 2)

        with nc.Block() as block:
            @block.sync
            def _(sp):
                sp.dma_start(w_eg[0:8, :], w["L0_gnn_Wedge"]).then_inc(w_in, 16)
                sp.dma_start(w_eg[8:16, :], w["L0_gnn_Wgate"]).then_inc(w_in, 16)
                sp.dma_start(tailf[0:E_TAIL, :], c.edge_attr[P * E_MAIN:E, :]).then_inc(w_in, 16)
                sp.dma_start(c.samples_d, c.dst.rearrange("(b r) -> r b", r=BLK)[0:1, :],
                             allow_slow_non_contiguous=True).then_inc(heads_out, 16)
                sp.wait_ge(heads_out, 16)
                sp.dma_start(heads[:], c.samples_d.to_broadcast([P, NBLK])).then_inc(heads_in, 16)
                sp.dma_start(c.src_pad[0:E].rearrange("(a b) -> a b", a=50),
                             c.src.rearrange("(a b) -> a b", a=50)).then_inc(pads, 16)
                sp.wait_ge(zero_done, 1)
                sp.dma_start(c.src_pad[E:E + 16].rearrange("(a b) -> a b", a=1), zeros_i[:]).then_inc(pads, 16)
                sp.dma_start(c.edge_gate[E:E + SLOTS, :].rearrange("(o a) b -> o (a b)", o=1), zeros[:]).then_inc(pads, 16)
                for i in range(2):
                    sp.dma_start(feat[:, i, :, :], ea[i]).then_inc(feat_in[i], 16)
                sp.wait_ge(pads, 48)
                h = E // 2
                for a, b in ((0, h), (h, E + 1)):
                    sp.dma_start(c.src_win[a:b, :], bass.AP(c.src_pad.tensor, a, [[1, b - a], [1, SLOTS]])).then_inc(wins, 16)
                at = n_win = 0

                def gate_windows(steps, end):
                    for par in range(2):
                        sp.wait_ge(res_out[par], res_count(steps, par))
                    sp.dma_start(c.gate_win[at:end, :], bass.AP(c.edge_gate.tensor, 16 * at, [[16, end - at], [1, 16 * SLOTS]])).then_inc(gwins, 16)
                    return end

                for i in range(2, ESTEPS):
                    if i >= FS:
                        sp.wait_ge(tr_done, 3 * (i - FS + 1))
                    sp.dma_start(feat[:, i % FS, :, :], ea[i]).then_inc(feat_in[i % FS], 16)
                    done = i - FS - 1
                    if done >= WIN_EVERY and done % WIN_EVERY == 0:
                        at = gate_windows(done, done * P * ER - SLOTS)
                        n_win += 1
                gate_windows(ESTEPS, E + 1)
                sp.wait_ge(wins, 32)
                sp.wait_ge(gwins, 16 * (n_win + 1))

            @block.tensor
            def _(pe):
                def degrees():
                    pe.wait_ge(mats, 1)
                    nc.tensor.matmul(pn, up1[:], c.start[:], start=True, stop=False)
                    nc.tensor.matmul(pn, up127[:], nxt[:], start=False, stop=True).then_inc(shifted, 1)

                def counts(k):
                    if k == 0:
                        pe.wait_ge(hot_done, 1)
                    else:
                        pe.wait_ge(counts_got, k)
                    part = hotf[:, k * CH:(k + 1) * CH]
                    nc.tensor.matmul(pc[0][:, 0:CH], ones_b[:], part, start=True, stop=True)
                    nc.tensor.matmul(pc[1][:, 0:CH], below[:], part, start=True, stop=True).then_inc(counted, 1)

                def tallest():
                    pe.wait_ge(ids_done, 1)
                    nc.tensor.transpose(pt, c.deg[:], c.ident[:]).then_inc(tr, 1)

                    pe.wait_ge(dj_done, 1)
                    nc.tensor.matmul(pj, c.ones[0:T, :], dj[:].rearrange("a b t -> a (b t)"), start=True, stop=True).then_inc(bcast, 1)

                def rows_before():
                    pe.wait_ge(rows_done, 1)
                    nc.tensor.matmul(pcum, before[:], cum[:, LW // RING - 1, :], start=True, stop=True).then_inc(rows_sum, 1)

                beside = {PE_DEGREES: degrees, PE_TALLEST: tallest, PE_BEFORE: rows_before}
                pe.wait_ge(w_in, 48)
                nc.tensor.transpose(pT[0][:, 0, 0:16], w_eg[:], c.ident[0:16, 0:16])
                nc.tensor.transpose(pT[0][:, 1, 0:E_TAIL], tailf[0:E_TAIL, :], c.ident[0:E_TAIL, 0:E_TAIL]).then_inc(w_ready, 1)
                pe.wait_ge(w_t, 1)
                nc.tensor.matmul(pO[0][0:E_TAIL, 0, :], featT[:, 0, 0, 0:E_TAIL], w_egT[:], start=True, stop=True).then_inc(w_ready, 1)

                def project_step(i):
                    pe.wait_ge(tr_copied, 3 * (i + 1))
                    if i != 1:
                        pe.wait_ge(res_done, max(i, 1))
                    for r in range(ER):
                        mm = nc.tensor.matmul(pO[i % 2][:, r, :], featT[:, i % 2, r, :], w_egT[:], start=True, stop=True)
                    mm.then_inc(mm_done, 1)

                for i in range(ESTEPS):
                    pe.wait_ge(feat_in[i % FS], 16 * (i // FS + 1))
                    for q, (a, b) in enumerate(((0, 4), (4, 8), (8, ER))):
                        if i:
                            pe.wait_ge(tr_copied, 3 * (i - 1) + q + 1)
                        else:
                            pe.wait_ge(w_t, 1)
                        for r in range(a, b):
                            mm = nc.tensor.transpose(pT[q][:, r - a, :], feat[:, i % FS, r, :], c.ident[:])
                        mm.then_inc(tr_done, 1)
                    if i:
                        project_step(i - 1)
                    if i in beside:
                        beside[i]()
                    if i == PE_COUNTS:
                        for k in range(CHUNKS):
                            counts(k)
                project_step(ESTEPS - 1)

            @block.scalar
            def _(act):
                act.wait_ge(w_ready, 1)
                nc.scalar.copy(w_egT[:], pT[0][:, 0, 0:16])
                nc.scalar.copy(featT[:, 0, 0, 0:E_TAIL], pT[0][:, 1, 0:E_TAIL]).then_inc(w_t, 1)
                act.wait_ge(w_ready, 2)
                nc.scalar.copy(res[0:E_TAIL, 0, 0, 0:8], pO[0][0:E_TAIL, 0, 0:8])
                nc.scalar.activation(res[0:E_TAIL, 0, 0, 8:16], pO[0][0:E_TAIL, 0, 8:16], ACT.Sigmoid).then_inc(res_done, 1)
                act.wait_ge(res_done, 1)
                act.dma_start(c.edge_gate[P * E_MAIN:E, :], res[0:E_TAIL, 0, 0, :]).then_inc(res_out[0], 16)

                def results(i):
                    act.wait_ge(mm_done, i + 1)
                    n = (i // 2 + (1 if i % 2 == 0 else 0))
                    if n:
                        act.wait_ge(res_out[i % 2], 16 * n)
                    nc.scalar.copy(res[:, i % 2, :, 0:8], pO[i % 2][:, :, 0:8])
                    nc.scalar.activation(res[:, i % 2, :, 8:16], pO[i % 2][:, :, 8:16], ACT.Sigmoid).then_inc(res_done, 1)
                    act.wait_ge(res_done, i + 2)
                    act.dma_start(eg[i], res[:, i % 2, :, :]).then_inc(res_out[i % 2], 16)

                for i in range(ESTEPS):
                    for q, (a, b) in enumerate(((0, 4), (4, 8), (8, ER))):
                        act.wait_ge(tr_done, 3 * i + q + 1)
                        if i >= 2:
                            act.wait_ge(mm_done, i - 1)
                        nc.scalar.copy(featT[:, i % 2, a:b, :], pT[q][:, 0:b - a, :]).then_inc(tr_copied, 1)
                    if i:
                        results(i - 1)
                results(ESTEPS - 1)
                for par in range(2):
                    act.wait_ge(res_out[par], res_count(ESTEPS, par))

            @block.gpsimd
            def _(pool):
                io = dict(allow_small_or_imprecise_dtypes=True)
                nc.gpsimd.iota(node[:], pattern=[[P, T]], base=0, channel_multiplier=1, **io)
                nc.gpsimd.iota(cls_io[:], pattern=[[1, B]], base=0, channel_multiplier=0, **io)
                nc.gpsimd.iota(item[:], pattern=[[1, LW]], base=0, channel_multiplier=LW, **io).then_inc(node_done, 1)
                dst_rows = c.dst.rearrange("(b r) -> b r", r=BLK)
                for g in range(NG):
                    pool.wait_ge(blk_done, g + 1)
                    if g >= 2:
                        pool.wait_ge(rows_used, g - 1)
                    for k in range(GT):
                        i = g * GT + k
                        pool.indirect_dma_start(out=rows[:, g % 2, k, :], out_offset=None, in_=dst_rows,
                                                in_offset=bass.IndirectOffsetOnAxis(ap=blk_i[:, i:i + 1], axis=0)).then_inc(rows_in[g % 2], 16)
                pool.wait_ge(rank_done, 1)
                with pool.Fori(0, NG) as g:
                    nc.gpsimd.tensor_copy(rank_st[:], rank_i[:, bass.ds(g * GT, GT)])
                    nc.gpsimd.tensor_copy(rec_st[:], recs[:, bass.ds(g * GT, GT), :])
                    pool.drain()
                    for k in range(GT):
                        pool.indirect_dma_start(out=c.order, out_offset=bass.IndirectOffsetOnAxis(ap=rank_st[:, k:k + 1], axis=0),
                                                in_=rec_st[:, k, :], in_offset=None).then_inc(order_out, 16)
                    pool.wait_ge(order_out, (g + 1) * (16 * GT))
                    held(c, pool)
                pool.wait_ge(order_out, 16 * T)
                pool.dma_start(back[:], c.order.rearrange("(t p) c -> p t c", p=P)).then_inc(order_in, 16)
                pool.wait_ge(ids_done, 1)
                for i in range(T):
                    n = LAST if i == T - 1 else P
                    pool.indirect_dma_start(out=c.X[0:n, i, :], out_offset=None, in_=c.x,
                                            in_offset=bass.IndirectOffsetOnAxis(ap=c.ids[0:n, i:i + 1], axis=0)).then_inc(x_in, 16)
                pool.wait_ge(meta_done, 1)
                pool.dma_start(c.meta_d[0:CAP // BATCH, :].rearrange("(p w) (i c) -> p (w i) c", p=P, i=BATCH), meta[:]).then_inc(meta_out, 16)
                pool.wait_ge(meta_out, 16)
                nb = body_count(c, pool)
                def bring(b, h):
                    pool.dma_start(mrow[:, h * HI:(h + 1) * HI, :].rearrange("p i c -> p (i c)"),
                                   c.meta_d.rearrange("(a s) c -> a (s c)", s=QS // 2)[bass.ds(b * 2 + h, 1), :].to_broadcast([P, HI * 4])
                                   ).then_inc(mrow_in[h], 16)

                def windows(b, h):
                    pool.wait_ge(off_done, b * 2 + (h + 1))
                    held(c, pool)
                    for i in range(h * HI, (h + 1) * HI):
                        pool.indirect_dma_start(out=win[:, i, :], out_offset=None, in_=c.src_win,
                                                in_offset=bass.IndirectOffsetOnAxis(ap=off[:, i:i + 1], axis=0)).then_inc(win_in[h], 16)

                def put(b, h):
                    pool.wait_ge(rec_done, b * 2 + (h + 1))
                    pool.dma_start(c.rec_d.rearrange("(a s) p c -> a p s c", s=QS // 2)[bass.ds(b * 2 + h, 1), :, :, :].rearrange("o p s c -> (o p) s c"),
                                   rec[:, h * (QS // 2):(h + 1) * (QS // 2), :]).then_inc(rec_out[h], 16)

                bring(0, 0)
                bring(0, 1)
                windows(0, 0)
                with pool.Fori(0, nb) as b:
                    windows(b, 1)
                    with pool.If(b < nb - 1):
                        bring(b + 1, 0)
                    put(b, 0)
                    with pool.If(b < nb - 1):
                        bring(b + 1, 1)
                        windows(b + 1, 0)
                    put(b, 1)
                for h in range(2):
                    pool.wait_ge(rec_out[h], nb * 16)
                pool.wait_ge(x_in, 16 * T)
                held(c, pool)

            @block.vector
            def _(dve):
                v = nc.vector
                v.memset(zeros[:], 0.0)
                v.memset(zeros_i[:], 0).then_inc(zero_done, 1)
                v.memset(c.X[:, T - 1, :], 0.0)
                v.memset(recs[:], 0)
                v.memset(rec[:], 0)
                v.memset(meta[:], 0)
                v.memset(zw[:], 0.0)
                v.memset(ones_b[:], 1.0)
                v.memset(zero, 0.0)
                v.memset(nxt[:, T - 1:T], float(E))
                v.tensor_scalar(up1[:], c.diag[:], -1.0, None, ALU.is_equal)
                v.tensor_scalar(up127[:], c.diag[:], 127.0, None, ALU.is_equal)
                v.tensor_scalar(below[:], c.diag[:], 0.0, None, ALU.is_gt)
                v.tensor_scalar(before[:], c.diag[:], 0.0, None, ALU.is_gt)
                dve.wait_ge(node_done, 1)
                dve.wait_ge(heads_in, 16)

                def group(a, g):
                    return a[:, g * GT:(g + 1) * GT]

                def find_row(g):
                    v.tensor_tensor(less[:], heads[:].unsqueeze(1).to_broadcast([P, GT, NBLK]),
                                    group(node, g).unsqueeze(2).to_broadcast([P, GT, NBLK]), ALU.is_lt)
                    dve.drain()
                    v.tensor_reduce(cnt[:], less[:], X_AXIS, ALU.add)
                    dve.drain()
                    v.tensor_scalar(group(blk, g), cnt[:], -1.0, 0.0, ALU.add, ALU.max)
                    dve.drain()
                    v.tensor_copy(group(blk_i, g), group(blk, g)).then_inc(blk_done, 1)

                def find_in_row(g):
                    dve.wait_ge(rows_in[g % 2], (g // 2 + 1) * (16 * GT))
                    v.tensor_tensor(less[:, :, 0:BLK], rows[:, g % 2, :, :],
                                    group(node, g).unsqueeze(2).to_broadcast([P, GT, BLK]), ALU.is_lt)
                    dve.drain().then_inc(rows_used, 1)
                    v.tensor_reduce(cnt[:], less[:, :, 0:BLK], X_AXIS, ALU.add)
                    dve.drain()
                    v.scalar_tensor_tensor(group(c.start, g), group(blk, g), float(BLK), cnt[:], ALU.mult, ALU.add)

                find_row(0)
                for g in range(1, NG):
                    find_row(g)
                    find_in_row(g - 1)
                find_in_row(NG - 1)
                dve.drain()

                v.tensor_copy(nxt[:, 0:T - 1], c.start[:, 1:T]).then_inc(mats, 1)
                v.tensor_copy(recs[:, :, 0], node[:])
                v.tensor_copy(recs[:, :, 1], c.start[:])
                dve.wait_ge(shifted, 1)
                v.tensor_tensor(deg[:], pn, c.start[:], ALU.subtract)
                dve.drain()
                v.tensor_copy(recs[:, :, 2], deg[:])
                v.tensor_scalar(cls[:], deg[:], -1.0, float(B - 1), ALU.mult, ALU.add)
                dve.drain()
                v.tensor_scalar(cls[:], cls[:], 0.0, None, ALU.max)
                dve.drain()
                v.tensor_tensor(hot[:], cls_io[:].unsqueeze(2).to_broadcast([P, B, T]),
                                cls[:].unsqueeze(1).to_broadcast([P, B, T]), ALU.is_equal).then_inc(hot_done, 1)
                for k in range(CHUNKS):
                    dve.wait_ge(counted, k + 1)
                    v.tensor_copy(tot[:, k * CH:(k + 1) * CH], pc[0][:, 0:CH])
                    v.tensor_copy(pre[:, k * CH:(k + 1) * CH], pc[1][:, 0:CH]).then_inc(counts_got, 1)
                dve.drain()
                v.tensor_tensor_scan(incl, tot, zero, 0.0, ALU.add, ALU.add)
                v.tensor_tensor(pre, pre, tot, ALU.subtract)
                dve.drain()
                v.tensor_tensor(incl, incl, pre, ALU.add)
                dve.drain()
                v.tensor_tensor(incl, incl, hotf, ALU.mult)
                dve.drain()
                v.tensor_reduce(rank[:], incl.rearrange("p (b t) -> p t b", t=T), X_AXIS, ALU.add)
                dve.drain()
                v.tensor_copy(rank_i[:], rank[:]).then_inc(rank_done, 1)
                dve.wait_ge(order_in, 16)
                v.tensor_copy(c.first[:], back[:, :, 1])
                v.tensor_copy(c.ids[:], back[:, :, 0])
                v.tensor_copy(c.deg[:], back[:, :, 2])
                dve.drain()
                dve.sem_inc(ids_done, 1)

                dve.wait_ge(tr, 1)
                v.tensor_reduce(jmax[:, 0:1], pt, X_AXIS, ALU.max)
                dve.drain()
                v.tensor_scalar(jint[:], jmax[:, 0:1], float(SLOTS - 1), None, ALU.add)
                dve.drain()
                v.tensor_scalar(jint[:], jint[:], 3, None, ALU.logical_shift_right)
                dve.drain()
                v.tensor_copy(jmax[:, 1:2], jint[:])
                dve.drain()
                v.tensor_scalar(dj[:, 0, :], c.ident[0:T, 0:T], jmax[:, 0:1], None, ALU.mult)
                v.tensor_scalar(dj[:, 1, :], c.ident[0:T, 0:T], jmax[:, 1:2], None, ALU.mult).then_inc(dj_done, 1)
                dve.wait_ge(bcast, 1)
                v.tensor_copy(jn[:].rearrange("p b t -> p (b t)"), pj)
                dve.drain()
                v.tensor_tensor_scan(iend[:], jn[:, 1, :], zw[:], 0.0, ALU.add, ALU.add)
                dve.drain()
                v.tensor_tensor(ibeg[:], iend[:], jn[:, 1, :], ALU.subtract)
                v.tensor_scalar(nb_f[:], iend[0:1, T - 1:T], float(RING - 1), None, ALU.add)
                ib = item[:].unsqueeze(2).to_broadcast([P, LW, T])
                bt = lambda a: a.unsqueeze(1).to_broadcast([P, LW, T])
                dve.drain()
                v.tensor_copy(nb_i[:], nb_f[:])
                v.tensor_tensor(past, bt(iend[:]), ib, ALU.is_le)
                v.tensor_tensor(begun, bt(ibeg[:]), ib, ALU.is_le)
                dve.drain()
                v.tensor_scalar(c.bodies[:], nb_i[:], 3, None, ALU.logical_shift_right)
                v.tensor_reduce(tile_of[:], past, X_AXIS, ALU.add)
                v.tensor_tensor(begun, begun, past, ALU.subtract)
                dve.drain()
                v.tensor_tensor(past, past, bt(jn[:, 1, :]), ALU.mult)
                v.tensor_tensor(begun, begun, bt(jn[:, 0, :]), ALU.mult)
                dve.drain()
                v.tensor_reduce(base[:], past, X_AXIS, ALU.add)
                v.tensor_reduce(jm[:], begun, X_AXIS, ALU.add)
                dve.drain()
                v.tensor_tensor(s0[:], item[:], base[:], ALU.subtract)
                dve.drain()
                v.tensor_scalar(s0[:], s0[:], float(SLOTS), None, ALU.mult)
                dve.drain()
                v.tensor_tensor(jm[:], jm[:], s0[:], ALU.subtract)
                dve.drain()
                v.tensor_scalar(tile_of[:], tile_of[:], float(T - 1), None, ALU.min)
                v.tensor_scalar(jm[:], jm[:], 0.0, float(SLOTS), ALU.max, ALU.min)
                v.tensor_copy(meta[:, :, 2], s0[:])
                dve.drain()
                v.tensor_copy(meta[:, :, 0], tile_of[:])
                v.tensor_copy(meta[:, :, 1], jm[:])
                jq = jm[:].rearrange("p (q u i) -> p q u i", u=QS, i=BATCH)
                v.tensor_tensor(pair[:], jq[:, :, :, 0], jq[:, :, :, 1], ALU.add)
                dve.drain()
                for u in range(QS):
                    last = v.tensor_tensor_scan(cum[:, :, u], pair[:, :, u], zw[:, 0:LW // RING], 0.0, ALU.add, ALU.add)
                last.then_inc(rows_done, 1)
                dve.wait_ge(rows_sum, 1)
                m3 = meta[:, :, 3].rearrange("p (q u i) -> p q u i", u=QS, i=BATCH)
                v.tensor_tensor(m3[:, :, :, 0], cum[:], pcum.unsqueeze(1).to_broadcast([P, LW // RING, QS]), ALU.add)
                m3 = meta[:, :, 3].rearrange("p (s i) -> p s i", i=BATCH)
                pairs = tile_of[:].rearrange("p (s i) -> p s i", i=BATCH)
                v.scalar_tensor_tensor(m3[:, :, 1], pairs[:, :, 1], float(TILE_BASE), pairs[:, :, 0], ALU.mult, ALU.add)
                dve.drain()
                dve.sem_inc(meta_done, 1)

                nb = body_count(c, dve)

                def offsets(b, h):
                    dve.wait_ge(mrow_in[h], (b + 1) * 16)
                    held(c, dve)
                    half = slice(h * HI, (h + 1) * HI)
                    for i in range(h * HI, (h + 1) * HI):
                        if i % BATCH == 0:
                            both = two_tiles(c, dve, mrow[0:1, i + 1, 3:4])
                        t = both[i % BATCH]
                        v.tensor_tensor(offf[:, i:i + 1], c.first[:, bass.ds(t, 1)], mrow[:, i, 2:3], ALU.add)
                        v.tensor_tensor(left[:, i:i + 1], c.deg[:, bass.ds(t, 1)], mrow[:, i, 2:3], ALU.subtract)
                    dve.drain()
                    v.tensor_scalar(off[:, half], offf[:, half], float(E), None, ALU.min).then_inc(off_done, 1)

                def record(b, h, again):
                    if again:
                        dve.wait_ge(rec_out[h], b * 16)
                    dve.wait_ge(win_in[h], (b + 1) * (16 * HI))
                    held(c, dve)
                    for q in range(h * (QS // 2), (h + 1) * (QS // 2)):
                        two = slice(q * BATCH, (q + 1) * BATCH)
                        v.tensor_copy(rec[:, q, 0:BJ], win[:, two, :].rearrange("p i j -> p (i j)"))
                        v.tensor_copy(rec[:, q, FIRST_AT:FIRST_AT + BATCH], off[:, two])
                        for i in range(BATCH):
                            v.tensor_scalar(maskf[:, q, MASK_AT + i * SLOTS:MASK_AT + (i + 1) * SLOTS], c.slot[:],
                                            left[:, q * BATCH + i:q * BATCH + i + 1], MASKED, ALU.is_ge, ALU.mult)
                    dve.drain()
                    dve.sem_inc(rec_done, 1)

                offsets(0, 0)
                offsets(0, 1)
                record(0, 0, False)
                with dve.If(nb > 1):
                    offsets(1, 0)
                record(0, 1, False)
                with dve.Fori(1, nb) as b:
                    offsets(b, 1)
                    record(b, 0, True)
                    with dve.If(b < nb - 1):
                        offsets(b + 1, 0)
                    record(b, 1, True)


def held(c, eng):
    eng.sem_inc(c.passed, 1)


def two_tiles(c, eng, word):
    both = eng.value_load(word, min_val=0, max_val=TILE_BASE * (T - 1) + T - 1)
    return [c.nc.s_assert_within(both % TILE_BASE, 0, T - 1), both // TILE_BASE]


def body_count(c, eng):
    return eng.value_load(c.bodies[0:1, 0:1], min_val=1, max_val=CAP // RING)


Q0, V0, K0, NODE0, W1 = (F * i for i in range(5))
SRC2 = W1 + F + 8
DST2 = SRC2 + F + 4
KQ3 = DST2 + F + 4
WT_W = KQ3 + F
PROJECTED = {0: (Q0, 3 * F), 1: (W1, F + 8), 2: (SRC2, 2 * F + 8), 3: (KQ3, F)}
TABLE_W = [2 * F, F + 4, F + 4, 64 + F, F + 1]


def load_weights(c):
    nc, w = c.nc, c.w
    c.wt = c.sb("wt", [P, WT_W])
    c.att2 = c.sb("att2", [P, F])
    c.att2_relu = c.sb("att2_relu", [P, F])
    c.bias = c.sb("bias", [P, F])
    c.gamma = c.sb("gamma", [P, F])
    c.beta = c.sb("beta", [P, F])
    c.bkq = c.sb("bkq", [P, F])
    w_in, turned = c.sem("w_in"), c.sem("w_turned")
    with ExitStack() as local:
        raw = c.sb("raw", [P, 6, F], F32, local)
        att1 = c.sb("att1", [P, 2, F], F32, local)
        tmp = c.sb("w_tmp", [P, 4, F], F32, local)
        dots = c.sb("w_dots", [P, 4, 4], F32, local)
        pw = local.enter_context(nc.psum_tensor("pw", [P, 8, F], F32))
        with nc.Block() as block:
            @block.sync
            def _(sp):
                for i, name in enumerate(("L0_gnn_Wq", "L0_gnn_Wv", "L0_gnn_Wk", "L0_gnn_Wnode", "L1_gnn_W")):
                    sp.dma_start(raw[:, i, :], w[name]).then_inc(w_in, 16)
                sp.dma_start(raw[0:64, 5, :], w["L3_gnn_Wk"]).then_inc(w_in, 16)
                sp.dma_start(raw[64:P, 5, :], w["L3_gnn_Wq"]).then_inc(w_in, 16)
                sp.dma_start(c.wt[:, SRC2:SRC2 + F], w["L2_gnn_W_src"]).then_inc(w_in, 16)
                sp.dma_start(c.wt[:, DST2:DST2 + F], w["L2_gnn_W_dst"]).then_inc(w_in, 16)
                n = 9
                row = lambda v: v.rearrange("(a b) -> a b", a=1)
                flat = lambda v: row(v.rearrange("h d -> (h d)"))
                for to, of in ((att1[:, 0, :], flat(w["L1_gnn_att_src"])), (att1[:, 1, :], flat(w["L1_gnn_att_dst"])),
                               (c.att2[:], flat(w["L2_gnn_att"])), (c.bias[:], row(w["L2_gnn_bias"])),
                               (c.gamma[:], row(w["L2_gnn_bn_gamma"])), (c.beta[:], row(w["L2_gnn_bn_beta"])),
                               (c.bkq[:, 0:64], row(w["L3_gnn_bk"])), (c.bkq[:, 64:F], row(w["L3_gnn_bq"]))):
                    sp.dma_start(to, of.to_broadcast(list(to.shape))).then_inc(w_in, 16)
                    n += 1
                sp.wait_ge(w_in, 16 * n)

            @block.tensor
            def _(pe):
                pe.wait_ge(w_in, 16 * 17)
                for i in range(6):
                    mm = nc.tensor.transpose(pw[:, i, :], raw[:, i, :], c.ident[:])
                mm.then_inc(turned, 1)

            @block.vector
            def _(dve):
                v = nc.vector
                dve.wait_ge(turned, 1)
                v.tensor_copy(c.wt[:, 0:5 * F].rearrange("p (a f) -> p a f", f=F), pw[:, 0:5, :])
                v.tensor_copy(c.wt[:, KQ3:KQ3 + F], pw[:, 5, :])
                v.tensor_scalar(c.att2_relu[:], c.att2[:], 0.8, None, ALU.mult)
                v.tensor_tensor(tmp[:, 0:2, :], pw[:, 4, :].unsqueeze(1).to_broadcast([P, 2, F]), att1[:], ALU.mult)
                v.tensor_tensor(tmp[:, 2, :], c.wt[:, SRC2:SRC2 + F], c.att2[:], ALU.mult)
                v.tensor_tensor(tmp[:, 3, :], c.wt[:, DST2:DST2 + F], c.att2[:], ALU.mult)
                dve.drain()
                v.tensor_reduce(dots[:].rearrange("p a h -> p (a h)"), tmp[:].rearrange("p a (h d) -> p (a h) d", h=4), X_AXIS, ALU.add)
                dve.drain()
                v.tensor_copy(c.wt[:, W1 + F:W1 + F + 8], dots[:, 0:2, :].rearrange("p a h -> p (a h)"))
                v.tensor_scalar(c.wt[:, SRC2 + F:SRC2 + F + 4], dots[:, 2, :], 0.2, None, ALU.mult)
                v.tensor_scalar(c.wt[:, DST2 + F:DST2 + F + 4], dots[:, 3, :], 0.2, None, ALU.mult)


def project(c, layer):
    nc = c.nc
    last = layer == 5
    R = 0 if last else TABLE_W[layer]
    col, width = PROJECTED.get(layer, (0, 0))
    products = width > 0
    closes = layer > 0
    tag = f"pr{layer}_"
    BANKS, EARLY = 5, 4
    with ExitStack() as local:
        sb = lambda n, s, d=F32: c.sb(tag + n, s, d, local)
        ps = lambda n, s: local.enter_context(nc.psum_tensor(tag + n, s, F32))
        xg = sb("xg", [P, GT, F])
        xT = sb("xT", [P, 2, F])
        st = None if last else sb("st", [P, GT, R])
        tmp = sb("tmp", [P, GT, F])
        mean = sb("mean", [P, GT])
        var = sb("var", [P, GT])
        recip = sb("recip", [P, GT * 4])
        pX = [ps(f"pX{i}", [P, 512]) for i in range(2)]
        pW = [ps(f"pW{i}", [P, 512]) for i in range(BANKS)]
        turned, copied, mm_done, rows_done, scat, stage_free, summed, rooted, closed, staged = c.project_sems
        first = layer == 0
        with nc.Block() as block:
            @block.gpsimd
            def _(pool):
                if last:
                    for i in range(T):
                        n = LAST if i == T - 1 else P
                        if i % GT == 0:
                            pool.wait_ge(closed, NG * (layer - 1) + i // GT + 1)
                        pool.indirect_dma_start(out=c.out, out_offset=bass.IndirectOffsetOnAxis(ap=c.ids[0:n, i:i + 1], axis=0),
                                                in_=c.X[0:n, i, :], in_offset=None).then_inc(c.y_out, 16)
                    pool.wait_ge(c.y_out, 16 * T)
                    return
                with pool.Fori(0, NG) as g:
                    G = g + NG * layer
                    nc.gpsimd.tensor_copy(c.id_st[:], c.ids[:, bass.ds(g * GT, GT)])
                    pool.drain()
                    for k in range(GT):
                        pool.wait_ge(rows_done, G * GT + (k + 2))
                        held(c, pool)
                        pool.indirect_dma_start(out=c.tab[layer], out_offset=bass.IndirectOffsetOnAxis(ap=c.id_st[:, k:k + 1], axis=0),
                                                in_=st[:, k, :], in_offset=None).then_inc(scat, 16)
                    pool.wait_ge(scat, (G + 1) * (16 * GT))
                    pool.sem_inc(stage_free, 1)

            if products:
                @block.tensor
                def _(pe):
                    def turn(G, k):
                        if k == 0:
                            pe.wait_ge(staged, G + 1)
                        if k >= 2:
                            pe.wait_ge(copied, G * GT + (k - 1))
                        nc.tensor.transpose(pX[k % 2][:, 0:F], xg[:, k, :], c.ident[:]).then_inc(turned, 1)

                    if first:
                        pe.sem_inc(mm_done, 1)
                    with pe.Fori(0, NG) as g:
                        G = g + NG * layer
                        turn(G, 0)
                        for k in range(GT):
                            if k + 1 < GT:
                                turn(G, k + 1)
                            pe.wait_ge(copied, G * GT + (k + 1))
                            pe.wait_ge(rows_done, G * GT + (1 + max(0, k - BANKS + 1)))
                            nc.tensor.matmul(pW[k % BANKS][:, 0:width], xT[:, k % 2, :], c.wt[:, col:col + width],
                                             start=True, stop=True).then_inc(mm_done, 1)

            if products or closes:
                @block.scalar
                def _(act):
                    def root(g):
                        if closes:
                            act.wait_ge(summed, g + (NG * (layer - 1) + 1))
                            if layer == 4:
                                nc.scalar.activation(var[:], var[:], ACT.Sqrt).then_inc(rooted, 1)
                            else:
                                nc.scalar.activation(var[:], var[:], ACT.Sqrt, bias=c.eps[:], scale=1.0 / F).then_inc(rooted, 1)

                    def tiles(g, a, b):
                        G = g + NG * layer
                        if not products:
                            return
                        if a == 0:
                            if closes:
                                act.wait_ge(closed, g + (NG * (layer - 1) + 1))
                                held(c, act)
                            nc.scalar.copy(xg[:], c.X[:, bass.ds(g * GT, GT), :]).then_inc(staged, 1)
                        for k in range(a, b):
                            act.wait_ge(turned, G * GT + (k + 1))
                            if k >= 2:
                                act.wait_ge(mm_done, G * GT + k)
                            nc.scalar.copy(xT[:, k % 2, :], pX[k % 2][:, 0:F]).then_inc(copied, 1)

                    root(0)
                    with act.Fori(0, NG - 1) as g:
                        tiles(g, 0, EARLY)
                        root(g + 1)
                        tiles(g, EARLY, GT)
                    tiles(NG - 1, 0, GT)

            @block.vector
            def _(dve):
                v = nc.vector
                if first:
                    dve.sem_inc(stage_free, 1)
                    dve.sem_inc(rows_done, 1)
                O4 = sums_view(c, 4)

                def group(a, g):
                    return a[:, bass.ds(g * GT, GT), :]

                def at(a, t, n, n0=0):
                    return a[:, bass.ds(t, 1), n0:n0 + n].rearrange("p a f -> p (a f)")

                def wide(a):
                    return a[:].unsqueeze(2).to_broadcast([P, GT, F])

                def close_sums(g):
                    x = group(c.X, g)
                    if layer == 4:
                        v.tensor_tensor(tmp[:], group(flat_rows(c), g), x, ALU.subtract)
                        dve.drain()
                        v.tensor_tensor(tmp[:], tmp[:], tmp[:], ALU.mult)
                        dve.drain()
                        v.tensor_scalar(tmp[:], tmp[:], 0.1, None, ALU.max)
                        dve.drain()
                        v.tensor_reduce(var[:], tmp[:], X_AXIS, ALU.add).then_inc(summed, 1)
                        return
                    if layer == 2:
                        o = group(O4, g).rearrange("p t (h d) -> p (t h) d", h=4)
                        v.tensor_scalar(recip[:], o[:, :, F // 4], 1e-16, None, ALU.add)
                        dve.drain()
                        v.reciprocal(recip[:], recip[:])
                        dve.drain()
                        v.tensor_tensor(tmp[:].rearrange("p t (h d) -> p (t h) d", h=4), o[:, :, 0:F // 4],
                                        recip[:].unsqueeze(2).to_broadcast([P, GT * 4, F // 4]), ALU.mult)
                        dve.drain()
                    if layer == 3:
                        v.tensor_tensor(tmp[:], group(c.K, g), over_tiles(c.gamma[:], [P, GT, F]), ALU.mult)
                        dve.drain()
                        v.tensor_tensor(tmp[:], tmp[:], over_tiles(c.beta[:], [P, GT, F]), ALU.add)
                        dve.drain()
                        v.scalar_tensor_tensor(tmp[:], tmp[:], 0.02, tmp[:], ALU.mult, ALU.max)
                        dve.drain()
                    if layer == 5:
                        o = group(sums_view(c, 1, 1), g)
                        v.tensor_tensor(tmp[:], x, o[:, :, F + 1:F + 2].to_broadcast([P, GT, F]), ALU.mult)
                        v.tensor_scalar(recip[:, 0:GT], o[:, :, F], 1e-16, None, ALU.add)
                        dve.drain()
                        v.tensor_tensor(tmp[:], o[:, :, 0:F], tmp[:], ALU.subtract)
                        v.reciprocal(recip[:, 0:GT], recip[:, 0:GT])
                        dve.drain()
                        v.tensor_tensor(tmp[:], tmp[:], recip[:, 0:GT].unsqueeze(2).to_broadcast([P, GT, F]), ALU.mult)
                        dve.drain()
                    if layer != 1:
                        v.tensor_tensor(x, x, tmp[:], ALU.add)
                        dve.drain()
                    v.tensor_reduce(mean[:], x, X_AXIS, ALU.add)
                    dve.drain()
                    v.tensor_scalar(mean[:], mean[:], 1.0 / F, None, ALU.mult)
                    dve.drain()
                    v.tensor_tensor(x, x, wide(mean), ALU.subtract)
                    dve.drain()
                    v.tensor_tensor(tmp[:], x, x, ALU.mult)
                    dve.drain()
                    v.tensor_reduce(var[:], tmp[:], X_AXIS, ALU.add).then_inc(summed, 1)

                def close(g):
                    dve.wait_ge(rooted, g + (NG * (layer - 1) + 1))
                    held(c, dve)
                    if layer == 4:
                        v.reciprocal(c.g[:, bass.ds(g * GT, GT)], var[:])
                        dve.drain().then_inc(closed, 1)
                        return
                    v.reciprocal(var[:], var[:])
                    dve.drain()
                    x = group(c.X, g)
                    v.tensor_tensor(x, x, wide(var), ALU.mult)
                    dve.drain().then_inc(closed, 1)

                def rows(g):
                    G = g + NG * layer
                    if last:
                        return
                    dve.wait_ge(stage_free, G + 1)
                    held(c, dve)
                    for k in range(GT):
                        t = g * GT + k
                        here = at(c.K, t, F)
                        if products:
                            dve.wait_ge(mm_done, G * GT + (k + 2))
                            held(c, dve)
                        W = pW[k % BANKS]
                        if layer == 0:
                            v.tensor_copy(st[:, k, :], W[:, 0:2 * F])
                            v.tensor_copy(here, W[:, 2 * F:3 * F])
                        elif layer in (1, 2):
                            v.tensor_copy(st[:, k, :], W[:, 0:R])
                            if layer == 2:
                                v.tensor_copy(here, W[:, R:R + F])
                            v.tensor_copy(at(c.adst, t, 4), W[:, width - 4:width])
                            v.tensor_copy(at(c.S, t, 4), W[:, F:F + 4])
                            v.tensor_copy(at(O4, t, F + 4).rearrange("p (h d) -> p h d", h=4)[:, :, 0:F // 4],
                                          W[:, 0:F].rearrange("p (h d) -> p h d", h=4))
                        elif layer == 3:
                            v.tensor_tensor(st[:, k, 0:64], W[:, 0:64], c.bkq[:, 0:64], ALU.add)
                            v.tensor_tensor(here[:, 0:64], W[:, 64:F], c.bkq[:, 64:F], ALU.add)
                            v.tensor_copy(st[:, k, 64:R], at(c.X, t, F))
                        else:
                            v.tensor_copy(st[:, k, 0:F], at(c.X, t, F))
                            v.tensor_copy(st[:, k, F:F + 1], c.g[:, bass.ds(t, 1)])
                        dve.drain().then_inc(rows_done, 1)
                    if layer in (1, 2):
                        o = group(O4, g).rearrange("p t (h d) -> p (t h) d", h=4)
                        v.tensor_copy(o[:, :, F // 4], c.ones[:, 0:GT * 4])
                        M, src, dst = (a[:, bass.ds(g * GT, GT), 0:4] for a in (c.M, c.S, c.adst))
                        v.tensor_tensor(M, src, dst, ALU.add)
                        if layer == 2:
                            z = tmp[:].rearrange("p t (h d) -> p (t h) d", h=4)
                            v.tensor_tensor(z, o[:, :, 0:F // 4], group(c.K, g).rearrange("p t (h d) -> p (t h) d", h=4), ALU.add)
                            dve.drain()
                            v.scalar_tensor_tensor(tmp[:], tmp[:], 0.0, over_tiles(c.att2_relu[:], [P, GT, F]), ALU.max, ALU.mult)
                            dve.drain()
                            v.tensor_reduce(recip[:], z, X_AXIS, ALU.add)
                            dve.drain()
                            v.tensor_tensor(M, M, recip[:].rearrange("p (t h) -> p t h", h=4), ALU.add)
                        else:
                            dve.drain()
                            v.tensor_scalar(recip[:].rearrange("p (t h) -> p t h", h=4), M, 0.2, None, ALU.mult)
                            dve.drain()
                            v.tensor_tensor(M, M, recip[:].rearrange("p (t h) -> p t h", h=4), ALU.max)
                        dve.drain()

                if closes:
                    close_sums(0)
                    close(0)
                with dve.Fori(0, NG - 1) as g:
                    if closes:
                        close_sums(g + 1)
                    rows(g)
                    if closes:
                        close(g + 1)
                rows(NG - 1)


def over_tiles(a, dims):
    return a.unsqueeze(1).to_broadcast(dims)


def flat_rows(c):
    return c.O[:, 0:T * F].rearrange("p (t f) -> p t f", f=F)


def node_product(c):
    nc = c.nc
    with ExitStack() as local:
        ps = lambda n, s: local.enter_context(nc.psum_tensor(n, s, F32))
        og = c.sb("og", [P, 2, GT, F], F32, local)
        oT = c.sb("oT", [P, 2, F], F32, local)
        pX = [ps(f"cX{i}", [P, 512]) for i in range(2)]
        pW = [ps(f"cW{i}", [P, 4, P]) for i in range(4)]
        staged, turned, copied, mm_done, taken, used = (c.sem("c0_" + n) for n in ("staged", "turned", "copied", "mm", "taken", "used"))
        H, D = 8, F // 8
        with nc.Block() as block:
            @block.vector
            def _(dve):
                v = nc.vector
                o = sums_view(c, H).rearrange("p t (h d) -> p (t h) d", h=H)
                r = c.rs[:].rearrange("p t h -> p (t h)")
                v.tensor_scalar(r, o[:, :, D], 1e-30, None, ALU.max)
                dve.drain()
                v.reciprocal(r, r)
                dve.drain()

                def stage(g):
                    a, b = g * GT * H, (g + 1) * GT * H
                    v.tensor_tensor(og[:, g % 2, :, :].rearrange("p t (h d) -> p (t h) d", h=H), o[:, a:b, 0:D],
                                    r[:, a:b].unsqueeze(2).to_broadcast([P, GT * H, D]), ALU.mult).then_inc(staged, 1)

                def take(g):
                    for h, (a, b) in enumerate(((0, 4), (4, GT))):
                        x = c.X[:, g * GT + a:g * GT + b, :]
                        dve.wait_ge(mm_done, g * GT + b)
                        v.tensor_tensor(x, x, pW[(2 * g + h) % 4][:, 0:b - a, :], ALU.add).then_inc(taken, 1)

                stage(0)
                for g in range(NG):
                    if g + 1 < NG:
                        if g >= 1:
                            dve.wait_ge(turned, g * GT)
                        stage(g + 1)
                    take(g)

            @block.tensor
            def _(pe):
                def turn(n):
                    if n % GT == 0:
                        pe.wait_ge(staged, n // GT + 1)
                    if n >= 2:
                        pe.wait_ge(copied, n - 1)
                    nc.tensor.transpose(pX[n % 2][:, 0:F], og[:, n // GT % 2, n % GT, :], c.ident[:]).then_inc(turned, 1)

                turn(0)
                for n in range(T):
                    if n + 1 < T:
                        turn(n + 1)
                    pe.wait_ge(copied, n + 1)
                    half = 2 * (n // GT) + (n % GT >= 4)
                    if half >= 4:
                        pe.wait_ge(taken, half - 3)
                    nc.tensor.matmul(pW[half % 4][:, n % GT % 4, :], oT[:, n % 2, :], c.wt[:, NODE0:NODE0 + F],
                                     start=True, stop=True).then_inc(mm_done, 1)

            @block.scalar
            def _(act):
                for n in range(T):
                    act.wait_ge(turned, n + 1)
                    if n >= 2:
                        act.wait_ge(mm_done, n - 1)
                    nc.scalar.copy(oT[:, n % 2, :], pX[n % 2][:, 0:F]).then_inc(copied, 1)


def batch_statistics(c):
    nc = c.nc
    full = [P, T, F]
    with ExitStack() as local:
        mean = c.sb("mean", [P, F], F32, local)
        sd = c.sb("sd", [P, F], F32, local)
        pm = local.enter_context(nc.psum_tensor("pm", [P, F], F32))
        pv = local.enter_context(nc.psum_tensor("pv", [P, F], F32))
        rows_done, summed, centred, squared, var_sum, rooted = (
            c.sem("c2_" + n) for n in ("rows", "sum", "cen", "sq", "var", "root"))
        cuts = [0, 16, 32, T]
        with nc.Block() as block:
            @block.vector
            def _(dve):
                v = nc.vector
                H, D = 4, F // 4
                o = sums_view(c, H).rearrange("p t (h d) -> p (t h) d", h=H)
                r = c.rs[:].rearrange("p t h -> p (t h)")[:, 0:T * H]
                v.tensor_scalar(r, o[:, :, D], 1e-30, None, ALU.max)
                dve.drain()
                v.reciprocal(r, r)
                dve.drain()
                for a, b in zip(cuts, cuts[1:]):
                    k = c.K[:, a:b, :]
                    v.tensor_tensor(k.rearrange("p t (h d) -> p (t h) d", h=H), o[:, a * H:b * H, 0:D],
                                    r[:, a * H:b * H].unsqueeze(2).to_broadcast([P, (b - a) * H, D]), ALU.mult)
                    dve.drain()
                    v.tensor_tensor(k, k, over_tiles(c.bias[:], [P, b - a, F]), ALU.add).then_inc(rows_done, 1)
                dve.wait_ge(summed, 1)
                v.tensor_scalar(mean[:], pm[:], 1.0 / N, None, ALU.mult)
                dve.drain()
                for a, b in zip(cuts, cuts[1:]):
                    v.tensor_tensor(c.K[:, a:b, :], c.K[:, a:b, :], over_tiles(mean[:], [P, b - a, F]), ALU.subtract).then_inc(centred, 1)
                dve.wait_ge(rooted, 1)
                v.reciprocal(sd[:], sd[:])
                dve.drain()
                v.tensor_tensor(c.gamma[:], sd[:], c.gamma[:], ALU.mult)

            @block.tensor
            def _(pe):
                def sum_nodes(to, rows, ready, done):
                    for n, (a, b) in enumerate(zip(cuts, cuts[1:])):
                        pe.wait_ge(ready, n + 1)
                        for t in range(a, b):
                            mm = nc.tensor.matmul(to[:], (c.valid if t == T - 1 else c.ones)[:], rows[:, t, :],
                                                  start=t == 0, stop=t == T - 1)
                    mm.then_inc(done, 1)

                sum_nodes(pm, c.K, rows_done, summed)
                sum_nodes(pv, flat_rows(c), squared, var_sum)

            @block.scalar
            def _(act):
                sq = flat_rows(c)
                for n, (a, b) in enumerate(zip(cuts, cuts[1:])):
                    act.wait_ge(centred, n + 1)
                    nc.scalar.activation(sq[:, a:b, :], c.K[:, a:b, :], ACT.Square).then_inc(squared, 1)
                act.wait_ge(var_sum, 1)
                nc.scalar.activation(sd[:], pv[:], ACT.Sqrt, bias=c.eps[:], scale=1.0 / N).then_inc(rooted, 1)


HEADS = {"L0": 8, "L1": 4, "L2": 4, "L3a": 4, "L3c": 1}
TABLE = {"L0": 0, "L1": 1, "L2": 2, "L3a": 3, "L3c": 4}


PASSES = ["L0", "L1", "L2", "L3a", "L3c"]


def sums_view(c, H, more=0):
    w = F + H + more
    return c.O[:, 0:T * w].rearrange("p (t w) -> p t w", w=w)


def edge_pass(c, kind):
    nc = c.nc
    H, tab = HEADS[kind], c.tab[TABLE[kind]]
    R = TABLE_W[TABLE[kind]]
    D = F // H
    tag = kind + "_"
    grand = kind == "L3a"
    rows_at = 64 if grand else F if kind == "L0" else 0
    W = 4 * F if grand else F + H + (kind == "L3c")
    C = 5 if kind == "L3c" else H
    with ExitStack() as local:
        sb = lambda n, s, d=F32: c.sb(tag + n, s, d, local)
        meta = sb("meta", [1, QS, BATCH * 4], I32)
        rec = sb("rec", [P, QS, REC], I32)
        got = sb("got", [P, QS, BJ, R])
        gate = sb("gate", [P, QS, BJ, 16]) if kind == "L0" else None
        raw = sb("raw", [P, QS, BJ, 4]) if kind in ("L3a", "L3c") else None
        prod = sb("prod", [P, BJ, 64 if grand else F]) if kind in ("L0", "L2", "L3a") else None
        wrow = sb("wrow", [P, BATCH, SLOTS, W])
        lg = sb("lg", [P, QS, BJ + BATCH, C])
        ex = sb("ex", [P, QS, BJ + BATCH, C])
        wt = sb("w", [P, BJ, max(H, 4)])
        watt = sb("watt", [P, BJ])
        mx = sb("mx", [P, BATCH, H])
        mnew = sb("mnew", [P, BATCH, H])
        psum_s = sb("ps", [P, BATCH, H])
        A = sb("A", [P, W]) if grand else None
        collapse = sb("col", [P, W]) if grand else None
        rS = sb("rS", [P, H])
        acc = [local.enter_context(nc.psum_tensor(tag + f"acc{i}", [P, 512], F32)) for i in range(BATCH)]
        got_in = [c.sem(tag + f"got{q}") for q in range(QS)]
        raw_out = [c.sem(tag + f"ro{q}") for q in range(QS)] if kind == "L3a" else None
        raw_in = [c.sem(tag + f"ri{q}") for q in range(QS)] if kind == "L3c" else None
        raw_done = c.sem(tag + "rd") if kind == "L3a" else None
        z_done, relu_done = (c.sem(tag + "z"), c.sem(tag + "relu")) if kind == "L2" else (None, None)
        rec_in, batch_done, lg_done, ex_done, w_done, acc_done, taken, here = c.pass_sems
        n_pass = PASSES.index(kind)
        maskf = rec[:].bitcast(F32)
        O = flat_rows(c) if grand else sums_view(c, H, 1 if kind == "L3c" else 0)
        last_meta = sb("last_meta", [1, 2, BATCH * 4], I32)
        on_act = 2 if grand else 0
        act_w_done = c.sem(tag + "aw") if grand else None
        m0 = 4 if kind == "L3c" else 0
        with nc.Block() as block:
            @block.gpsimd
            def _(pool):
                nc.gpsimd.memset(got[:, QS // 2:QS, :, :], 0.0)

            @block.vector
            def _(dve):
                v = nc.vector
                v.memset(got[:, 0:QS // 2, :, :], 0.0)
                if kind == "L3c":
                    v.memset(lg[:], 0.0)
                if kind in ("L0", "L3c"):
                    v.memset(c.O[:], 0.0)
                if kind not in ("L1", "L2"):
                    v.memset(c.M[:, :, m0:m0 + H], LOWEST)
                if grand:
                    v.memset(c.S[:], 0.0)
                    v.memset(A[:], 0.0)
        with nc.Block() as block:
            @block.sync
            def _(sp):
                nb = body_count(c, sp)

                def fill(b, q):
                    s = b * QS + q
                    sp.wait_ge(batch_done, (b + nb * n_pass) * QS + (q + 1))
                    if grand:
                        held(c, sp)
                        sp.wait_ge(act_w_done, b * RING + (q + 1) * BATCH)
                    sp.dma_start(meta[:, q, :], c.meta_d[bass.ds(s, 1), :]).then_inc(rec_in[q], 16)
                    sp.dma_start(rec[:, q, :], c.rec_d[bass.ds(s, 1), :, :].rearrange("o p c -> (o p) c")).then_inc(rec_in[q], 16)
                    if kind == "L3c":
                        sp.dma_start(raw[:, q, :, :].rearrange("p j h -> p (j h)"),
                                     c.logit_d[bass.ds(s, 1), :, :].rearrange("o p c -> (o p) c")).then_inc(raw_in[q], 16)

                def arrived(b, q):
                    sp.wait_ge(rec_in[q], (b + nb * n_pass) * 32 + 32)
                    held(c, sp)
                    gathers = sp.value_load(meta[0:1, q, 3:4], min_val=1, max_val=CAP * SLOTS)
                    sp.wait_ge(got_in[q], (gathers + (b + 1) * BATCH) * 16 if kind == "L0" else gathers * 16)
                    sp.sem_inc(here, 1)

                for q in range(QS):
                    fill(0, q)
                with sp.Fori(0, nb) as b:
                    for q in range(QS):
                        arrived(b, q)
                        if q >= 1:
                            with sp.If(b < nb - 1):
                                fill(b + 1, q - 1)
                        else:
                            with sp.If(b > 0):
                                fill(b, QS - 1)

            @block.gpsimd
            def _(pool):
                nb = body_count(c, pool)
                with pool.Fori(0, nb) as b:
                    for q in range(QS):
                        pool.wait_ge(rec_in[q], (b + nb * n_pass) * 32 + 32)
                        held(c, pool)
                        for i in range(BATCH):
                            used = pool.value_load(meta[0:1, q, 4 * i + 1:4 * i + 2], min_val=0, max_val=SLOTS)
                            if kind == "L0":
                                pool.indirect_dma_start(out=gate[:, q, i * SLOTS:(i + 1) * SLOTS, :].rearrange("p j h -> p (j h)"),
                                                        out_offset=None, in_=c.gate_win,
                                                        in_offset=bass.IndirectOffsetOnAxis(ap=rec[:, q, FIRST_AT + i:FIRST_AT + i + 1], axis=0)
                                                        ).then_inc(got_in[q], 16)
                            for j in range(i * SLOTS, (i + 1) * SLOTS):
                                with pool.If(used > j - i * SLOTS):
                                    pool.indirect_dma_start(out=got[:, q, j, :], out_offset=None, in_=tab,
                                                            in_offset=bass.IndirectOffsetOnAxis(ap=rec[:, q, j:j + 1], axis=0)).then_inc(got_in[q], 16)

            @block.scalar
            def _(act):
                nb = body_count(c, act)
                if kind == "L3a":
                    act.sem_inc(act_w_done, RING)
                    for q in range(QS):
                        act.sem_inc(raw_out[q], 16)
                with act.Fori(0, nb) as b:
                    for q in range(QS):
                        if kind == "L2":
                            act.wait_ge(z_done, b * QS + (q + 1))
                            nc.scalar.activation(prod[:], prod[:], ACT.Relu).then_inc(relu_done, 1)
                        if kind == "L3a":
                            act.wait_ge(raw_done, b * QS + (q + 1))
                            act.dma_start(c.logit_d[bass.ds(b * QS + q, 1), :, :].rearrange("o p c -> (o p) c"),
                                          raw[:, q, :, :].rearrange("p j h -> p (j h)")).then_inc(raw_out[q], 16)
                        act.wait_ge(lg_done, (b + nb * n_pass) * QS + (q + 1))
                        nc.scalar.activation(ex[:, q, :, :], lg[:, q, :, :], ACT.Exp).then_inc(ex_done, 1)
                        if grand:
                            act.wait_ge(ex_done, (b + nb * n_pass) * QS + (q + 1))
                            for i in range(BATCH):
                                act.wait_ge(taken, (b + nb * n_pass) * RING + (i + 1 + q * BATCH))
                                held(c, act)
                                for j in range(SLOTS):
                                    for h in range(H - on_act, H):
                                        at_j = i * SLOTS + j
                                        done = nc.scalar.mul(wrow[:, i, j, h * F:(h + 1) * F], got[:, q, at_j, rows_at:rows_at + F],
                                                             ex[:, q, at_j, h:h + 1])
                                done.then_inc(act_w_done, 1)
                if kind == "L3a":
                    for q in range(QS):
                        act.wait_ge(raw_out[q], nb * 16 + 16)
                    held(c, act)

            @block.tensor
            def _(pe):
                if n_pass == 0:
                    pe.sem_inc(acc_done, RING)
                nb = body_count(c, pe)
                with pe.Fori(0, nb) as b:
                    for u in range(RING):
                        pe.wait_ge(taken, (b + nb * n_pass) * RING + (u + 1))
                        pe.wait_ge(w_done, (b + nb * n_pass) * RING + (u + 1))
                        if grand:
                            pe.wait_ge(act_w_done, b * RING + (RING + u + 1))
                        for j in range(SLOTS):
                            mm = nc.tensor.matmul(acc[u % BATCH][:, 0:W], c.ident[:], wrow[:, u % BATCH, j, :],
                                                  start=(j == 0), stop=(j == SLOTS - 1))
                        mm.then_inc(acc_done, 1)

            @block.vector
            def _(dve):
                v = nc.vector
                if n_pass == 0:
                    dve.sem_inc(batch_done, QS)
                    dve.sem_inc(taken, BATCH)
                nb = body_count(c, dve)
                tiles = {}

                def at(a, q, i, n, n0=0):
                    return a[:, bass.ds(tiles[q][i], 1), n0:n0 + n].rearrange("p a f -> p (a f)")

                def over(ap, n=SLOTS):
                    return ap.unsqueeze(1).to_broadcast([ap.shape[0], n, ap.shape[1]])

                def item(i):
                    return slice(i * SLOTS, (i + 1) * SLOTS)

                def arrive(b, q):
                    dve.wait_ge(rec_in[q], (b + nb * n_pass) * 32 + 32)
                    if kind == "L3c":
                        dve.wait_ge(raw_in[q], b * 16 + 16)
                    if kind == "L3a":
                        dve.wait_ge(raw_out[q], b * 16 + 16)
                    held(c, dve)
                    tiles[q] = two_tiles(c, dve, meta[0:1, q, 7:8])
                    dve.wait_ge(here, (b + nb * n_pass) * QS + (q + 1))

                def logits(b, q):
                    l = lg[:, q, 0:BJ, m0:m0 + H]
                    mask = maskf[:, q, MASK_AT:MASK_AT + BJ]
                    wide = mask.unsqueeze(2).to_broadcast([P, BJ, H])
                    G = got[:, q, :, :]
                    if kind == "L0":
                        for i in range(BATCH):
                            v.tensor_tensor(prod[:, item(i), :], G[:, item(i), 0:F], over(at(c.K, q, i, F)), ALU.mult)
                        dve.drain()
                        v.tensor_reduce(l, prod[:].rearrange("p j (h d) -> p j h d", h=H), X_AXIS, ALU.add)
                        dve.drain()
                        v.tensor_scalar(l, l, 5.0, -5.0, ALU.min, ALU.max)
                        dve.drain()
                        v.tensor_tensor(l, l, gate[:, q, :, 0:8], ALU.add)
                        dve.drain()
                        v.scalar_tensor_tensor(l, l, L0_SCALE, wide, ALU.mult, ALU.add)
                    elif kind == "L1":
                        for i in range(BATCH):
                            v.tensor_tensor(lg[:, q, item(i), :], G[:, item(i), F:F + 4], over(at(c.adst, q, i, 4)), ALU.add)
                        dve.drain()
                        v.scalar_tensor_tensor(l, l, 0.2, l, ALU.mult, ALU.max)
                        dve.drain()
                        v.tensor_tensor(l, l, wide, ALU.add)
                    elif kind == "L2":
                        dve.wait_ge(relu_done, b * QS + (q + 1))
                        v.tensor_tensor(prod[:], prod[:], over(c.att2_relu[:], BJ), ALU.mult)
                        for i in range(BATCH):
                            v.tensor_tensor(wt[:, item(i), :], G[:, item(i), F:F + 4], over(at(c.adst, q, i, 4)), ALU.add)
                        dve.drain()
                        v.tensor_reduce(l, prod[:].rearrange("p j (h d) -> p j h d", h=H), X_AXIS, ALU.add)
                        v.tensor_tensor(wt[:], wt[:], wide, ALU.add)
                        dve.drain()
                        v.tensor_tensor(l, l, wt[:], ALU.add)
                    elif kind == "L3a":
                        for i in range(BATCH):
                            v.tensor_tensor(prod[:, item(i), :], G[:, item(i), 0:64], over(at(c.K, q, i, 64)), ALU.mult)
                        dve.drain()
                        v.tensor_reduce(l, prod[:].rearrange("p j (h d) -> p j h d", h=H), X_AXIS, ALU.add)
                        dve.drain()
                        v.scalar_tensor_tensor(raw[:, q, :, :], l, 0.25, wide, ALU.mult, ALU.add)
                        dve.drain().then_inc(raw_done, 1)
                        l = raw[:, q, :, :]
                    else:
                        for i in range(BATCH):
                            v.tensor_tensor(lg[:, q, item(i), 0:4], raw[:, q, item(i), :], over(at(c.M, q, i, 4)), ALU.subtract)
                            v.scalar_tensor_tensor(lg[:, q, item(i), 4], G[:, item(i), F], c.g[:, bass.ds(tiles[q][i], 1)],
                                                   mask[:, item(i)], ALU.add, ALU.add)
                    dve.drain()
                    v.tensor_reduce(mx[:], l.rearrange("p (i j) h -> p i h j", i=BATCH), X_AXIS, ALU.max)
                    dve.drain()
                    for i in range(BATCH):
                        M = at(c.M, q, i, H, m0)
                        v.tensor_tensor(mnew[:, i, :], M, mx[:, i, :], ALU.max)
                        dve.drain()
                        v.tensor_tensor(lg[:, q, BJ + i, m0:m0 + H], M, mnew[:, i, :], ALU.subtract)
                        last = v.tensor_tensor(lg[:, q, item(i), m0:m0 + H], l[:, item(i), :], over(mnew[:, i, :]), ALU.subtract)
                        if i == BATCH - 1:
                            last.then_inc(lg_done, 1)
                        dve.drain()
                        v.tensor_copy(M, mnew[:, i, :])
                        if i < BATCH - 1:
                            dve.drain()

                def weights(b, q):
                    dve.wait_ge(ex_done, (b + nb * n_pass) * QS + (q + 1))
                    held(c, dve)
                    e = ex[:, q, 0:BJ, m0:m0 + H]
                    if kind == "L0":
                        v.tensor_tensor(wt[:], e, gate[:, q, :, 8:16], ALU.mult)
                        dve.drain()
                    if kind == "L3c":
                        for i in range(BATCH):
                            v.tensor_tensor(wt[:, item(i), :], ex[:, q, item(i), 0:4], over(at(c.rs, q, i, 4)), ALU.mult)
                        dve.drain()
                        v.tensor_reduce(watt[:], wt[:], X_AXIS, ALU.add)
                        dve.drain()
                        v.tensor_tensor(watt[:], watt[:], ex[:, q, 0:BJ, 4], ALU.mult)
                        dve.drain()
                    if grand:
                        v.tensor_reduce(psum_s[:], e.rearrange("p (i j) h -> p i h j", i=BATCH), X_AXIS, ALU.add)

                def weigh(b, q, i):
                    x = got[:, q, item(i), rows_at:rows_at + F]
                    to = wrow[:, i, :, :]
                    ei = ex[:, q, item(i), m0:m0 + H]
                    if grand:
                        n = H - on_act
                        v.tensor_tensor(to[:, :, 0:n * F].rearrange("p j (h f) -> p j h f", h=n), x.unsqueeze(2).to_broadcast([P, SLOTS, n, F]),
                                        ei[:, :, 0:n].unsqueeze(3).to_broadcast([P, SLOTS, n, F]), ALU.mult).then_inc(w_done, 1)
                        s = at(c.S, q, i, H)
                        v.tensor_tensor(s, s, ex[:, q, BJ + i, :], ALU.mult)
                        dve.drain()
                        v.tensor_tensor(s, s, psum_s[:, i, :], ALU.add)
                        dve.drain()
                    elif kind == "L3c":
                        v.tensor_copy(to[:, :, F], ex[:, q, item(i), 4])
                        v.tensor_copy(to[:, :, F + 1], watt[:, item(i)])
                        v.tensor_tensor(to[:, :, 0:F], x, watt[:, item(i)].unsqueeze(2).to_broadcast([P, SLOTS, F]),
                                        ALU.mult).then_inc(w_done, 1)
                    else:
                        parts = to.rearrange("p j (h d) -> p j h d", h=H)
                        a = wt[:, item(i), :] if kind == "L0" else ei
                        v.tensor_copy(parts[:, :, :, D], ei)
                        v.tensor_tensor(parts[:, :, :, 0:D], x.rearrange("p j (h d) -> p j h d", h=H),
                                        a.unsqueeze(3).to_broadcast([P, SLOTS, H, D]), ALU.mult).then_inc(w_done, 1)

                def release():
                    dve.drain().then_inc(batch_done, 1)

                def add_up(b, q, i, after=None):
                    corr = ex[:, q, BJ + i, m0:m0 + H]
                    if grand:
                        o, n = A[:].rearrange("p (h d) -> p h d", h=H), F
                        v.tensor_scalar(rS[:], at(c.S, q, i, H), 1e-16, float(H), ALU.add, ALU.mult)
                    elif kind == "L3c":
                        o, n = at(O, q, i, W).unsqueeze(1), W
                    else:
                        o, n = at(O, q, i, W).rearrange("p (h d) -> p h d", h=H), D + 1
                    v.tensor_tensor(o, o, corr.unsqueeze(2).to_broadcast([P, H, n]), ALU.mult)
                    dve.drain()
                    if grand:
                        v.reciprocal(rS[:], rS[:])
                    dve.wait_ge(acc_done, (b + nb * n_pass) * RING + (RING + q * BATCH + i + 1))
                    v.tensor_tensor(o, o, acc[i][:, 0:W].rearrange("p (h d) -> p h d", h=H), ALU.add).then_inc(taken, 1)
                    if i == 0 or grand:
                        dve.drain()
                    if grand and after is None:
                        mean_of_heads(q, i)
                    elif grand:
                        with dve.If(tiles[q][i] < after):
                            mean_of_heads(q, i)

                def mean_of_heads(q, i):
                    v.tensor_tensor(collapse[:].rearrange("p (h f) -> p h f", h=H), A[:].rearrange("p (h d) -> p h d", h=H),
                                    rS[:].unsqueeze(2).to_broadcast([P, H, F]), ALU.mult)
                    v.tensor_copy(at(c.rs, q, i, H), rS[:])
                    dve.drain()
                    v.tensor_reduce(at(O, q, i, F), collapse[:].rearrange("p (h f) -> p f h", h=H), X_AXIS, ALU.add)
                    dve.drain()

                def add_rows(b, q):
                    for i in range(BATCH):
                        last = v.tensor_tensor(prod[:, item(i), :], got[:, q, item(i), 0:F], over(at(c.K, q, i, F)), ALU.add)
                    last.then_inc(z_done, 1)

                def finish(b, q, again=True):
                    weights(b, q)
                    weigh(b, q, 0)
                    if q >= 1:
                        add_up(b, q - 1, 1, tiles[q][0])
                    elif again:
                        add_up(b - 1, QS - 1, 1, tiles[0][0])
                    weigh(b, q, 1)
                    release()

                def old_tiles():
                    for n in range(2):
                        tiles[QS - 2 + n] = two_tiles(c, dve, last_meta[0:1, n, 7:8])

                def body(b, again):
                    for q in range(QS):
                        arrive(b, q)
                        if q >= QS - 2:
                            v.tensor_copy(last_meta[:, q - QS + 2, :], meta[:, q, :])
                        if kind == "L2":
                            add_rows(b, q)
                        if q >= 1:
                            finish(b, q - 1, again)
                            logits(b, q)
                            add_up(b, q - 1, 0, tiles[q - 1][1])
                        else:
                            if again:
                                held(c, dve)
                                old_tiles()
                                finish(b - 1, QS - 1)
                            logits(b, q)
                            if again:
                                add_up(b - 1, QS - 1, 0, tiles[QS - 1][1])

                body(0, False)
                with dve.Fori(1, nb) as b:
                    body(b, True)
                old_tiles()
                finish(nb - 1, QS - 1)
                add_up(nb - 1, QS - 1, 0)
                add_up(nb - 1, QS - 1, 1)


_INS = ("x", "src", "dst", "edge_attr_128")


def kernel(**inputs):
    import numpy as np
    import concourse.bacc as bacc
    from concourse.bass_utils import run_bass_kernel_spmd

    nc = bacc.Bacc("TRN2", target_bir_lowering=False, num_devices=1)
    arrays, aps = {}, {}
    for name in inputs:
        a = np.ascontiguousarray(inputs[name])
        arrays["in_" + name] = a
        aps[name] = nc.dram_tensor("in_" + name, a.shape, mybir.dt.from_np(a.dtype), kind="ExternalInput").ap()
    out = nc.dram_tensor("out_x", (N, F), F32, kind="ExternalOutput").ap()
    weights = {name: ap for name, ap in aps.items() if name not in _INS}
    build(nc, aps["x"], aps["src"], aps["dst"], aps["edge_attr_128"], weights, out)
    return run_bass_kernel_spmd(nc, [arrays], core_ids=[0]).results[0]["out_x"]
```
